# Optimizing a Trainium2 kernel written in Bass

```python
import numpy as np
import jax
import jax.numpy as jnp

def _softmax(x, axis=-1):
    return jax.nn.softmax(x, axis=axis)

def _gelu(x):
    return jax.nn.gelu(x, approximate=True)

def _silu(x):
    return jax.nn.silu(x)

def _sigmoid(x):
    return jax.nn.sigmoid(x)

def _layernorm(x, axis=-1, eps=1e-05):
    m = jnp.mean(x, axis=axis, keepdims=True)
    v = jnp.var(x, axis=axis, keepdims=True)
    return (x - m) / jnp.sqrt(v + eps)

def _scatter_add(tgt, idx, src, axis=0):
    return tgt.at[idx].add(src)

def _segment_sum(src, seg, n):
    return jax.ops.segment_sum(src, seg, n)
kernel_name = 'mk_conv_preact_d2_conv_nhwc512_r4_a4fb91'

def setup_inputs(seed: int=0):
    np.random.seed(seed)
    _w = jnp.asarray

    def _rec_inputs():
        import jax
        import jax.numpy as jnp
        _gk = jax.random.key(seed)
        x = -0.0003957 + 1 * jax.random.normal(jax.random.fold_in(_gk, 1), (8, 56, 56, 128), jnp.float32)
        return x
    x = _rec_inputs()

    def _L0_conv_setup():
        import jax, jax.numpy as jnp
        import numpy as np
        EMBED_DIM = 128
        NUM_HEADS = 8
        EXPAND = 2
        D1 = EXPAND * EMBED_DIM
        HEAD_DIM = D1 // NUM_HEADS
        RPE_DIM = 128
        RPE_LAYERS = 3
        N = 56
        M = 56
        BATCH = 8
        EPS = 1e-08

        def simple_rms(x):
            d = x.shape[-1]
            norm = jnp.linalg.norm(x, axis=-1, keepdims=True)
            return x / (norm * d ** (-0.5) + EPS)
        _DP = np.arange(-(N - 1), N, dtype=np.float32)
        _DQ = np.arange(-(M - 1), M, dtype=np.float32)
        _COORDS = np.stack(np.meshgrid(_DP, _DQ, indexing='ij'), axis=-1)
        _RI = (np.arange(2 * N - 1) - (N - 1)) % (2 * N)
        _CI = (np.arange(2 * M - 1) - (M - 1)) % (2 * M)

        def rpe_coeffs(rpe_in_w, rpe_in_b, rpe_h_w, rpe_h_b, rpe_out_w, rpe_out_b):
            t = jnp.asarray(_COORDS) @ rpe_in_w.T + rpe_in_b
            for i in range(RPE_LAYERS):
                t = jax.nn.relu(simple_rms(t)) @ rpe_h_w[i].T + rpe_h_b[i]
            g = jax.nn.relu(simple_rms(t)) @ rpe_out_w.T + rpe_out_b
            g = g.reshape(2 * N - 1, 2 * M - 1, NUM_HEADS, HEAD_DIM)
            return g.transpose(2, 0, 1, 3)

        def tno2d(v, g):
            a = jnp.zeros((NUM_HEADS, 2 * N, 2 * M, HEAD_DIM), dtype=g.dtype)
            a = a.at[:, _RI[:, None], _CI[None, :], :].set(g)
            vf = jnp.fft.rfft2(v, s=(2 * N, 2 * M), axes=(2, 3))
            af = jnp.fft.rfft2(a, axes=(1, 2))
            y = jnp.fft.irfft2(vf * af[None], s=(2 * N, 2 * M), axes=(2, 3))
            return y[:, :, :N, :M, :]
        key = jax.random.key(seed)
        ks = jax.random.split(key, 16)

        def nrm(k, shape, std=0.02):
            return jax.random.normal(k, shape, dtype=jnp.float32) * std
        return {'x': jax.random.normal(ks[0], (BATCH, N, M, EMBED_DIM), dtype=jnp.float32), 'W_u': nrm(ks[1], (D1, EMBED_DIM)), 'b_u': nrm(ks[2], (D1,)), 'W_v': nrm(ks[3], (D1, EMBED_DIM)), 'b_v': nrm(ks[4], (D1,)), 'W_o': nrm(ks[5], (EMBED_DIM, D1)), 'b_o': nrm(ks[6], (EMBED_DIM,)), 'rpe_in_w': nrm(ks[7], (RPE_DIM, 2), 0.5), 'rpe_in_b': nrm(ks[8], (RPE_DIM,), 0.5), 'rpe_h_w': nrm(ks[9], (RPE_LAYERS, RPE_DIM, RPE_DIM), 0.05), 'rpe_h_b': nrm(ks[10], (RPE_LAYERS, RPE_DIM), 0.05), 'rpe_out_w': nrm(ks[11], (NUM_HEADS * HEAD_DIM, RPE_DIM), 0.05), 'rpe_out_b': nrm(ks[12], (NUM_HEADS * HEAD_DIM,), 0.05), 'H': N, 'W': M}
    _L0_conv_all = _L0_conv_setup()
    _L0_conv_in = {k: v for k, v in _L0_conv_all.items() if k in ('W_u', 'b_u', 'W_v', 'b_v', 'W_o', 'b_o', 'rpe_in_w', 'rpe_in_b', 'rpe_h_w', 'rpe_h_b', 'rpe_out_w', 'rpe_out_b')}
    del _L0_conv_all

    def _L1_conv_setup():
        import jax, jax.numpy as jnp
        import numpy as np
        EPS = 1e-12
        HEADS = 8
        DIM_HEAD = 16

        def _l2norm(t):
            n = jnp.linalg.norm(t, axis=-1, keepdims=True)
            return t / jnp.maximum(n, EPS)
        key = jax.random.key(seed)
        ks = jax.random.split(key, 7)
        b, h, w, c = (4, 16, 16, 128)
        s = 0.02
        return {'x': jax.random.normal(ks[0], (b, h, w, c), jnp.float32), 'Wq': jax.random.normal(ks[1], (c, c), jnp.float32) * s, 'Wk': jax.random.normal(ks[2], (c, c), jnp.float32) * s, 'Wv': jax.random.normal(ks[3], (c, c), jnp.float32) * s, 'conv_w': jax.random.normal(ks[4], (c, c, 1, 1), jnp.float32) * s, 'proj_w': jax.random.normal(ks[5], (c, c), jnp.float32) * s, 'proj_b': jnp.zeros((c,), jnp.float32)}
    _L1_conv_all = _L1_conv_setup()
    _L1_conv_in = {k: v for k, v in _L1_conv_all.items() if k in ('Wq', 'Wk', 'Wv', 'conv_w', 'proj_w', 'proj_b')}
    del _L1_conv_all
    return {'x': x, 'L0_conv_W_u': _L0_conv_in['W_u'], 'L0_conv_b_u': _L0_conv_in['b_u'], 'L0_conv_W_v': _L0_conv_in['W_v'], 'L0_conv_b_v': _L0_conv_in['b_v'], 'L0_conv_W_o': _L0_conv_in['W_o'], 'L0_conv_b_o': _L0_conv_in['b_o'], 'L0_conv_rpe_in_w': _L0_conv_in['rpe_in_w'], 'L0_conv_rpe_in_b': _L0_conv_in['rpe_in_b'], 'L0_conv_rpe_h_w': _L0_conv_in['rpe_h_w'], 'L0_conv_rpe_h_b': _L0_conv_in['rpe_h_b'], 'L0_conv_rpe_out_w': _L0_conv_in['rpe_out_w'], 'L0_conv_rpe_out_b': _L0_conv_in['rpe_out_b'], 'L1_conv_Wq': _L1_conv_in['Wq'], 'L1_conv_Wk': _L1_conv_in['Wk'], 'L1_conv_Wv': _L1_conv_in['Wv'], 'L1_conv_conv_w': _L1_conv_in['conv_w'], 'L1_conv_proj_w': _L1_conv_in['proj_w'], 'L1_conv_proj_b': _L1_conv_in['proj_b']}

def reference(x, L0_conv_W_u, L0_conv_b_u, L0_conv_W_v, L0_conv_b_v, L0_conv_W_o, L0_conv_b_o, L0_conv_rpe_in_w, L0_conv_rpe_in_b, L0_conv_rpe_h_w, L0_conv_rpe_h_b, L0_conv_rpe_out_w, L0_conv_rpe_out_b, L1_conv_Wq, L1_conv_Wk, L1_conv_Wv, L1_conv_conv_w, L1_conv_proj_w, L1_conv_proj_b):
    import jax
    import jax.numpy as jnp

    def _L0_conv_ref(x, W_u, b_u, W_v, b_v, W_o, b_o, rpe_in_w, rpe_in_b, rpe_h_w, rpe_h_b, rpe_out_w, rpe_out_b, H, W):
        import jax, jax.numpy as jnp
        import numpy as np
        EMBED_DIM = 128
        NUM_HEADS = 8
        EXPAND = 2
        D1 = EXPAND * EMBED_DIM
        HEAD_DIM = D1 // NUM_HEADS
        RPE_DIM = 128
        RPE_LAYERS = 3
        N = 56
        M = 56
        BATCH = 8
        EPS = 1e-08

        def simple_rms(x):
            d = x.shape[-1]
            norm = jnp.linalg.norm(x, axis=-1, keepdims=True)
            return x / (norm * d ** (-0.5) + EPS)
        _DP = np.arange(-(N - 1), N, dtype=np.float32)
        _DQ = np.arange(-(M - 1), M, dtype=np.float32)
        _COORDS = np.stack(np.meshgrid(_DP, _DQ, indexing='ij'), axis=-1)
        _RI = (np.arange(2 * N - 1) - (N - 1)) % (2 * N)
        _CI = (np.arange(2 * M - 1) - (M - 1)) % (2 * M)

        def rpe_coeffs(rpe_in_w, rpe_in_b, rpe_h_w, rpe_h_b, rpe_out_w, rpe_out_b):
            t = jnp.asarray(_COORDS) @ rpe_in_w.T + rpe_in_b
            for i in range(RPE_LAYERS):
                t = jax.nn.relu(simple_rms(t)) @ rpe_h_w[i].T + rpe_h_b[i]
            g = jax.nn.relu(simple_rms(t)) @ rpe_out_w.T + rpe_out_b
            g = g.reshape(2 * N - 1, 2 * M - 1, NUM_HEADS, HEAD_DIM)
            return g.transpose(2, 0, 1, 3)

        def tno2d(v, g):
            a = jnp.zeros((NUM_HEADS, 2 * N, 2 * M, HEAD_DIM), dtype=g.dtype)
            a = a.at[:, _RI[:, None], _CI[None, :], :].set(g)
            vf = jnp.fft.rfft2(v, s=(2 * N, 2 * M), axes=(2, 3))
            af = jnp.fft.rfft2(a, axes=(1, 2))
            y = jnp.fft.irfft2(vf * af[None], s=(2 * N, 2 * M), axes=(2, 3))
            return y[:, :, :N, :M, :]
        shortcut = x
        xn = simple_rms(x)
        u = jax.nn.silu(xn @ W_u.T + b_u)
        v = jax.nn.silu(xn @ W_v.T + b_v)
        b = v.shape[0]
        v = v.reshape(b, N, M, NUM_HEADS, HEAD_DIM).transpose(0, 3, 1, 2, 4)
        g = rpe_coeffs(rpe_in_w, rpe_in_b, rpe_h_w, rpe_h_b, rpe_out_w, rpe_out_b)
        y = tno2d(v, g)
        y = y.transpose(0, 2, 3, 1, 4).reshape(b, N, M, D1)
        out = u * y
        return out @ W_o.T + b_o + shortcut

    def _L1_conv_ref(x, Wq, Wk, Wv, conv_w, proj_w, proj_b):
        import jax, jax.numpy as jnp
        import numpy as np
        EPS = 1e-12
        HEADS = 8
        DIM_HEAD = 16

        def _l2norm(t):
            n = jnp.linalg.norm(t, axis=-1, keepdims=True)
            return t / jnp.maximum(n, EPS)
        b, h, w, c = x.shape
        n = h * w
        xs = x.reshape(b, n, c)
        q = xs @ Wq.T
        k = xs @ Wk.T
        v = xs @ Wv.T
        v = v + v
        q = q.reshape(b, n, HEADS, DIM_HEAD)
        k = k.reshape(b, n, HEADS, DIM_HEAD)
        v = v.reshape(b, n, HEADS, DIM_HEAD)
        q = _l2norm(q)
        k = _l2norm(k)
        v_h = _l2norm(v)
        attn_head = jax.nn.softmax(jnp.einsum('bnhd,bngd->bnhg', v_h, v_h), axis=-1)
        q = jnp.einsum('bnhg,bngd->bnhd', attn_head, q)
        k = jnp.einsum('bnhg,bngd->bnhd', attn_head, k)
        attn = jax.nn.softmax(jnp.einsum('bnhd,bnhe->bnde', k, q), axis=-1)
        out = jnp.einsum('bnhd,bnde->bnhe', v, attn)
        out = jnp.transpose(out, (0, 3, 1, 2)).reshape(b, n, HEADS * DIM_HEAD)
        out = out @ proj_w.T + proj_b
        return out.reshape(b, h, w, c)

    def _gn(v, G=32, eps=1e-05):
        B_, H_, W_, C_ = v.shape
        g = v.reshape(B_, H_, W_, G, C_ // G)
        m = jnp.mean(g, axis=(1, 2, 4), keepdims=True)
        s = jnp.var(g, axis=(1, 2, 4), keepdims=True)
        return ((g - m) / jnp.sqrt(s + eps)).reshape(v.shape)

    def _ln_c(v, eps=1e-06):
        m = jnp.mean(v, axis=-1, keepdims=True)
        s = jnp.var(v, axis=-1, keepdims=True)
        return (v - m) / jnp.sqrt(s + eps)

    def _ln_t(v, eps=1e-05):
        m = jnp.mean(v, axis=-1, keepdims=True)
        s = jnp.var(v, axis=-1, keepdims=True)
        return (v - m) / jnp.sqrt(s + eps)

    def _to_tokens(v):
        B_, H_, W_, C_ = v.shape
        return v.reshape(B_, H_ * W_, C_)

    def _from_tokens(t, like):
        return t.reshape(like.shape)
    x = x + _L0_conv_ref(_gn(x), L0_conv_W_u, L0_conv_b_u, L0_conv_W_v, L0_conv_b_v, L0_conv_W_o, L0_conv_b_o, L0_conv_rpe_in_w, L0_conv_rpe_in_b, L0_conv_rpe_h_w, L0_conv_rpe_h_b, L0_conv_rpe_out_w, L0_conv_rpe_out_b, 56, 56)
    x = x + _L1_conv_ref(_gn(x), L1_conv_Wq, L1_conv_Wk, L1_conv_Wv, L1_conv_conv_w, L1_conv_proj_w, L1_conv_proj_b)
    return x

_drawn_inputs = setup_inputs


def setup_inputs(seed=0):
    import zlib

    import numpy as np

    out = dict(_drawn_inputs(seed))
    spreads = {'L1_conv_proj_b': (0.0, 0.1)}
    factors = {'L0_conv_b_o': 5.64,
     'L0_conv_rpe_in_b': 5.431,
     'L1_conv_Wq': 8.0,
     'L1_conv_Wk': 8.0,
     'L1_conv_Wv': 4.699,
     'L1_conv_proj_w': 4.774}
    for name, (base, spread) in spreads.items():
        noise = np.random.default_rng([zlib.crc32(name.encode()), seed]).standard_normal(out[name].shape)
        drawn = base * np.exp(spread * noise) if base else spread * noise
        out[name] = jnp.asarray(drawn.astype(out[name].dtype))
    for name, factor in factors.items():
        out[name] = (out[name] * factor).astype(out[name].dtype)
    return out
```

```python
from contextlib import ExitStack

import concourse.bass as bass
from concourse import mybir

BATCH, SIDE, CH = 8, 56, 128
TOK = SIDE * SIDE
EXP = 2 * CH
GROUP_CH = 4
TAPS = 2 * SIDE - 1
NFFT = 2 * SIDE
NF = NFFT // 2 + 1
HEADS, HD = 8, 16

TT = 112
TPC = 4
COLS = TT * TPC
NCH = TOK // COLS
RC = 4 * TAPS
NRC = TAPS * NFFT // RC
CC = 8
NCC = EXP // CC
RPI = TOK // HEADS // 2
NL = 16
RTOT = BATCH * RPI
RG = 112
NG = RTOT // RG
HALF = RPI // 2

F32 = mybir.dt.float32
ALU = mybir.AluOpType
ACT = mybir.ActivationFunctionType
AX = mybir.AxisListType.X


def bcast(ap, axis, n):
    shape = list(ap.shape)
    shape.insert(axis, n)
    return ap.unsqueeze(axis).to_broadcast(shape)


class Net:
    pass


def scratch(nc, t):
    def dram(name, shape):
        return nc.dram_tensor(name, shape, F32, kind="Internal").ap()
    t.U = dram("gate_u", (BATCH, EXP, TOK))
    t.V = dram("conv_in", (BATCH, EXP, TOK))
    t.S = dram("shortcut", (BATCH, CH, TOK))
    t.G = dram("taps", (EXP, TAPS, NFFT))
    t.Y = dram("conv_out", (BATCH, EXP, TOK))
    t.X1 = dram("x_mid", (BATCH, CH, TOK))
    t.XN = dram("x_mid_normed", (NL, CH, RTOT))
    t.O = dram("heads_out", (RTOT, HD, NL, HEADS))


WEIGHT_TILES = 15
WU, WV, WO, RH, RO, WQ, WK, WVV, PW = 0, 2, 4, 6, 9, 11, 12, 13, 14


def load_weights(nc, t, k):
    with ExitStack() as ctx:
        raw = ctx.enter_context(nc.sbuf_tensor("w_raw", [128, WEIGHT_TILES, 128], F32))
        ps = [ctx.enter_context(nc.psum_tensor(f"w_ps{n}", [128, 512], F32)) for n in range(4)]
        loaded = ctx.enter_context(nc.semaphore("w_loaded"))
        turned = ctx.enter_context(nc.semaphore("w_turned"))
        copied = ctx.enter_context(nc.semaphore("w_copied"))
        filled = ctx.enter_context(nc.semaphore("w_filled"))
        consts = ctx.enter_context(nc.semaphore("consts_loaded"))
        block = ctx.enter_context(nc.Block())
        rows = [
            (WU, 2, t.L0_conv_W_u.rearrange("(a p) c -> p a c", p=128)),
            (WV, 2, t.L0_conv_W_v.rearrange("(a p) c -> p a c", p=128)),
            (WO, 2, t.L0_conv_W_o.rearrange("p (a c) -> p a c", a=2)),
            (RH, 3, t.L0_conv_rpe_h_w.rearrange("a p c -> p a c")),
            (RO, 2, t.L0_conv_rpe_out_w.rearrange("(a p) c -> p a c", p=128)),
            (WQ, 1, t.L1_conv_Wq), (WK, 1, t.L1_conv_Wk), (WVV, 1, t.L1_conv_Wv),
            (PW, 1, t.L1_conv_proj_w),
        ]
        biases = [
            (0, 2, t.L0_conv_b_u.rearrange("(a p) -> p a", p=128)),
            (2, 2, t.L0_conv_b_v.rearrange("(a p) -> p a", p=128)),
            (4, 1, t.L0_conv_b_o.rearrange("(a p) -> p a", p=128)),
            (5, 3, t.L0_conv_rpe_h_b.rearrange("a p -> p a")),
            (8, 2, t.L0_conv_rpe_out_b.rearrange("(a p) -> p a", p=128)),
        ]
        consts_in = [(k.ident[:], t.c_ident), (k.avg[:], t.c_avg), (k.fwd_h[:], t.c_fwd_h),
                     (k.fwd_w[:], t.c_fwd_w), (k.tap_p[:], t.c_tap_p), (k.tap_q[:], t.c_tap_q),
                     (k.inv_w[:], t.c_inv_w), (k.inv_h[:], t.c_inv_h),
                     (k.rpe_in[0:2, :], t.L0_conv_rpe_in_w.rearrange("o i -> i o")),
                     (k.rpe_in[2:3, :], t.L0_conv_rpe_in_b.rearrange("(a o) -> a o", a=1)),
                     (k.proj_b[:], t.L1_conv_proj_b.rearrange("(a o) -> a o", a=1).to_broadcast([128, CH]))]

        @block.sync
        def _(sp):
            for at, n, src in rows:
                dst = raw[:, at:at + n, :] if n > 1 else raw[:, at, :]
                sp.dma_start(dst, src).then_inc(loaded, 16)

        @block.scalar
        def _(act):
            for at, n, src in biases:
                act.dma_start(k.bias[:, at:at + n], src, allow_slow_non_contiguous=True).then_inc(consts, 16)
            for dst, src in consts_in:
                act.dma_start(dst, src, allow_slow_non_contiguous=True).then_inc(consts, 16)
            act.wait_ge(consts, 16 * (len(biases) + len(consts_in)))
            act.wait_ge(loaded, 16 * len(rows))

        @block.vector
        def _(dve):
            dve.memset(k.ones[:], 1.0).then_inc(filled, 1)
            dve.wait_ge(filled, 1)
            for n in range(4):
                lo, hi = 4 * n, min(4 * n + 4, WEIGHT_TILES)
                dve.wait_ge(turned, n + 1)
                dve.tensor_copy(k.w[:, lo:hi, :],
                                ps[n][:, 0:128 * (hi - lo)].rearrange("p (a c) -> p a c", c=128)).then_inc(copied, 1)
            dve.wait_ge(copied, 4)

        @block.tensor
        def _(pe):
            pe.wait_ge(loaded, 16 * len(rows))
            pe.wait_ge(consts, 16 * (len(biases) + len(consts_in)))
            for n in range(4):
                lo, hi = 4 * n, min(4 * n + 4, WEIGHT_TILES)
                for m in range(lo, hi):
                    last = pe.transpose(ps[n][:, 128 * (m - lo):128 * (m - lo) + 128], raw[:, m, :], k.ident[:])
                last.then_inc(turned, 1)


class GroupStats:

    def __init__(self, ctx, nc, name):
        def sb(n, shape):
            return ctx.enter_context(nc.sbuf_tensor(f"{name}_{n}", shape, F32))

        def sem(n):
            return ctx.enter_context(nc.semaphore(f"{name}_{n}"))
        self.parts = sb("bn_parts", [128, NCH, 6])
        self.mv = sb("chan_mv", [128, 2])
        self.gm = sb("group_mv", [128, 2])
        self.dev = sb("dev", [128, 1])
        self.dev2 = sb("dev2", [128, 1])
        self.var = sb("var", [128, 1])
        self.std = sb("std", [128, 1])
        self.scale = sb("scale", [128, 1])
        self.shift = sb("shift", [128, 1])
        self.ps = ctx.enter_context(nc.psum_tensor(f"{name}_ps", [128, 512], F32))
        self.s_seen = sem("seen")
        self.s_parts, self.s_mv, self.s_gm_ps, self.s_gm = sem("parts"), sem("mv"), sem("gm_ps"), sem("gm")
        self.s_dev, self.s_dev2, self.s_dev_ps, self.s_var = sem("dev"), sem("dev2"), sem("dev_ps"), sem("var")
        self.s_var_eps, self.s_std, self.s_scale, self.s_shift = sem("var_eps"), sem("std"), sem("scale_r"), sem("shift_r")

    def on_vector(self, dve, b):
        dve.wait_ge(self.s_parts, (b + 1) * NCH)
        dve.sem_inc(self.s_seen, 1)
        dve.bn_aggr(self.mv[:], self.parts[:]).then_inc(self.s_mv, 1)
        dve.wait_ge(self.s_gm_ps, b + 1)
        dve.tensor_copy(self.gm[:], self.ps[:, 0:2]).then_inc(self.s_gm, 1)
        dve.wait_ge(self.s_gm, b + 1)
        dve.tensor_tensor(self.dev[:], self.mv[:, 0:1], self.gm[:, 0:1], ALU.subtract).then_inc(self.s_dev, 1)
        dve.wait_ge(self.s_dev, b + 1)
        dve.tensor_tensor(self.dev2[:], self.dev[:], self.dev[:], ALU.mult).then_inc(self.s_dev2, 1)
        dve.wait_ge(self.s_dev_ps, b + 1)
        dve.tensor_tensor(self.var[:], self.ps[:, 2:3], self.gm[:, 1:2], ALU.add).then_inc(self.s_var, 1)
        dve.wait_ge(self.s_var, b + 1)
        dve.tensor_scalar(self.var[:], self.var[:], 1e-5, None, ALU.add).then_inc(self.s_var_eps, 1)
        dve.wait_ge(self.s_std, b + 1)
        dve.reciprocal(self.scale[:], self.std[:]).then_inc(self.s_scale, 1)
        dve.wait_ge(self.s_scale, b + 1)
        dve.tensor_scalar(self.shift[:], self.gm[:, 0:1], self.scale[:, 0:1], -1.0, ALU.mult, ALU.mult).then_inc(self.s_shift, 1)
        dve.wait_ge(self.s_shift, b + 1)

    def on_tensor(self, pe, b, avg):
        pe.wait_ge(self.s_mv, b + 1)
        pe.matmul(self.ps[:, 0:2], avg, self.mv[:], start=True, stop=True).then_inc(self.s_gm_ps, 1)
        pe.wait_ge(self.s_dev2, b + 1)
        pe.matmul(self.ps[:, 2:3], avg, self.dev2[:], start=True, stop=True).then_inc(self.s_dev_ps, 1)

    def on_scalar(self, act, b):
        act.wait_ge(self.s_var_eps, b + 1)
        act.activation(self.std[:], self.var[:], ACT.Sqrt).then_inc(self.s_std, 1)


def project_in(nc, t, k):
    with ExitStack() as ctx:
        def sb(n, shape):
            return ctx.enter_context(nc.sbuf_tensor(n, shape, F32))

        def psum(n):
            return ctx.enter_context(nc.psum_tensor(n, [128, 512], F32))

        def sem(n):
            return ctx.enter_context(nc.semaphore(n))
        x_in = [sb(f"x_in{n}", [TT, TPC, CH]) for n in range(2)]
        xT = sb("xT", [128, TOK])
        xg = sb("xg", [128, TOK])
        xr = sb("xr", [128, TOK])
        short = sb("short", [128, TOK])
        sq = sb("sq", [128, COLS])
        rt = sb("rt", [TT, TPC])
        rt_eps = sb("rt_eps", [TT, TPC])
        rinv = sb("rinv", [TT, TPC])
        diag = sb("diag", [TT, TPC, TT])
        uv = [sb(f"uv{n}", [128, 4, COLS]) for n in range(2)]
        gs = GroupStats(ctx, nc, "gn0")
        ps_t, ps_ss, ps_bc = psum("ps_turn"), psum("ps_sumsq"), psum("ps_bcast")
        ps_uv = [psum(f"ps_uv{n}") for n in range(4)]
        x_loaded = [sem(f"x_loaded{n}") for n in range(2)]
        x_turned, x_copied, xg_ready, short_ready = sem("x_turned"), sem("x_copied"), sem("xg_ready"), sem("short_ready")
        sq_ready, ss_ready, rt_ready, eps_ready = sem("sq_ready"), sem("ss_ready"), sem("rt_ready"), sem("eps_ready")
        rinv_ready, diag_ready, bc_ready, xr_ready = sem("rinv_ready"), sem("diag_ready"), sem("bc_ready"), sem("xr_ready")
        uv_ps_ready, uv_ready = sem("uv_ps_ready"), sem("uv_ready")
        uv_stored = [sem(f"uv_stored{n}") for n in range(2)]
        short_stored = sem("short_stored")
        block = ctx.enter_context(nc.Block())
        PER = 2

        def each_chunk():
            return [(a, c, a * NCH + c) for a in range(PER) for c in range(NCH)]

        @block.gpsimd
        def _(pool):
            with pool.Fori(0, BATCH // PER) as i:
                for a, c, n in each_chunk():
                    pool.wait_ge(x_turned, i * (PER * NCH) + n + 1)
                    src = t.x_rows[bass.ds((i * PER + a) * TOK + c * COLS, COLS), :]
                    pool.dma_start(x_in[n % 2][:], src.rearrange("(a p) c -> p a c", p=TT)).then_inc(x_loaded[n % 2], 16)

        @block.tensor
        def _(pe):
            pe.sem_inc(x_turned, 2)
            with pe.Fori(0, BATCH // PER) as i:
                for a in range(PER):
                    b = i * PER + a
                    for c in range(NCH):
                        n = a * NCH + c
                        pe.wait_ge(x_loaded[n % 2], (i * NCH + n // 2 + 1) * 16)
                        pe.wait_ge(x_copied, b * NCH + c + 1)
                        for m in range(TPC):
                            last = pe.transpose(ps_t[:, m * TT:(m + 1) * TT], x_in[n % 2][:, m, :], k.ident[0:TT, 0:TT])
                        last.then_inc(x_turned, 1)
                    gs.on_tensor(pe, b, k.avg[:])
                    for c in range(NCH):
                        pe.wait_ge(sq_ready, b * NCH + c + 1)
                        for m in range(TPC):
                            last = pe.matmul(ps_ss[0:TT, m:m + 1], sq[:, m * TT:(m + 1) * TT], k.ones[:, 0:1], start=True, stop=True)
                        last.then_inc(ss_ready, 1)
                        pe.wait_ge(diag_ready, b * NCH + c + 1)
                        pe.matmul(ps_bc[:, 0:COLS], k.ones[0:TT, :], diag[:].rearrange("p a c -> p (a c)"),
                                  start=True, stop=True).then_inc(bc_ready, 1)
                    for c in range(NCH):
                        pe.wait_ge(xr_ready, b * NCH + c + 1)
                        for m in range(4):
                            pe.wait_ge(uv_ready, (b * NCH + c) * 4 + m + 1)
                            pe.matmul(ps_uv[m][:, 0:COLS], k.w[:, WU + m, :], xr[:, c * COLS:(c + 1) * COLS],
                                      start=True, stop=True).then_inc(uv_ps_ready, 1)

        @block.scalar
        def _(act):
            act.sem_inc(x_copied, 1)
            act.sem_inc(uv_ready, 4)
            with act.Fori(0, BATCH // PER) as i:
                for a in range(PER):
                    b = i * PER + a
                    for c in range(NCH):
                        act.wait_ge(x_turned, b * NCH + c + 3)
                        act.wait_ge(short_ready, (b + 1) * NCH)
                        act.activation(xT[:, c * COLS:(c + 1) * COLS], ps_t[:, 0:COLS], ACT.Copy).then_inc(x_copied, 1)
                    gs.on_scalar(act, b)
                    for c in range(NCH):
                        act.wait_ge(xg_ready, b * NCH + c + 1)
                        act.activation(sq[:], xg[:, c * COLS:(c + 1) * COLS], ACT.Square).then_inc(sq_ready, 1)
                        act.wait_ge(ss_ready, b * NCH + c + 1)
                        act.activation(rt[:], ps_ss[0:TT, 0:TPC], ACT.Sqrt, scale=1.0 / CH).then_inc(rt_ready, 1)
                    for c in range(NCH):
                        n = a * NCH + c
                        act.wait_ge(uv_stored[n % 2], (i * NCH + n // 2 + 1) * 32)
                        for m in range(4):
                            act.wait_ge(uv_ps_ready, (b * NCH + c) * 4 + m + 1)
                            act.activation(uv[n % 2][:, m, :], ps_uv[m][:, 0:COLS], ACT.Silu,
                                           bias=k.bias[:, m:m + 1]).then_inc(uv_ready, 1)

        @block.vector
        def _(dve):
            dve.sem_inc(short_ready, NCH)
            with dve.Fori(0, BATCH // PER) as i:
                for a in range(PER):
                    b = i * PER + a
                    for c in range(NCH):
                        dve.wait_ge(x_copied, b * NCH + c + 2)
                        dve.bn_stats(gs.parts[:, c, :], xT[:, c * COLS:(c + 1) * COLS]).then_inc(gs.s_parts, 1)
                    gs.on_vector(dve, b)
                    for c in range(NCH):
                        cols = slice(c * COLS, (c + 1) * COLS)
                        dve.tensor_scalar(xg[:, cols], xT[:, cols], gs.scale[:, 0:1], gs.shift[:, 0:1],
                                          ALU.mult, ALU.add).then_inc(xg_ready, 1)
                    for c in range(NCH):
                        cols = slice(c * COLS, (c + 1) * COLS)
                        dve.wait_ge(short_stored, (b + 1) * 16)
                        dve.wait_ge(xg_ready, b * NCH + c + 1)
                        dve.scalar_tensor_tensor(out=short[:, cols], in0=xT[:, cols], scalar=k.bias[:, 4:5], in1=xg[:, cols],
                                                 op0=ALU.add, op1=ALU.add).then_inc(short_ready, 1)
                        dve.wait_ge(rt_ready, b * NCH + c + 1)
                        dve.tensor_scalar(rt_eps[:], rt[:], 1e-8, None, ALU.add).then_inc(eps_ready, 1)
                        dve.wait_ge(eps_ready, b * NCH + c + 1)
                        dve.reciprocal(rinv[:], rt_eps[:]).then_inc(rinv_ready, 1)
                        dve.wait_ge(rinv_ready, b * NCH + c + 1)
                        dve.tensor_tensor(diag[:], bcast(k.ident[0:TT, 0:TT], 1, TPC), bcast(rinv[:], 2, TT),
                                          ALU.mult).then_inc(diag_ready, 1)
                        dve.wait_ge(bc_ready, b * NCH + c + 1)
                        dve.wait_ge(uv_ready, (b * NCH) * 4 + 4)
                        dve.tensor_tensor(xr[:, cols], xg[:, cols], ps_bc[:, 0:COLS], ALU.mult).then_inc(xr_ready, 1)

        @block.sync
        def _(sp):
            for n in range(2):
                sp.sem_inc(uv_stored[n], 32)
            sp.sem_inc(short_stored, 16)
            with sp.Fori(0, BATCH // PER) as i:
                for a in range(PER):
                    b = i * PER + a
                    sp.wait_ge(short_ready, (b + 2) * NCH)
                    sp.dma_start(t.S[bass.ds(b, 1)].rearrange("b p t -> (b p) t"), short[:]).then_inc(short_stored, 16)
                    for c in range(NCH):
                        n = a * NCH + c
                        sp.wait_ge(uv_ready, (b * NCH + c) * 4 + 8)
                        for m, dst in ((0, t.U), (2, t.V)):
                            sp.dma_start(dst[bass.ds(b, 1)].rearrange("b (a p) t -> p (b a) t", p=128)[:, :, c * COLS:(c + 1) * COLS],
                                           uv[n % 2][:, m:m + 2, :]).then_inc(uv_stored[n % 2], 16)
            sp.wait_ge(short_stored, 16 * (BATCH + 1))
            for n in range(2):
                sp.wait_ge(uv_stored[n], 32 * (BATCH * NCH // 2 + 1))


def make_taps(nc, t, k):
    with ExitStack() as ctx:
        def sb(n, shape):
            return ctx.enter_context(nc.sbuf_tensor(n, shape, F32))

        def psum(n):
            return ctx.enter_context(nc.psum_tensor(n, [128, 512], F32))

        def sem(n):
            return ctx.enter_context(nc.semaphore(n))
        acts = sb("acts", [128, NRC * RC])
        coords = [sb(f"coords{n}", [3, RC]) for n in range(2)]
        pos = [sb(f"pos_relu{n}", [128, RC]) for n in range(2)]
        sq = [sb(f"pos_sq{n}", [128, RC]) for n in range(2)]
        rt = [sb(f"pos_rt{n}", [TAPS, 4]) for n in range(2)]
        rt_eps = [sb(f"pos_eps{n}", [TAPS, 4]) for n in range(2)]
        rinv = [sb(f"pos_rinv{n}", [TAPS, 4]) for n in range(2)]
        diag = [sb(f"pos_diag{n}", [TAPS, 4, TAPS]) for n in range(2)]
        taps = [sb(f"taps_sb{n}", [128, 2, RC]) for n in range(2)]
        ps_t = [psum(f"ps_pos{n}") for n in range(2)]
        ps_ss = [psum(f"ps_pos_ss{n}") for n in range(2)]
        ps_bc = [psum(f"ps_pos_bc{n}") for n in range(2)]
        ps_g = [psum(f"ps_taps{n}") for n in range(2)]
        c_loaded = [sem(f"coords_loaded{n}") for n in range(2)]
        lin, relu, sqr, ss, rt_s = sem("pos_lin"), sem("pos_relu_r"), sem("pos_sq_r"), sem("pos_ss"), sem("pos_rt_r")
        eps, inv, dg, bc, act_r = sem("pos_eps_r"), sem("pos_inv"), sem("pos_diag_r"), sem("pos_bc"), sem("acts_ready")
        g_ps, g_sb = sem("taps_ps"), sem("taps_copied")
        g_stored = [sem(f"taps_stored{n}") for n in range(2)]
        block = ctx.enter_context(nc.Block())
        PAIRS = NRC // 2
        ROUNDS = 4

        @block.gpsimd
        def _(pool):
            with pool.Fori(0, PAIRS) as i:
                for n in range(2):
                    pool.wait_ge(lin, i * 2 + n + 1)
                    pool.dma_start(coords[n][:], t.c_coords[:, bass.ds((i * 2 + n) * RC, RC)]).then_inc(c_loaded[n], 16)

        @block.tensor
        def _(pe):
            pe.sem_inc(lin, 2)
            for r in range(ROUNDS):
                with pe.Fori(0, PAIRS) as i:
                    for n in range(2):
                        at = i * 2 + n + r * NRC
                        pe.wait_ge(sqr, at + 1)
                        if r == 0:
                            pe.wait_ge(c_loaded[n], i * 16 + 16)
                            pe.matmul(ps_t[n][:, 0:RC], k.rpe_in[:], coords[n][:], start=True, stop=True).then_inc(lin, 1)
                        else:
                            pe.wait_ge(act_r, at - NRC + 3)
                            pe.matmul(ps_t[n][:, 0:RC], k.w[:, RH + r - 1, :], acts[:, bass.ds((i * 2 + n) * RC, RC)],
                                      start=True, stop=True).then_inc(lin, 1)
                    for n in range(2):
                        at = i * 2 + n + r * NRC
                        pe.wait_ge(sqr, at + 3)
                        for m in range(4):
                            last = pe.matmul(ps_ss[n][0:TAPS, m:m + 1], sq[n][:, m * TAPS:(m + 1) * TAPS], k.ones[:, 0:1],
                                             start=True, stop=True)
                        last.then_inc(ss, 1)
                    for n in range(2):
                        at = i * 2 + n + r * NRC
                        pe.wait_ge(dg, at + 1)
                        pe.matmul(ps_bc[n][:, 0:RC], k.ones[0:TAPS, :], diag[n][:].rearrange("p a c -> p (a c)"),
                                  start=True, stop=True).then_inc(bc, 1)
            with pe.Fori(0, PAIRS) as i:
                for n in range(2):
                    pe.wait_ge(act_r, i * 2 + n + (ROUNDS - 1) * NRC + 3)
                    for h in range(2):
                        pe.wait_ge(g_sb, (i * 2 + n) * 2 + h + 1)
                        pe.matmul(ps_g[h][:, 0:RC], k.w[:, RO + h, :], acts[:, bass.ds((i * 2 + n) * RC, RC)],
                                  start=True, stop=True).then_inc(g_ps, 1)

        @block.scalar
        def _(act):
            act.sem_inc(sqr, 2)
            act.sem_inc(g_sb, 2)
            for r in range(ROUNDS):
                bias = 0.0 if r == 0 else k.bias[:, 4 + r:5 + r]
                with act.Fori(0, PAIRS) as i:
                    for n in range(2):
                        at = i * 2 + n + r * NRC
                        act.wait_ge(lin, at + 3)
                        act.wait_ge(act_r, at + 1)
                        act.activation(pos[n][:], ps_t[n][:, 0:RC], ACT.Relu, bias=bias).then_inc(relu, 1)
                        act.activation(sq[n][:], ps_t[n][:, 0:RC], ACT.Square, bias=bias).then_inc(sqr, 1)
                    for n in range(2):
                        at = i * 2 + n + r * NRC
                        act.wait_ge(ss, at + 1)
                        act.activation(rt[n][:], ps_ss[n][0:TAPS, 0:4], ACT.Sqrt, scale=1.0 / CH).then_inc(rt_s, 1)
            with act.Fori(0, PAIRS) as i:
                for n in range(2):
                    act.wait_ge(g_stored[n], i * 16 + 16)
                    for h in range(2):
                        act.wait_ge(g_ps, (i * 2 + n) * 2 + h + 1)
                        act.activation(taps[n][:, h, :], ps_g[h][:, 0:RC], ACT.Identity,
                                       bias=k.bias[:, 8 + h:9 + h]).then_inc(g_sb, 1)

        @block.vector
        def _(dve):
            dve.sem_inc(act_r, 2)
            for r in range(ROUNDS):
                with dve.Fori(0, PAIRS) as i:
                    for n in range(2):
                        at = i * 2 + n + r * NRC
                        dve.wait_ge(rt_s, at + 1)
                        dve.tensor_scalar(rt_eps[n][:], rt[n][:], 1e-8, None, ALU.add).then_inc(eps, 1)
                        dve.wait_ge(eps, at + 1)
                        dve.reciprocal(rinv[n][:], rt_eps[n][:]).then_inc(inv, 1)
                        dve.wait_ge(inv, at + 1)
                        dve.tensor_tensor(diag[n][:], bcast(k.ident[0:TAPS, 0:TAPS], 1, 4), bcast(rinv[n][:], 2, TAPS),
                                          ALU.mult).then_inc(dg, 1)
                    for n in range(2):
                        at = i * 2 + n + r * NRC
                        dve.wait_ge(bc, at + 1)
                        dve.wait_ge(relu, at + 1)
                        dve.tensor_tensor(acts[:, bass.ds((i * 2 + n) * RC, RC)], pos[n][:], ps_bc[n][:, 0:RC],
                                          ALU.mult).then_inc(act_r, 1)

        @block.sync
        def _(sp):
            flat = t.G.rearrange("(a p) r q -> p a (r q)", p=128)
            for n in range(2):
                sp.sem_inc(g_stored[n], 16)
            with sp.Fori(0, PAIRS) as i:
                for n in range(2):
                    sp.wait_ge(g_sb, (i * 2 + n) * 2 + 4)
                    sp.dma_start(flat[:, :, bass.ds((i * 2 + n) * RC, RC)], taps[n][:]).then_inc(g_stored[n], 16)
            for n in range(2):
                sp.wait_ge(g_stored[n], 16 * (PAIRS + 1))


def convolve(nc, t, k):
    PC = CC * NF
    with ExitStack() as ctx:
        def sb(n, shape):
            return ctx.enter_context(nc.sbuf_tensor(n, shape, F32))

        def psum(n):
            return ctx.enter_context(nc.psum_tensor(n, [128, 512], F32))

        def sem(n):
            return ctx.enter_context(nc.semaphore(n))
        g_in = sb("g_in", [TAPS, CC, TAPS])
        g_half = sb("g_half", [TAPS, 2, CC, NF])
        spec = sb("spec", [NFFT, 3, PC])
        v_in = [sb(f"v_in{n}", [120, CC, 120]) for n in range(2)]
        x_half = sb("x_half", [120, PC])
        prod = sb("prod", [NFFT, 3, PC])
        q_half = sb("q_half", [2 * NF, CC // 2, 2, SIDE])
        y_sb = [sb(f"y_sb{n}", [2 * SIDE, CC // 2, SIDE]) for n in range(2)]
        ps_g = [psum(f"ps_g{n}") for n in range(2)]
        ps_x, ps_q, ps_y = psum("ps_x"), psum("ps_q"), psum("ps_y")
        ps_z = [psum(f"ps_z{n}") for n in range(3)]
        cleared = sem("v_cleared")
        g_loaded, g_ps, g_half_r, a_ps, a_ready = sem("g_loaded"), sem("g_half_ps"), sem("g_half_r"), sem("spec_ps"), sem("spec_ready")
        v_loaded = [sem(f"v_loaded{n}") for n in range(2)]
        x_ps, x_half_r, z_ps, prod_r, q_ps, q_r = sem("x_ps"), sem("x_half_r"), sem("z_ps"), sem("prod_r"), sem("q_ps"), sem("q_r")
        y_ps, y_r = sem("y_ps"), sem("y_r")
        y_stored = [sem(f"y_stored{n}") for n in range(2)]
        block = ctx.enter_context(nc.Block())

        @block.gpsimd
        def _(pool):
            pool.wait_ge(cleared, 2)
            with pool.Fori(0, NCC) as i:
                pool.wait_ge(g_ps, i * 2 + 1)
                pool.dma_start(g_in[:], t.G[bass.ds(i * CC, CC), :, 0:TAPS].rearrange("c p q -> p c q")).then_inc(g_loaded, 16)
                for b in range(BATCH):
                    pool.wait_ge(x_ps, i * BATCH + b + 1)
                    src = t.V[b, bass.ds(i * CC, CC), :].rearrange("c (h w) -> h c w", w=SIDE)
                    for at in (0, 64):
                        pool.dma_start(v_in[b % 2][at:at + SIDE, :, at:at + SIDE], src).then_inc(v_loaded[b % 2], 16)

        @block.tensor
        def _(pe):
            pe.sem_inc(x_ps, 2)
            pe.sem_inc(g_ps, 1)
            with pe.Fori(0, NCC) as i:
                def image_h(b):
                    pe.wait_ge(v_loaded[b % 2], (i * (BATCH // 2) + b // 2 + 1) * 32)
                    for c in range(CC):
                        last = pe.matmul(ps_x[0:120, c * NF:(c + 1) * NF], v_in[b % 2][:, c, :], k.fwd_h[:], start=True, stop=True)
                    last.then_inc(x_ps, 1)

                def image_w(b):
                    pe.wait_ge(x_half_r, i * BATCH + b + 1)
                    for n in range(3):
                        last = pe.matmul(ps_z[n][0:NFFT, 0:PC], k.fwd_w[:, n, :], x_half[:], start=True, stop=True)
                    last.then_inc(z_ps, 1)

                def back_w(b):
                    pe.wait_ge(prod_r, i * BATCH + b + 1)
                    for c in range(CC // 2):
                        for n in range(3):
                            pair = prod[:, n, c * 2 * NF:(c + 1) * 2 * NF]
                            last = pe.matmul(ps_q[0:2 * NF, c * NFFT:(c + 1) * NFFT], pair, k.inv_w[:, n, :],
                                             start=(n == 0), stop=(n == 2))
                    last.then_inc(q_ps, 1)

                def back_h(b):
                    pe.wait_ge(q_r, i * BATCH + b + 1)
                    pe.wait_ge(y_r, i * BATCH + b + 1)
                    for n in range(2):
                        last = pe.matmul(ps_y[0:2 * SIDE, 0:CC // 2 * SIDE], k.inv_h[:, n, :], q_half[:, :, n, :],
                                         start=(n == 0), stop=(n == 1))
                    last.then_inc(y_ps, 1)

                pe.wait_ge(g_loaded, i * 16 + 16)
                for n in range(2):
                    for c in range(4):
                        last = pe.matmul(ps_g[n][0:TAPS, c * 2 * NF:(c + 1) * 2 * NF], g_in[:, 4 * n + c, :], k.tap_p[:],
                                         start=True, stop=True)
                    last.then_inc(g_ps, 1)
                image_h(0)
                pe.wait_ge(g_half_r, i * 2 + 2)
                for n in range(3):
                    for ri in range(2):
                        last = pe.matmul(ps_z[n][0:NFFT, 0:PC], k.tap_q[:, 2 * n + ri, :],
                                         g_half[:, ri].rearrange("p c f -> p (c f)"), start=(ri == 0), stop=(ri == 1))
                last.then_inc(a_ps, 1)
                pe.wait_ge(a_ready, i * 3 + 3)
                image_w(0)
                for b in range(BATCH):
                    if b + 1 < BATCH:
                        image_h(b + 1)
                    back_w(b)
                    if b + 1 < BATCH:
                        image_w(b + 1)
                    back_h(b)

        @block.scalar
        def _(act):
            with act.Fori(0, NCC) as i:
                def copy_x(b):
                    act.wait_ge(x_ps, i * BATCH + b + 3)
                    act.activation(x_half[:], ps_x[0:120, 0:PC], ACT.Copy).then_inc(x_half_r, 1)

                for n in range(2):
                    act.wait_ge(g_ps, i * 2 + n + 2)
                    act.activation(g_half[:, :, 4 * n:4 * n + 4, :].rearrange("p r c f -> p c r f"),
                                   ps_g[n][0:TAPS, 0:PC].rearrange("p (c r f) -> p c r f", r=2, f=NF), ACT.Copy).then_inc(g_half_r, 1)
                copy_x(0)
                act.wait_ge(a_ps, i + 1)
                for n in range(3):
                    act.activation(spec[:, n, :], ps_z[n][0:NFFT, 0:PC], ACT.Copy).then_inc(a_ready, 1)
                for b in range(BATCH):
                    if b + 1 < BATCH:
                        copy_x(b + 1)
                    act.wait_ge(q_ps, i * BATCH + b + 1)
                    act.activation(q_half[:].rearrange("p c r w -> p (c r w)"), ps_q[0:2 * NF, 0:CC // 2 * NFFT], ACT.Copy).then_inc(q_r, 1)

        @block.vector
        def _(dve):
            for n in range(2):
                dve.memset(v_in[n][:], 0.0).then_inc(cleared, 1)
            dve.sem_inc(y_r, 1)
            with dve.Fori(0, NCC) as i:
                def copy_y(b):
                    dve.wait_ge(y_ps, i * BATCH + b + 1)
                    dve.wait_ge(y_stored[b % 2], (i * (BATCH // 2) + b // 2 + 1) * 32)
                    dve.tensor_copy(y_sb[b % 2][:].rearrange("p c w -> p (c w)"), ps_y[0:2 * SIDE, 0:CC // 2 * SIDE]).then_inc(y_r, 1)

                dve.wait_ge(a_ready, i * 3 + 3)
                for b in range(BATCH):
                    dve.wait_ge(z_ps, i * BATCH + b + 1)
                    for n, z in ((0, 2), (1, 0), (2, 1)):
                        last = dve.tensor_tensor(prod[:, n, :], spec[:, n, :], ps_z[z][0:NFFT, 0:PC], ALU.mult)
                    last.then_inc(prod_r, 1)
                    if b:
                        copy_y(b - 1)
                copy_y(BATCH - 1)

        @block.sync
        def _(sp):
            for n in range(2):
                sp.sem_inc(y_stored[n], 32)
            with sp.Fori(0, NCC) as i:
                for b in range(BATCH):
                    sp.wait_ge(y_r, i * BATCH + b + 2)
                    for a in range(2):
                        dst = t.Y[b, bass.ds(i * CC, CC), :].rearrange("(c a) (h w) -> a h c w", a=2, w=SIDE)
                        sp.dma_start(dst[a], y_sb[b % 2][a * SIDE:(a + 1) * SIDE]).then_inc(y_stored[b % 2], 16)
            for n in range(2):
                sp.wait_ge(y_stored[n], 32 * (NCC * BATCH // 2 + 1))


def project_out(nc, t, k):
    with ExitStack() as ctx:
        def sb(n, shape):
            return ctx.enter_context(nc.sbuf_tensor(n, shape, F32))

        def psum(n):
            return ctx.enter_context(nc.psum_tensor(n, [128, 512], F32))

        def sem(n):
            return ctx.enter_context(nc.semaphore(n))
        u = [sb(f"u{n}", [128, 2, COLS]) for n in range(2)]
        y = [sb(f"y{n}", [128, 2, COLS]) for n in range(2)]
        s = [sb(f"s{n}", [128, COLS]) for n in range(2)]
        z = [sb(f"z{n}", [128, 2, COLS]) for n in range(2)]
        x1 = sb("x1", [128, TOK])
        xn = sb("xn1", [128, NL, RPI])
        gs = GroupStats(ctx, nc, "gn1")
        ps = [psum(f"ps_wo{n}") for n in range(2)]
        loaded = [sem(f"uys_loaded{n}") for n in range(2)]
        z_ready, o_ps, x1_ready, xn_ready = sem("z_ready"), sem("wo_ps"), sem("x1_ready"), sem("xn_ready")
        x1_stored, xn_stored = sem("x1_stored"), sem("xn_stored")
        block = ctx.enter_context(nc.Block())
        PER = 2

        @block.gpsimd
        def _(pool):
            with pool.Fori(0, BATCH // PER) as i:
                for n in range(PER * NCH):
                    b, c = i * PER + n // NCH, n % NCH
                    cols = slice(c * COLS, (c + 1) * COLS)
                    pool.wait_ge(x1_ready, i * (PER * NCH) + n + 1)
                    for dst, src in ((u, t.U), (y, t.Y)):
                        pool.dma_start(dst[n % 2][:], src[bass.ds(b, 1)].rearrange("b (a p) t -> p (b a) t", p=128)[:, :, cols])\
                          .then_inc(loaded[n % 2], 16)
                    pool.dma_start(s[n % 2][:], t.S[bass.ds(b, 1)].rearrange("b p t -> (b p) t")[:, cols]).then_inc(loaded[n % 2], 16)

        @block.vector
        def _(dve):
            dve.sem_inc(x1_ready, 2)
            with dve.Fori(0, BATCH // PER) as i:
                for a in range(PER):
                    b = i * PER + a
                    dve.wait_ge(x1_stored, (b + 1) * 16)
                    dve.wait_ge(xn_ready, (b + 1) * 4)
                    def gate(c):
                        n = a * NCH + c
                        dve.wait_ge(loaded[n % 2], (i * NCH + n // 2 + 1) * 48)
                        dve.tensor_tensor(z[n % 2][:], u[n % 2][:], y[n % 2][:], ALU.mult).then_inc(z_ready, 1)
                    gate(0)
                    for c in range(NCH):
                        n = a * NCH + c
                        if c + 1 < NCH:
                            gate(c + 1)
                        dve.wait_ge(o_ps, b * NCH + c + 1)
                        dve.tensor_tensor(x1[:, c * COLS:(c + 1) * COLS], s[n % 2][:], ps[n % 2][:, 0:COLS], ALU.add).then_inc(x1_ready, 1)
                        dve.wait_ge(x1_ready, b * NCH + c + 3)
                        dve.bn_stats(gs.parts[:, c, :], x1[:, c * COLS:(c + 1) * COLS]).then_inc(gs.s_parts, 1)
                    gs.on_vector(dve, b)

        @block.tensor
        def _(pe):
            with pe.Fori(0, BATCH // PER) as i:
                for a in range(PER):
                    b = i * PER + a
                    for c in range(NCH):
                        n = a * NCH + c
                        pe.wait_ge(z_ready, b * NCH + c + 1)
                        pe.wait_ge(x1_ready, b * NCH + c + 1)
                        for m in range(2):
                            last = pe.matmul(ps[n % 2][:, 0:COLS], k.w[:, WO + m, :], z[n % 2][:, m, :], start=(m == 0), stop=(m == 1))
                        last.then_inc(o_ps, 1)
                    gs.on_tensor(pe, b, k.avg[:])

        @block.scalar
        def _(act):
            act.sem_inc(xn_ready, 4)
            with act.Fori(0, BATCH // PER) as i:
                for a in range(PER):
                    b = i * PER + a
                    gs.on_scalar(act, b)
                    act.wait_ge(gs.s_shift, b + 1)
                    act.wait_ge(xn_stored, (b + 1) * 16)
                    rows = x1[:].rearrange("p (r n) -> p n r", n=NL)
                    for m in range(4):
                        act.activation(xn[:, 4 * m:4 * m + 4, :], rows[:, 4 * m:4 * m + 4, :], ACT.Identity,
                                       bias=gs.shift[:, 0:1], scale=gs.scale[:, 0:1]).then_inc(xn_ready, 1)

        @block.sync
        def _(sp):
            sp.sem_inc(x1_stored, 16)
            sp.sem_inc(xn_stored, 16)
            with sp.Fori(0, BATCH) as b:
                sp.wait_ge(x1_ready, b * NCH + NCH + 2)
                sp.dma_start(t.X1[bass.ds(b, 1)].rearrange("b p t -> (b p) t"), x1[:]).then_inc(x1_stored, 16)
                sp.wait_ge(xn_ready, b * 4 + 8)
                sp.dma_start(t.XN[:, :, bass.ds(b * RPI, RPI)].rearrange("n p r -> p n r"), xn[:]).then_inc(xn_stored, 16)
            sp.wait_ge(x1_stored, 16 * (BATCH + 1))
            sp.wait_ge(xn_stored, 16 * (BATCH + 1))


def attend(nc, t, k):
    with ExitStack() as ctx:
        def sb(n, shape):
            return ctx.enter_context(nc.sbuf_tensor(n, shape, F32))

        def psum(n):
            return ctx.enter_context(nc.psum_tensor(n, [128, 512], F32))

        def sem(n):
            return ctx.enter_context(nc.semaphore(n))

        def two(n, shape):
            return [sb(f"{n}{m}", shape) for m in range(2)]
        D = CH
        xn = [sb(f"xn_in{m}", [128, 2, RG]) for m in range(2)]
        sq = two("sq", [RG, 3 * D])
        v2 = two("v2", [RG, D])
        norm_sq, norm, norm_c, norm_i = two("norm_sq", [RG, 24]), two("norm", [RG, 24]), two("norm_c", [RG, 24]), two("norm_i", [RG, 24])
        qk, vh = two("qk", [RG, 2 * D]), two("vh", [RG, D])
        small = two("small_prod", [RG, HEADS * HEADS * HD])
        big = two("big_prod", [RG, HEADS * HD * HD])
        S, S_max, S_sh, A_exp = two("S", [RG, 64]), two("S_max", [RG, 8]), two("S_sh", [RG, 64]), two("A_exp", [RG, 64])
        A_sum, A_inv, A, B = two("A_sum", [RG, 8]), two("A_inv", [RG, 8]), two("A", [RG, 64]), two("B", [RG, 64])
        L_max, L_sh, P_exp = two("L_max", [RG, 16]), two("L_sh", [RG, 256]), two("P_exp", [RG, 256])
        P_sum, P_inv, v_sc = two("P_sum", [RG, 16]), two("P_inv", [RG, 16]), two("v_sc", [RG, D])
        o_sb = [sb(f"o_sb{m}", [RG, HD, NL, HEADS]) for m in range(2)]
        ps_qkv = [psum(f"ps_qkv{m}") for m in range(2)]
        ps_r = [psum(f"ps_sum{m}") for m in range(2)]
        xn_loaded = [sem(f"xn_loaded{m}") for m in range(2)]
        names = ("qkv_ps sq_r sqv_r v2_r nsq_r norm_r nc_r ni_r qh_r vh_r sprod_r s_r smax_r ssh_r aexp_r asum_r ainv_r a_r "
                 "bprod_r b_r mprod_r m_ps lprod_r l_ps lmax_r lsh_r pexp_r psum_r pinv_r vsc_r oprod_r o_ps o_r").split()
        s = {n: sem("at_" + n) for n in names}
        o_stored = sem("o_stored")
        block = ctx.enter_context(nc.Block())
        PAIRS = NL // 2

        @block.gpsimd
        def _(pool):
            with pool.Fori(0, NG) as g:
                with pool.Fori(0, PAIRS // 2) as p:
                    for m in range(2):
                        i = g * PAIRS + p * 2 + m
                        pool.wait_ge(s["qkv_ps"], i * 2 + 2)
                        pool.dma_start(xn[m][:], t.XN[bass.ds(p * 4 + m * 2, 2), :, bass.ds(g * RG, RG)].rearrange("n p r -> p n r"))\
                          .then_inc(xn_loaded[m], 16)

        def pair_loop(eng, body):
            with eng.Fori(0, NG) as g:
                with eng.Fori(0, PAIRS // 2) as p:
                    for m in range(2):
                        body(g, p, m, (g * PAIRS + p * 2 + m) * 2)

        @block.tensor
        def _(pe):
            pe.sem_inc(s["qkv_ps"], 4)

            def body(g, p, m, i):
                pe.wait_ge(xn_loaded[m], g * (PAIRS // 2 * 16) + p * 16 + 16)
                for j in range(2):
                    pe.wait_ge(s["qh_r"], i + j + 1)
                    pe.wait_ge(s["v2_r"], i + j + 1)
                    pe.matmul(ps_qkv[j][0:RG, 0:3 * D], xn[m][:, j, :], k.w[:, WQ:WQ + 3, :].rearrange("p a c -> p (a c)"),
                              start=True, stop=True).then_inc(s["qkv_ps"], 1)

                def summed(j, product, ready, terms, width, done):
                    pe.wait_ge(s[ready], i + j + 1)
                    for n in range(terms):
                        last = pe.matmul(ps_r[j][0:RG, 0:width], k.ident[0:RG, 0:RG], product[:, n * width:(n + 1) * width],
                                         start=(n == 0), stop=(n == terms - 1))
                    last.then_inc(s[done], 1)
                for j in range(2):
                    pe.wait_ge(s["o_r"], i + j + 1)
                    summed(j, big[j][:, 0:8 * 128], "mprod_r", HEADS, 128, "m_ps")
                for j in range(2):
                    summed(j, big[j][:, :], "lprod_r", HEADS, 256, "l_ps")
                for j in range(2):
                    summed(j, big[j][:, :], "oprod_r", HD, 128, "o_ps")
            pair_loop(pe, body)

        @block.scalar
        def _(act):
            act.sem_inc(s["v2_r"], 2)
            act.sem_inc(s["o_r"], 2)

            def body(g, p, m, i):
                for j in range(2):
                    act.wait_ge(s["qkv_ps"], i + j + 5)
                    act.activation(sq[j][:, 0:2 * D], ps_qkv[j][0:RG, 0:2 * D], ACT.Square).then_inc(s["sq_r"], 1)
                    act.activation(sq[j][:, 2 * D:3 * D], ps_qkv[j][0:RG, 2 * D:3 * D], ACT.Square, scale=2.0).then_inc(s["sqv_r"], 1)
                    act.activation(v2[j][:], ps_qkv[j][0:RG, 2 * D:3 * D], ACT.Copy, scale=2.0).then_inc(s["v2_r"], 1)
                for j in range(2):
                    act.wait_ge(s["nsq_r"], i + j + 1)
                    act.activation(norm[j][:], norm_sq[j][:], ACT.Sqrt).then_inc(s["norm_r"], 1)
                for j in range(2):
                    act.wait_ge(s["ssh_r"], i + j + 1)
                    act.activation(A_exp[j][:], S_sh[j][:], ACT.Exp).then_inc(s["aexp_r"], 1)
                for j in range(2):
                    act.wait_ge(s["lsh_r"], i + j + 1)
                    act.activation(P_exp[j][:], L_sh[j][:], ACT.Exp).then_inc(s["pexp_r"], 1)
                act.wait_ge(o_stored, g * 16 + 16)
                for j in range(2):
                    act.wait_ge(s["o_ps"], i + j + 1)
                    act.activation(o_sb[0][:, :, bass.ds(p * 4 + m * 2 + j, 1), :].rearrange("p e n h -> p e (n h)"),
                                   ps_r[j][0:RG, 0:128].rearrange("p (e h) -> p e h", h=HEADS), ACT.Copy).then_inc(s["o_r"], 1)
            pair_loop(act, body)

        @block.vector
        def _(dve):
            dve.sem_inc(s["qh_r"], 2)

            def body(g, p, m, i):
                both = range(2)

                def after(j, *waits):
                    for n in waits:
                        dve.wait_ge(s[n], i + j + 1)
                for j in both:
                    after(j, "sq_r", "sqv_r")
                    dve.tensor_reduce(norm_sq[j][:], sq[j][:].rearrange("p (a d) -> p a d", d=HD), AX, ALU.add).then_inc(s["nsq_r"], 1)
                for j in both:
                    after(j, "norm_r")
                    dve.tensor_scalar(norm_c[j][:], norm[j][:], 1e-12, None, ALU.max).then_inc(s["nc_r"], 1)
                for j in both:
                    after(j, "nc_r")
                    dve.reciprocal(norm_i[j][:], norm_c[j][:]).then_inc(s["ni_r"], 1)
                for j in both:
                    after(j, "ni_r")
                    dve.wait_ge(s["v2_r"], i + j + 3)
                    dve.tensor_tensor(vh[j][:].rearrange("p (h d) -> p h d", d=HD), v2[j][:].rearrange("p (h d) -> p h d", d=HD),
                                      bcast(norm_i[j][:, 16:24], 2, HD), ALU.mult).then_inc(s["vh_r"], 1)
                    dve.tensor_tensor(qk[j][:].rearrange("p (h d) -> p h d", d=HD),
                                      ps_qkv[j][0:RG, 0:2 * D].rearrange("p (h d) -> p h d", d=HD),
                                      bcast(norm_i[j][:, 0:16], 2, HD), ALU.mult).then_inc(s["qh_r"], 1)
                for j in both:
                    after(j, "vh_r")
                    v = vh[j][:].rearrange("p (h d) -> p h d", d=HD)
                    dve.tensor_tensor(small[j][:].rearrange("p (h g d) -> p h g d", h=HEADS, d=HD), bcast(v, 2, HEADS), bcast(v, 1, HEADS),
                                      ALU.mult).then_inc(s["sprod_r"], 1)
                for j in both:
                    after(j, "sprod_r")
                    dve.tensor_reduce(S[j][:], small[j][:].rearrange("p (a d) -> p a d", d=HD), AX, ALU.add).then_inc(s["s_r"], 1)
                for j in both:
                    after(j, "s_r")
                    dve.tensor_reduce(S_max[j][:], S[j][:].rearrange("p (h g) -> p h g", g=HEADS), AX, ALU.max).then_inc(s["smax_r"], 1)
                for j in both:
                    after(j, "smax_r")
                    dve.tensor_tensor(S_sh[j][:].rearrange("p (h g) -> p h g", g=HEADS), S[j][:].rearrange("p (h g) -> p h g", g=HEADS),
                                      bcast(S_max[j][:], 2, HEADS), ALU.subtract).then_inc(s["ssh_r"], 1)
                for j in both:
                    after(j, "aexp_r")
                    dve.tensor_reduce(A_sum[j][:], A_exp[j][:].rearrange("p (h g) -> p h g", g=HEADS), AX, ALU.add).then_inc(s["asum_r"], 1)
                for j in both:
                    after(j, "asum_r")
                    dve.reciprocal(A_inv[j][:], A_sum[j][:]).then_inc(s["ainv_r"], 1)
                for j in both:
                    after(j, "ainv_r")
                    dve.tensor_tensor(A[j][:].rearrange("p (h g) -> p h g", g=HEADS), A_exp[j][:].rearrange("p (h g) -> p h g", g=HEADS),
                                      bcast(A_inv[j][:], 2, HEADS), ALU.mult).then_inc(s["a_r"], 1)
                for j in both:
                    after(j, "a_r")
                    a = A[j][:].rearrange("p (h g) -> p g h", g=HEADS)
                    dve.tensor_tensor(small[j][:, 0:512].rearrange("p (g f h) -> p g f h", g=HEADS, h=HEADS), bcast(a, 2, HEADS), bcast(a, 1, HEADS),
                                      ALU.mult).then_inc(s["bprod_r"], 1)
                for j in both:
                    after(j, "bprod_r")
                    dve.tensor_reduce(B[j][:], small[j][:, 0:512].rearrange("p (a h) -> p a h", h=HEADS), AX, ALU.add).then_inc(s["b_r"], 1)
                for j in both:
                    after(j, "b_r")
                    dve.wait_ge(s["qh_r"], i + j + 3)
                    q = qk[j][:, 0:D].rearrange("p (h d) -> p h d", d=HD)
                    dve.tensor_tensor(big[j][:, 0:1024].rearrange("p (f g e) -> p f g e", f=HEADS, e=HD),
                                      bcast(B[j][:].rearrange("p (f g) -> p f g", f=HEADS), 3, HD), bcast(q, 2, HEADS),
                                      ALU.mult).then_inc(s["mprod_r"], 1)
                for j in both:
                    after(j, "m_ps")
                    kk = qk[j][:, D:2 * D].rearrange("p (h d) -> p h d", d=HD)
                    mm = ps_r[j][0:RG, 0:128].rearrange("p (g e) -> p g e", e=HD)
                    dve.tensor_tensor(big[j][:].rearrange("p (g d e) -> p g d e", g=HEADS, e=HD), bcast(kk, 3, HD), bcast(mm, 2, HD),
                                      ALU.mult).then_inc(s["lprod_r"], 1)
                for j in both:
                    after(j, "l_ps")
                    dve.tensor_reduce(L_max[j][:], ps_r[j][0:RG, 0:256].rearrange("p (d e) -> p d e", e=HD), AX, ALU.max).then_inc(s["lmax_r"], 1)
                for j in both:
                    after(j, "lmax_r")
                    dve.tensor_tensor(L_sh[j][:].rearrange("p (d e) -> p d e", e=HD), ps_r[j][0:RG, 0:256].rearrange("p (d e) -> p d e", e=HD),
                                      bcast(L_max[j][:], 2, HD), ALU.subtract).then_inc(s["lsh_r"], 1)
                for j in both:
                    after(j, "pexp_r")
                    dve.tensor_reduce(P_sum[j][:], P_exp[j][:].rearrange("p (d e) -> p d e", e=HD), AX, ALU.add).then_inc(s["psum_r"], 1)
                for j in both:
                    after(j, "psum_r")
                    dve.reciprocal(P_inv[j][:], P_sum[j][:]).then_inc(s["pinv_r"], 1)
                for j in both:
                    after(j, "pinv_r")
                    dve.tensor_tensor(v_sc[j][:].rearrange("p (d h) -> p d h", h=HEADS), v2[j][:].rearrange("p (h d) -> p d h", d=HD),
                                      bcast(P_inv[j][:], 2, HEADS), ALU.mult).then_inc(s["vsc_r"], 1)
                for j in both:
                    after(j, "vsc_r")
                    dve.tensor_tensor(big[j][:].rearrange("p (d e h) -> p d e h", d=HD, h=HEADS),
                                      bcast(P_exp[j][:].rearrange("p (d e) -> p d e", e=HD), 3, HEADS),
                                      bcast(v_sc[j][:].rearrange("p (d h) -> p d h", h=HEADS), 2, HD), ALU.mult).then_inc(s["oprod_r"], 1)
            pair_loop(dve, body)

        @block.sync
        def _(sp):
            sp.sem_inc(o_stored, 16)
            with sp.Fori(0, NG) as g:
                sp.wait_ge(s["o_r"], g * NL + NL + 2)
                sp.dma_start(t.O[bass.ds(g * RG, RG)].rearrange("r e n h -> r (e n h)"),
                               o_sb[0][:].rearrange("r e n h -> r (e n h)")).then_inc(o_stored, 16)
            sp.wait_ge(o_stored, 16 * (NG + 1))


def project_final(nc, t, k):
    with ExitStack() as ctx:
        def sb(n, shape):
            return ctx.enter_context(nc.sbuf_tensor(n, shape, F32))

        def psum(n):
            return ctx.enter_context(nc.psum_tensor(n, [128, 512], F32))

        def sem(n):
            return ctx.enter_context(nc.semaphore(n))
        o_in = [sb(f"o_in{n}", [HALF, 2, 2, 128]) for n in range(2)]
        x_in = [sb(f"x1_in{n}", [128, 2, 2, HALF]) for n in range(2)]
        oT = [sb(f"oT{n}", [128, 4, HALF]) for n in range(2)]
        res = [sb(f"res{n}", [HALF, 4, CH]) for n in range(2)]
        ps_t = [psum(f"ps_ot{n}") for n in range(2)]
        ps_o = [psum(f"ps_out{n}") for n in range(2)]
        loaded = [sem(f"fin_loaded{n}") for n in range(2)]
        turned, copied, summed, done = sem("o_turned"), sem("o_copied"), sem("out_ps"), sem("out_ready")
        stored = [sem(f"out_stored{n}") for n in range(2)]
        block = ctx.enter_context(nc.Block())
        STEPS = BATCH * HD // 2
        EP = HD // 2

        def step_loop(eng, body):
            with eng.Fori(0, BATCH) as b:
                with eng.Fori(0, EP // 2) as q:
                    for n in range(2):
                        body(b, q, n, b * EP + q * 2 + n)

        @block.gpsimd
        def _(pool):
            def body(b, q, n, at):
                pool.wait_ge(summed, at + 1)
                for half in range(2):
                    pool.dma_start(o_in[n][:, half],
                                 t.O[bass.ds(b * RPI + half * HALF, HALF), bass.ds(q * 4 + n * 2, 2)].rearrange("r e n h -> r e (n h)"))\
                      .then_inc(loaded[n], 16)
                pool.dma_start(x_in[n][:].rearrange("p e a r -> p (e a r)"),
                             t.X1[bass.ds(b, 1)].rearrange("b p t -> (b p) t")[:, bass.ds((q * 2 + n) * 2 * RPI, 2 * RPI)])\
                  .then_inc(loaded[n], 16)
            step_loop(pool, body)

        @block.tensor
        def _(pe):
            pe.sem_inc(summed, 2)

            def body(b, q, n, at):
                pe.wait_ge(loaded[n], b * (EP // 2 * 48) + q * 48 + 48)
                for e in range(2):
                    for half in range(2):
                        m = 2 * e + half
                        last = pe.transpose(ps_t[n][:, m * HALF:(m + 1) * HALF], o_in[n][:, half, e, :], k.ident[0:HALF, 0:HALF])
                last.then_inc(turned, 1)
                pe.wait_ge(copied, at + 1)
                pe.wait_ge(done, at + 1)
                for m in range(4):
                    out = ps_o[n][0:HALF, m * CH:(m + 1) * CH]
                    pe.matmul(out, oT[n][:, m, :], k.w[:, PW, :], start=True, stop=False)
                    last = pe.matmul(out, x_in[n][:, m // 2, m % 2, :], k.ident[:], start=False, stop=True)
                last.then_inc(summed, 1)
            step_loop(pe, body)

        @block.scalar
        def _(act):
            def body(b, q, n, at):
                act.wait_ge(turned, at + 1)
                act.activation(oT[n][:].rearrange("p a r -> p (a r)"), ps_t[n][:, 0:4 * HALF], ACT.Copy).then_inc(copied, 1)
            step_loop(act, body)

        @block.vector
        def _(dve):
            dve.sem_inc(done, 2)

            def body(b, q, n, at):
                dve.wait_ge(summed, at + 3)
                dve.wait_ge(stored[n], b * (EP // 2 * 16) + q * 16 + 16)
                dve.tensor_tensor(res[n][:], ps_o[n][0:HALF, :].rearrange("p (a c) -> p a c", a=4),
                                  bcast(k.proj_b[0:HALF, :], 1, 4), ALU.add).then_inc(done, 1)
            step_loop(dve, body)

        @block.sync
        def _(sp):
            for n in range(2):
                sp.sem_inc(stored[n], 16)

            def body(b, q, n, at):
                sp.wait_ge(done, at + 3)
                row = b * TOK + (q * 2 + n) * 2 * RPI
                sp.dma_start(t.out_rows[bass.ds(row, 2 * RPI), :].rearrange("(a r) c -> r a c", r=HALF), res[n][:]).then_inc(stored[n], 16)
            step_loop(sp, body)
            for n in range(2):
                sp.wait_ge(stored[n], 16 * (STEPS // 2 + 1))


def build(nc, t):
    scratch(nc, t)
    with ExitStack() as ctx:
        k = Net()

        def sb(n, shape):
            return ctx.enter_context(nc.sbuf_tensor(n, shape, F32))
        k.w = sb("weights", [128, WEIGHT_TILES, 128])
        k.bias = sb("biases", [128, 10])
        k.ident, k.avg, k.ones = sb("ident", [128, 128]), sb("group_avg", [128, 128]), sb("ones", [128, 128])
        k.rpe_in = sb("rpe_in", [3, 128])
        k.proj_b = sb("proj_b", [128, CH])
        k.fwd_h, k.fwd_w = sb("fwd_h", [120, NF]), sb("fwd_w", [120, 3, NFFT])
        k.tap_p, k.tap_q = sb("tap_p", [TAPS, 2 * NF]), sb("tap_q", [TAPS, 6, NFFT])
        k.inv_w, k.inv_h = sb("inv_w", [NFFT, 3, NFFT]), sb("inv_h", [2 * NF, 2, 2 * SIDE])
        load_weights(nc, t, k)
        project_in(nc, t, k)
        make_taps(nc, t, k)
        convolve(nc, t, k)
        project_out(nc, t, k)
        attend(nc, t, k)
        project_final(nc, t, k)


def tables():
    import numpy as np
    two_pi = 2.0 * np.pi / NFFT
    f, g, m = np.arange(NF), np.arange(NFFT), np.arange(SIDE)
    taps = np.arange(TAPS) - (SIDE - 1)
    c = {}
    c["c_ident"] = np.eye(128)
    c["c_avg"] = np.kron(np.eye(128 // GROUP_CH), np.full((GROUP_CH, GROUP_CH), 1.0 / GROUP_CH))
    a = two_pi * np.outer(m, f)
    fh = np.zeros((120, NF)); fh[0:SIDE], fh[64:120] = np.cos(a), -np.sin(a)
    c["c_fwd_h"] = fh
    a = two_pi * np.outer(m, g)
    cw, sw = np.cos(a), np.sin(a)
    fw = np.zeros((120, 3, NFFT))
    fw[0:SIDE, 0], fw[64:120, 0] = cw, sw
    fw[0:SIDE, 1], fw[64:120, 1] = -sw, cw
    fw[0:SIDE, 2], fw[64:120, 2] = cw - sw, cw + sw
    c["c_fwd_w"] = fw
    a = two_pi * np.outer(taps, f)
    c["c_tap_p"] = np.concatenate([np.cos(a), -np.sin(a)], axis=1)
    a = two_pi * np.outer(taps, g)
    cq, sq = np.cos(a), np.sin(a)
    c["c_tap_q"] = np.stack([cq, sq, -sq - cq, cq - sq, cq - sq, cq + sq], axis=1)
    a = two_pi * np.outer(g, m)
    ci, si = np.cos(a) / NFFT, np.sin(a) / NFFT
    c["c_inv_w"] = np.stack([np.concatenate([ci - si, ci + si], 1), np.concatenate([-si, ci], 1),
                             np.concatenate([-ci, -si], 1)], axis=1)
    a = two_pi * np.outer(f, m)
    weight = np.where((f == 0) | (f == NF - 1), 1.0, 2.0)[:, None] / NFFT
    ih = np.zeros((2 * NF, 2, 2 * SIDE))
    for n, part in enumerate((weight * np.cos(a), -weight * np.sin(a))):
        ih[0:NF, n, 0:SIDE], ih[NF:, n, SIDE:] = part, part
    c["c_inv_h"] = ih
    p, q = np.meshgrid(np.arange(TAPS), np.arange(NFFT), indexing="ij")
    c["c_coords"] = np.stack([(p - (SIDE - 1)).ravel(), (q - (SIDE - 1)).ravel(), np.ones(TAPS * NFFT)])
    return {n: np.ascontiguousarray(v, dtype=np.float32) for n, v in c.items()}


_INS = ['x', 'L0_conv_W_u', 'L0_conv_b_u', 'L0_conv_W_v', 'L0_conv_b_v', 'L0_conv_W_o', 'L0_conv_b_o', 'L0_conv_rpe_in_w',
        'L0_conv_rpe_in_b', 'L0_conv_rpe_h_w', 'L0_conv_rpe_h_b', 'L0_conv_rpe_out_w', 'L0_conv_rpe_out_b', 'L1_conv_Wq',
        'L1_conv_Wk', 'L1_conv_Wv', 'L1_conv_proj_w', 'L1_conv_proj_b']


def kernel(**inputs):
    import numpy as _np
    import concourse.bacc as _bacc
    from concourse import mybir as _mybir
    from concourse.bass_utils import run_bass_kernel_spmd as _run

    nc = _bacc.Bacc("TRN2", target_bir_lowering=False, num_devices=1)
    arrays = {f"in_{n}": _np.ascontiguousarray(inputs[n]) for n in _INS}
    consts = tables()
    arrays.update({f"in_{n}": a for n, a in consts.items()})
    t = Net()
    t.__dict__.update({n[3:]: nc.dram_tensor(n, a.shape, _mybir.dt.from_np(a.dtype), kind="ExternalInput").ap()
                       for n, a in arrays.items()})
    out = nc.dram_tensor("out_0", (BATCH, SIDE, SIDE, CH), F32, kind="ExternalOutput").ap()
    t.x_rows = t.x.rearrange("b h w c -> (b h w) c")
    t.out_rows = out.rearrange("b h w c -> (b h w) c")
    build(nc, t)
    r = _run(nc, [arrays], core_ids=[0])
    return r.results[0]["out_0"]
```

```python
from contextlib import ExitStack

import concourse.bass as bass
from concourse import mybir

BATCH, SIDE, CH = 8, 56, 128
TOK = SIDE * SIDE
EXP = 2 * CH
GROUP_CH = 4
TAPS = 2 * SIDE - 1
NFFT = 2 * SIDE
NF = NFFT // 2 + 1
HEADS, HD = 8, 16

TT = 112
TPC = 4
COLS = TT * TPC
NCH = TOK // COLS
RC = 4 * TAPS
NRC = TAPS * NFFT // RC
CC = 8
NCC = EXP // CC
RPI = TOK // HEADS // 2
NL = 16
RTOT = BATCH * RPI
RG = 112
NG = RTOT // RG
HALF = RPI // 2

F32 = mybir.dt.float32
ALU = mybir.AluOpType
ACT = mybir.ActivationFunctionType
AX = mybir.AxisListType.X


def bcast(ap, axis, n):
    shape = list(ap.shape)
    shape.insert(axis, n)
    return ap.unsqueeze(axis).to_broadcast(shape)


class Net:
    pass


def scratch(nc, t):
    def dram(name, shape):
        return nc.dram_tensor(name, shape, F32, kind="Internal").ap()
    t.U = dram("gate_u", (BATCH, EXP, TOK))
    t.V = dram("conv_in", (BATCH, EXP, TOK))
    t.S = dram("shortcut", (BATCH, CH, TOK))
    t.G = dram("taps", (EXP, TAPS, NFFT))
    t.Y = dram("conv_out", (BATCH, EXP, TOK))
    t.X1 = dram("x_mid", (BATCH, CH, TOK))
    t.XN = dram("x_mid_normed", (NL, CH, RTOT))
    t.O = dram("heads_out", (RTOT, NL // 2, HD * 2 * HEADS))


WEIGHT_TILES = 15
WU, WV, WO, RH, RO, WQ, WK, WVV, PW = 0, 2, 4, 6, 9, 11, 12, 13, 14


def load_weights(nc, t, k):
    with ExitStack() as ctx:
        raw = ctx.enter_context(nc.sbuf_tensor("w_raw", [128, WEIGHT_TILES, 128], F32))
        ps = [ctx.enter_context(nc.psum_tensor(f"w_ps{n}", [128, 512], F32)) for n in range(4)]
        loaded = ctx.enter_context(nc.semaphore("w_loaded"))
        turned = ctx.enter_context(nc.semaphore("w_turned"))
        copied = ctx.enter_context(nc.semaphore("w_copied"))
        filled = ctx.enter_context(nc.semaphore("w_filled"))
        consts = ctx.enter_context(nc.semaphore("consts_loaded"))
        block = ctx.enter_context(nc.Block())
        rows = [
            (WU, 2, t.L0_conv_W_u.rearrange("(a p) c -> p a c", p=128)),
            (WV, 2, t.L0_conv_W_v.rearrange("(a p) c -> p a c", p=128)),
            (WO, 2, t.L0_conv_W_o.rearrange("p (a c) -> p a c", a=2)),
            (RH, 3, t.L0_conv_rpe_h_w.rearrange("a p c -> p a c")),
            (RO, 2, t.L0_conv_rpe_out_w.rearrange("(a p) c -> p a c", p=128)),
            (WQ, 1, t.L1_conv_Wq), (WK, 1, t.L1_conv_Wk), (WVV, 1, t.L1_conv_Wv),
            (PW, 1, t.L1_conv_proj_w),
        ]
        biases = [
            (0, 2, t.L0_conv_b_u.rearrange("(a p) -> p a", p=128)),
            (2, 2, t.L0_conv_b_v.rearrange("(a p) -> p a", p=128)),
            (4, 1, t.L0_conv_b_o.rearrange("(a p) -> p a", p=128)),
            (5, 3, t.L0_conv_rpe_h_b.rearrange("a p -> p a")),
            (8, 2, t.L0_conv_rpe_out_b.rearrange("(a p) -> p a", p=128)),
        ]
        consts_in = [(k.ident[:], t.c_ident), (k.avg[:], t.c_avg), (k.fwd_h[:], t.c_fwd_h),
                     (k.fwd_w[:], t.c_fwd_w), (k.tap_p[:], t.c_tap_p), (k.tap_q[:], t.c_tap_q),
                     (k.inv_w[:], t.c_inv_w), (k.inv_h[:], t.c_inv_h),
                     (k.rpe_in[0:2, :], t.L0_conv_rpe_in_w.rearrange("o i -> i o")),
                     (k.rpe_in[2:3, :], t.L0_conv_rpe_in_b.rearrange("(a o) -> a o", a=1)),
                     (k.proj_b[:], t.L1_conv_proj_b.rearrange("(a o) -> a o", a=1).to_broadcast([128, CH]))]

        @block.sync
        def _(sp):
            for at, n, src in rows:
                dst = raw[:, at:at + n, :] if n > 1 else raw[:, at, :]
                sp.dma_start(dst, src).then_inc(loaded, 16)

        @block.scalar
        def _(act):
            for at, n, src in biases:
                act.dma_start(k.bias[:, at:at + n], src, allow_slow_non_contiguous=True).then_inc(consts, 16)
            for dst, src in consts_in:
                act.dma_start(dst, src, allow_slow_non_contiguous=True).then_inc(consts, 16)
            act.wait_ge(consts, 16 * (len(biases) + len(consts_in)))
            act.wait_ge(loaded, 16 * len(rows))

        @block.vector
        def _(dve):
            dve.memset(k.ones[:], 1.0).then_inc(filled, 1)
            dve.wait_ge(filled, 1)
            for n in range(4):
                lo, hi = 4 * n, min(4 * n + 4, WEIGHT_TILES)
                dve.wait_ge(turned, n + 1)
                dve.tensor_copy(k.w[:, lo:hi, :],
                                ps[n][:, 0:128 * (hi - lo)].rearrange("p (a c) -> p a c", c=128)).then_inc(copied, 1)
            dve.wait_ge(copied, 4)

        @block.tensor
        def _(pe):
            pe.wait_ge(loaded, 16 * len(rows))
            pe.wait_ge(consts, 16 * (len(biases) + len(consts_in)))
            for n in range(4):
                lo, hi = 4 * n, min(4 * n + 4, WEIGHT_TILES)
                for m in range(lo, hi):
                    last = pe.transpose(ps[n][:, 128 * (m - lo):128 * (m - lo) + 128], raw[:, m, :], k.ident[:])
                last.then_inc(turned, 1)


class GroupStats:

    def __init__(self, ctx, nc, name):
        def sb(n, shape):
            return ctx.enter_context(nc.sbuf_tensor(f"{name}_{n}", shape, F32))

        def sem(n):
            return ctx.enter_context(nc.semaphore(f"{name}_{n}"))
        self.parts = sb("bn_parts", [128, NCH, 6])
        self.mv = sb("chan_mv", [128, 2])
        self.gm = sb("group_mv", [128, 2])
        self.dev = sb("dev", [128, 1])
        self.dev2 = sb("dev2", [128, 1])
        self.var = sb("var", [128, 1])
        self.std = sb("std", [128, 1])
        self.scale = sb("scale", [128, 1])
        self.shift = sb("shift", [128, 1])
        self.ps = ctx.enter_context(nc.psum_tensor(f"{name}_ps", [128, 512], F32))
        self.s_seen = sem("seen")
        self.s_parts, self.s_mv, self.s_gm_ps, self.s_gm = sem("parts"), sem("mv"), sem("gm_ps"), sem("gm")
        self.s_dev, self.s_dev2, self.s_dev_ps, self.s_var = sem("dev"), sem("dev2"), sem("dev_ps"), sem("var")
        self.s_var_eps, self.s_std, self.s_scale, self.s_shift = sem("var_eps"), sem("std"), sem("scale_r"), sem("shift_r")

    def on_vector(self, dve, b):
        dve.wait_ge(self.s_parts, (b + 1) * NCH)
        dve.sem_inc(self.s_seen, 1)
        dve.bn_aggr(self.mv[:], self.parts[:]).then_inc(self.s_mv, 1)
        dve.wait_ge(self.s_gm_ps, b + 1)
        dve.tensor_copy(self.gm[:], self.ps[:, 0:2]).then_inc(self.s_gm, 1)
        dve.wait_ge(self.s_gm, b + 1)
        dve.tensor_tensor(self.dev[:], self.mv[:, 0:1], self.gm[:, 0:1], ALU.subtract).then_inc(self.s_dev, 1)
        dve.wait_ge(self.s_dev, b + 1)
        dve.tensor_tensor(self.dev2[:], self.dev[:], self.dev[:], ALU.mult).then_inc(self.s_dev2, 1)
        dve.wait_ge(self.s_dev_ps, b + 1)
        dve.tensor_tensor(self.var[:], self.ps[:, 2:3], self.gm[:, 1:2], ALU.add).then_inc(self.s_var, 1)
        dve.wait_ge(self.s_var, b + 1)
        dve.tensor_scalar(self.var[:], self.var[:], 1e-5, None, ALU.add).then_inc(self.s_var_eps, 1)
        dve.wait_ge(self.s_std, b + 1)
        dve.reciprocal(self.scale[:], self.std[:]).then_inc(self.s_scale, 1)
        dve.wait_ge(self.s_scale, b + 1)
        dve.tensor_scalar(self.shift[:], self.gm[:, 0:1], self.scale[:, 0:1], -1.0, ALU.mult, ALU.mult).then_inc(self.s_shift, 1)
        dve.wait_ge(self.s_shift, b + 1)

    def on_tensor(self, pe, b, avg):
        pe.wait_ge(self.s_mv, b + 1)
        pe.matmul(self.ps[:, 0:2], avg, self.mv[:], start=True, stop=True).then_inc(self.s_gm_ps, 1)
        pe.wait_ge(self.s_dev2, b + 1)
        pe.matmul(self.ps[:, 2:3], avg, self.dev2[:], start=True, stop=True).then_inc(self.s_dev_ps, 1)

    def on_scalar(self, act, b):
        act.wait_ge(self.s_var_eps, b + 1)
        act.activation(self.std[:], self.var[:], ACT.Sqrt).then_inc(self.s_std, 1)


def project_in(nc, t, k):
    with ExitStack() as ctx:
        def sb(n, shape):
            return ctx.enter_context(nc.sbuf_tensor(n, shape, F32))

        def psum(n):
            return ctx.enter_context(nc.psum_tensor(n, [128, 512], F32))

        def sem(n):
            return ctx.enter_context(nc.semaphore(n))
        x_in = [sb(f"x_in{n}", [TT, TPC, CH]) for n in range(2)]
        xT = sb("xT", [128, TOK])
        xg = sb("xg", [128, TOK])
        xr = sb("xr", [128, TOK])
        short = sb("short", [128, TOK])
        sq = sb("sq", [128, COLS])
        rt = sb("rt", [TT, TPC])
        rt_eps = sb("rt_eps", [TT, TPC])
        rinv = sb("rinv", [TT, TPC])
        diag = sb("diag", [TT, TPC, TT])
        uv = [sb(f"uv{n}", [128, 4, COLS]) for n in range(2)]
        gs = GroupStats(ctx, nc, "gn0")
        ps_t, ps_ss, ps_bc = psum("ps_turn"), psum("ps_sumsq"), psum("ps_bcast")
        ps_uv = [psum(f"ps_uv{n}") for n in range(4)]
        x_loaded = [sem(f"x_loaded{n}") for n in range(2)]
        x_turned, x_copied, xg_ready, short_ready = sem("x_turned"), sem("x_copied"), sem("xg_ready"), sem("short_ready")
        sq_ready, ss_ready, rt_ready, eps_ready = sem("sq_ready"), sem("ss_ready"), sem("rt_ready"), sem("eps_ready")
        rinv_ready, diag_ready, bc_ready, xr_ready = sem("rinv_ready"), sem("diag_ready"), sem("bc_ready"), sem("xr_ready")
        uv_ps_ready, uv_ready = sem("uv_ps_ready"), sem("uv_ready")
        uv_stored = [sem(f"uv_stored{n}") for n in range(2)]
        short_stored = sem("short_stored")
        block = ctx.enter_context(nc.Block())
        PER = 2

        def each_chunk():
            return [(a, c, a * NCH + c) for a in range(PER) for c in range(NCH)]

        @block.gpsimd
        def _(pool):
            with pool.Fori(0, BATCH // PER) as i:
                for a, c, n in each_chunk():
                    pool.wait_ge(x_turned, i * (PER * NCH) + n + 1)
                    src = t.x_rows[bass.ds((i * PER + a) * TOK + c * COLS, COLS), :]
                    pool.dma_start(x_in[n % 2][:], src.rearrange("(a p) c -> p a c", p=TT)).then_inc(x_loaded[n % 2], 16)

        @block.tensor
        def _(pe):
            pe.sem_inc(x_turned, 2)
            with pe.Fori(0, BATCH // PER) as i:
                for a in range(PER):
                    b = i * PER + a
                    for c in range(NCH):
                        n = a * NCH + c
                        pe.wait_ge(x_loaded[n % 2], (i * NCH + n // 2 + 1) * 16)
                        pe.wait_ge(x_copied, b * NCH + c + 1)
                        for m in range(TPC):
                            last = pe.transpose(ps_t[:, m * TT:(m + 1) * TT], x_in[n % 2][:, m, :], k.ident[0:TT, 0:TT])
                        last.then_inc(x_turned, 1)
                    gs.on_tensor(pe, b, k.avg[:])
                    for c in range(NCH):
                        pe.wait_ge(sq_ready, b * NCH + c + 1)
                        for m in range(TPC):
                            last = pe.matmul(ps_ss[0:TT, m:m + 1], sq[:, m * TT:(m + 1) * TT], k.ones[:, 0:1], start=True, stop=True)
                        last.then_inc(ss_ready, 1)
                        pe.wait_ge(diag_ready, b * NCH + c + 1)
                        pe.matmul(ps_bc[:, 0:COLS], k.ones[0:TT, :], diag[:].rearrange("p a c -> p (a c)"),
                                  start=True, stop=True).then_inc(bc_ready, 1)
                    for c in range(NCH):
                        pe.wait_ge(xr_ready, b * NCH + c + 1)
                        for m in range(4):
                            pe.wait_ge(uv_ready, (b * NCH + c) * 4 + m + 1)
                            pe.matmul(ps_uv[m][:, 0:COLS], k.w[:, WU + m, :], xr[:, c * COLS:(c + 1) * COLS],
                                      start=True, stop=True).then_inc(uv_ps_ready, 1)

        @block.scalar
        def _(act):
            act.sem_inc(x_copied, 1)
            act.sem_inc(uv_ready, 4)
            with act.Fori(0, BATCH // PER) as i:
                for a in range(PER):
                    b = i * PER + a
                    for c in range(NCH):
                        act.wait_ge(x_turned, b * NCH + c + 3)
                        act.wait_ge(short_ready, (b + 1) * NCH)
                        act.activation(xT[:, c * COLS:(c + 1) * COLS], ps_t[:, 0:COLS], ACT.Copy).then_inc(x_copied, 1)
                    gs.on_scalar(act, b)
                    for c in range(NCH):
                        act.wait_ge(xg_ready, b * NCH + c + 1)
                        act.activation(sq[:], xg[:, c * COLS:(c + 1) * COLS], ACT.Square).then_inc(sq_ready, 1)
                        act.wait_ge(ss_ready, b * NCH + c + 1)
                        act.activation(rt[:], ps_ss[0:TT, 0:TPC], ACT.Sqrt, scale=1.0 / CH).then_inc(rt_ready, 1)
                    for c in range(NCH):
                        n = a * NCH + c
                        act.wait_ge(uv_stored[n % 2], (i * NCH + n // 2 + 1) * 32)
                        for m in range(4):
                            act.wait_ge(uv_ps_ready, (b * NCH + c) * 4 + m + 1)
                            act.activation(uv[n % 2][:, m, :], ps_uv[m][:, 0:COLS], ACT.Silu,
                                           bias=k.bias[:, m:m + 1]).then_inc(uv_ready, 1)

        @block.vector
        def _(dve):
            dve.sem_inc(short_ready, NCH)
            with dve.Fori(0, BATCH // PER) as i:
                for a in range(PER):
                    b = i * PER + a
                    for c in range(NCH):
                        dve.wait_ge(x_copied, b * NCH + c + 2)
                        dve.bn_stats(gs.parts[:, c, :], xT[:, c * COLS:(c + 1) * COLS]).then_inc(gs.s_parts, 1)
                    gs.on_vector(dve, b)
                    for c in range(NCH):
                        cols = slice(c * COLS, (c + 1) * COLS)
                        dve.tensor_scalar(xg[:, cols], xT[:, cols], gs.scale[:, 0:1], gs.shift[:, 0:1],
                                          ALU.mult, ALU.add).then_inc(xg_ready, 1)
                    for c in range(NCH):
                        cols = slice(c * COLS, (c + 1) * COLS)
                        dve.wait_ge(short_stored, (b + 1) * 16)
                        dve.wait_ge(xg_ready, b * NCH + c + 1)
                        dve.scalar_tensor_tensor(out=short[:, cols], in0=xT[:, cols], scalar=k.bias[:, 4:5], in1=xg[:, cols],
                                                 op0=ALU.add, op1=ALU.add).then_inc(short_ready, 1)
                        dve.wait_ge(rt_ready, b * NCH + c + 1)
                        dve.tensor_scalar(rt_eps[:], rt[:], 1e-8, None, ALU.add).then_inc(eps_ready, 1)
                        dve.wait_ge(eps_ready, b * NCH + c + 1)
                        dve.reciprocal(rinv[:], rt_eps[:]).then_inc(rinv_ready, 1)
                        dve.wait_ge(rinv_ready, b * NCH + c + 1)
                        dve.tensor_tensor(diag[:], bcast(k.ident[0:TT, 0:TT], 1, TPC), bcast(rinv[:], 2, TT),
                                          ALU.mult).then_inc(diag_ready, 1)
                        dve.wait_ge(bc_ready, b * NCH + c + 1)
                        dve.wait_ge(uv_ready, (b * NCH) * 4 + 4)
                        dve.tensor_tensor(xr[:, cols], xg[:, cols], ps_bc[:, 0:COLS], ALU.mult).then_inc(xr_ready, 1)

        @block.sync
        def _(sp):
            for n in range(2):
                sp.sem_inc(uv_stored[n], 32)
            sp.sem_inc(short_stored, 16)
            with sp.Fori(0, BATCH // PER) as i:
                for a in range(PER):
                    b = i * PER + a
                    sp.wait_ge(short_ready, (b + 2) * NCH)
                    sp.dma_start(t.S[bass.ds(b, 1)].rearrange("b p t -> (b p) t"), short[:]).then_inc(short_stored, 16)
                    for c in range(NCH):
                        n = a * NCH + c
                        sp.wait_ge(uv_ready, (b * NCH + c) * 4 + 8)
                        for m, dst in ((0, t.U), (2, t.V)):
                            sp.dma_start(dst[bass.ds(b, 1)].rearrange("b (a p) t -> p (b a) t", p=128)[:, :, c * COLS:(c + 1) * COLS],
                                           uv[n % 2][:, m:m + 2, :]).then_inc(uv_stored[n % 2], 16)
            sp.wait_ge(short_stored, 16 * (BATCH + 1))
            for n in range(2):
                sp.wait_ge(uv_stored[n], 32 * (BATCH * NCH // 2 + 1))


def make_taps(nc, t, k):
    with ExitStack() as ctx:
        def sb(n, shape):
            return ctx.enter_context(nc.sbuf_tensor(n, shape, F32))

        def psum(n):
            return ctx.enter_context(nc.psum_tensor(n, [128, 512], F32))

        def sem(n):
            return ctx.enter_context(nc.semaphore(n))
        acts = sb("acts", [128, NRC * RC])
        coords = [sb(f"coords{n}", [3, RC]) for n in range(2)]
        pos = [sb(f"pos_relu{n}", [128, RC]) for n in range(2)]
        sq = [sb(f"pos_sq{n}", [128, RC]) for n in range(2)]
        rt = [sb(f"pos_rt{n}", [TAPS, 4]) for n in range(2)]
        rt_eps = [sb(f"pos_eps{n}", [TAPS, 4]) for n in range(2)]
        rinv = [sb(f"pos_rinv{n}", [TAPS, 4]) for n in range(2)]
        diag = [sb(f"pos_diag{n}", [TAPS, 4, TAPS]) for n in range(2)]
        taps = [sb(f"taps_sb{n}", [128, 2, RC]) for n in range(2)]
        ps_t = [psum(f"ps_pos{n}") for n in range(2)]
        ps_ss = [psum(f"ps_pos_ss{n}") for n in range(2)]
        ps_bc = [psum(f"ps_pos_bc{n}") for n in range(2)]
        ps_g = [psum(f"ps_taps{n}") for n in range(2)]
        c_loaded = [sem(f"coords_loaded{n}") for n in range(2)]
        lin, relu, sqr, ss, rt_s = sem("pos_lin"), sem("pos_relu_r"), sem("pos_sq_r"), sem("pos_ss"), sem("pos_rt_r")
        eps, inv, dg, bc, act_r = sem("pos_eps_r"), sem("pos_inv"), sem("pos_diag_r"), sem("pos_bc"), sem("acts_ready")
        g_ps, g_sb = sem("taps_ps"), sem("taps_copied")
        g_stored = [sem(f"taps_stored{n}") for n in range(2)]
        block = ctx.enter_context(nc.Block())
        PAIRS = NRC // 2
        ROUNDS = 4

        @block.gpsimd
        def _(pool):
            with pool.Fori(0, PAIRS) as i:
                for n in range(2):
                    pool.wait_ge(lin, i * 2 + n + 1)
                    pool.dma_start(coords[n][:], t.c_coords[:, bass.ds((i * 2 + n) * RC, RC)]).then_inc(c_loaded[n], 16)

        @block.tensor
        def _(pe):
            pe.sem_inc(lin, 2)
            for r in range(ROUNDS):
                with pe.Fori(0, PAIRS) as i:
                    for n in range(2):
                        at = i * 2 + n + r * NRC
                        pe.wait_ge(sqr, at + 1)
                        if r == 0:
                            pe.wait_ge(c_loaded[n], i * 16 + 16)
                            pe.matmul(ps_t[n][:, 0:RC], k.rpe_in[:], coords[n][:], start=True, stop=True).then_inc(lin, 1)
                        else:
                            pe.wait_ge(act_r, at - NRC + 3)
                            pe.matmul(ps_t[n][:, 0:RC], k.w[:, RH + r - 1, :], acts[:, bass.ds((i * 2 + n) * RC, RC)],
                                      start=True, stop=True).then_inc(lin, 1)
                    for n in range(2):
                        at = i * 2 + n + r * NRC
                        pe.wait_ge(sqr, at + 3)
                        for m in range(4):
                            last = pe.matmul(ps_ss[n][0:TAPS, m:m + 1], sq[n][:, m * TAPS:(m + 1) * TAPS], k.ones[:, 0:1],
                                             start=True, stop=True)
                        last.then_inc(ss, 1)
                    for n in range(2):
                        at = i * 2 + n + r * NRC
                        pe.wait_ge(dg, at + 1)
                        pe.matmul(ps_bc[n][:, 0:RC], k.ones[0:TAPS, :], diag[n][:].rearrange("p a c -> p (a c)"),
                                  start=True, stop=True).then_inc(bc, 1)
            with pe.Fori(0, PAIRS) as i:
                for n in range(2):
                    pe.wait_ge(act_r, i * 2 + n + (ROUNDS - 1) * NRC + 3)
                    for h in range(2):
                        pe.wait_ge(g_sb, (i * 2 + n) * 2 + h + 1)
                        pe.matmul(ps_g[h][:, 0:RC], k.w[:, RO + h, :], acts[:, bass.ds((i * 2 + n) * RC, RC)],
                                  start=True, stop=True).then_inc(g_ps, 1)

        @block.scalar
        def _(act):
            act.sem_inc(sqr, 2)
            act.sem_inc(g_sb, 2)
            for r in range(ROUNDS):
                bias = 0.0 if r == 0 else k.bias[:, 4 + r:5 + r]
                with act.Fori(0, PAIRS) as i:
                    for n in range(2):
                        at = i * 2 + n + r * NRC
                        act.wait_ge(lin, at + 3)
                        act.wait_ge(act_r, at + 1)
                        act.activation(pos[n][:], ps_t[n][:, 0:RC], ACT.Relu, bias=bias).then_inc(relu, 1)
                        act.activation(sq[n][:], ps_t[n][:, 0:RC], ACT.Square, bias=bias).then_inc(sqr, 1)
                    for n in range(2):
                        at = i * 2 + n + r * NRC
                        act.wait_ge(ss, at + 1)
                        act.activation(rt[n][:], ps_ss[n][0:TAPS, 0:4], ACT.Sqrt, scale=1.0 / CH).then_inc(rt_s, 1)
            with act.Fori(0, PAIRS) as i:
                for n in range(2):
                    act.wait_ge(g_stored[n], i * 16 + 16)
                    for h in range(2):
                        act.wait_ge(g_ps, (i * 2 + n) * 2 + h + 1)
                        act.activation(taps[n][:, h, :], ps_g[h][:, 0:RC], ACT.Identity,
                                       bias=k.bias[:, 8 + h:9 + h]).then_inc(g_sb, 1)

        @block.vector
        def _(dve):
            dve.sem_inc(act_r, 2)
            for r in range(ROUNDS):
                with dve.Fori(0, PAIRS) as i:
                    for n in range(2):
                        at = i * 2 + n + r * NRC
                        dve.wait_ge(rt_s, at + 1)
                        dve.tensor_scalar(rt_eps[n][:], rt[n][:], 1e-8, None, ALU.add).then_inc(eps, 1)
                        dve.wait_ge(eps, at + 1)
                        dve.reciprocal(rinv[n][:], rt_eps[n][:]).then_inc(inv, 1)
                        dve.wait_ge(inv, at + 1)
                        dve.tensor_tensor(diag[n][:], bcast(k.ident[0:TAPS, 0:TAPS], 1, 4), bcast(rinv[n][:], 2, TAPS),
                                          ALU.mult).then_inc(dg, 1)
                    for n in range(2):
                        at = i * 2 + n + r * NRC
                        dve.wait_ge(bc, at + 1)
                        dve.wait_ge(relu, at + 1)
                        dve.tensor_tensor(acts[:, bass.ds((i * 2 + n) * RC, RC)], pos[n][:], ps_bc[n][:, 0:RC],
                                          ALU.mult).then_inc(act_r, 1)

        @block.sync
        def _(sp):
            flat = t.G.rearrange("(a p) r q -> p a (r q)", p=128)
            for n in range(2):
                sp.sem_inc(g_stored[n], 16)
            with sp.Fori(0, PAIRS) as i:
                for n in range(2):
                    sp.wait_ge(g_sb, (i * 2 + n) * 2 + 4)
                    sp.dma_start(flat[:, :, bass.ds((i * 2 + n) * RC, RC)], taps[n][:]).then_inc(g_stored[n], 16)
            for n in range(2):
                sp.wait_ge(g_stored[n], 16 * (PAIRS + 1))


def convolve(nc, t, k):
    PC = CC * NF
    with ExitStack() as ctx:
        def sb(n, shape):
            return ctx.enter_context(nc.sbuf_tensor(n, shape, F32))

        def psum(n):
            return ctx.enter_context(nc.psum_tensor(n, [128, 512], F32))

        def sem(n):
            return ctx.enter_context(nc.semaphore(n))
        g_in = sb("g_in", [TAPS, CC, TAPS])
        g_half = sb("g_half", [TAPS, 2, CC, NF])
        spec = sb("spec", [NFFT, 3, PC])
        v_in = [sb(f"v_in{n}", [120, CC, 120]) for n in range(2)]
        x_half = sb("x_half", [120, PC])
        prod = sb("prod", [NFFT, 3, PC])
        q_half = sb("q_half", [2 * NF, CC // 2, 2, SIDE])
        y_sb = [sb(f"y_sb{n}", [2 * SIDE, CC // 2, SIDE]) for n in range(2)]
        ps_g = [psum(f"ps_g{n}") for n in range(2)]
        ps_x, ps_q, ps_y = psum("ps_x"), psum("ps_q"), psum("ps_y")
        ps_z = [psum(f"ps_z{n}") for n in range(3)]
        cleared = sem("v_cleared")
        g_loaded, g_ps, g_half_r, a_ps, a_ready = sem("g_loaded"), sem("g_half_ps"), sem("g_half_r"), sem("spec_ps"), sem("spec_ready")
        v_loaded = [sem(f"v_loaded{n}") for n in range(2)]
        x_ps, x_half_r, z_ps, prod_r, q_ps, q_r = sem("x_ps"), sem("x_half_r"), sem("z_ps"), sem("prod_r"), sem("q_ps"), sem("q_r")
        y_ps, y_r = sem("y_ps"), sem("y_r")
        y_stored = [sem(f"y_stored{n}") for n in range(2)]
        block = ctx.enter_context(nc.Block())

        @block.gpsimd
        def _(pool):
            pool.wait_ge(cleared, 2)
            with pool.Fori(0, NCC) as i:
                pool.wait_ge(g_ps, i * 2 + 1)
                pool.dma_start(g_in[:], t.G[bass.ds(i * CC, CC), :, 0:TAPS].rearrange("c p q -> p c q")).then_inc(g_loaded, 16)
                for b in range(BATCH):
                    pool.wait_ge(x_ps, i * BATCH + b + 1)
                    src = t.V[b, bass.ds(i * CC, CC), :].rearrange("c (h w) -> h c w", w=SIDE)
                    for at in (0, 64):
                        pool.dma_start(v_in[b % 2][at:at + SIDE, :, at:at + SIDE], src).then_inc(v_loaded[b % 2], 16)

        @block.tensor
        def _(pe):
            pe.sem_inc(x_ps, 2)
            pe.sem_inc(g_ps, 1)
            with pe.Fori(0, NCC) as i:
                def image_h(b):
                    pe.wait_ge(v_loaded[b % 2], (i * (BATCH // 2) + b // 2 + 1) * 32)
                    for c in range(CC):
                        last = pe.matmul(ps_x[0:120, c * NF:(c + 1) * NF], v_in[b % 2][:, c, :], k.fwd_h[:], start=True, stop=True)
                    last.then_inc(x_ps, 1)

                def image_w(b):
                    pe.wait_ge(x_half_r, i * BATCH + b + 1)
                    for n in range(3):
                        last = pe.matmul(ps_z[n][0:NFFT, 0:PC], k.fwd_w[:, n, :], x_half[:], start=True, stop=True)
                    last.then_inc(z_ps, 1)

                def back_w(b):
                    pe.wait_ge(prod_r, i * BATCH + b + 1)
                    for c in range(CC // 2):
                        for n in range(3):
                            pair = prod[:, n, c * 2 * NF:(c + 1) * 2 * NF]
                            last = pe.matmul(ps_q[0:2 * NF, c * NFFT:(c + 1) * NFFT], pair, k.inv_w[:, n, :],
                                             start=(n == 0), stop=(n == 2))
                    last.then_inc(q_ps, 1)

                def back_h(b):
                    pe.wait_ge(q_r, i * BATCH + b + 1)
                    pe.wait_ge(y_r, i * BATCH + b + 1)
                    for n in range(2):
                        last = pe.matmul(ps_y[0:2 * SIDE, 0:CC // 2 * SIDE], k.inv_h[:, n, :], q_half[:, :, n, :],
                                         start=(n == 0), stop=(n == 1))
                    last.then_inc(y_ps, 1)

                pe.wait_ge(g_loaded, i * 16 + 16)
                for n in range(2):
                    for c in range(4):
                        last = pe.matmul(ps_g[n][0:TAPS, c * 2 * NF:(c + 1) * 2 * NF], g_in[:, 4 * n + c, :], k.tap_p[:],
                                         start=True, stop=True)
                    last.then_inc(g_ps, 1)
                image_h(0)
                pe.wait_ge(g_half_r, i * 2 + 2)
                for n in range(3):
                    for ri in range(2):
                        last = pe.matmul(ps_z[n][0:NFFT, 0:PC], k.tap_q[:, 2 * n + ri, :],
                                         g_half[:, ri].rearrange("p c f -> p (c f)"), start=(ri == 0), stop=(ri == 1))
                last.then_inc(a_ps, 1)
                pe.wait_ge(a_ready, i * 3 + 3)
                image_w(0)
                for b in range(BATCH):
                    if b + 1 < BATCH:
                        image_h(b + 1)
                    back_w(b)
                    if b + 1 < BATCH:
                        image_w(b + 1)
                    back_h(b)

        @block.scalar
        def _(act):
            with act.Fori(0, NCC) as i:
                def copy_x(b):
                    act.wait_ge(x_ps, i * BATCH + b + 3)
                    act.activation(x_half[:], ps_x[0:120, 0:PC], ACT.Copy).then_inc(x_half_r, 1)

                for n in range(2):
                    act.wait_ge(g_ps, i * 2 + n + 2)
                    act.activation(g_half[:, :, 4 * n:4 * n + 4, :].rearrange("p r c f -> p c r f"),
                                   ps_g[n][0:TAPS, 0:PC].rearrange("p (c r f) -> p c r f", r=2, f=NF), ACT.Copy).then_inc(g_half_r, 1)
                copy_x(0)
                act.wait_ge(a_ps, i + 1)
                for n in range(3):
                    act.activation(spec[:, n, :], ps_z[n][0:NFFT, 0:PC], ACT.Copy).then_inc(a_ready, 1)
                for b in range(BATCH):
                    if b + 1 < BATCH:
                        copy_x(b + 1)
                    act.wait_ge(q_ps, i * BATCH + b + 1)
                    act.activation(q_half[:].rearrange("p c r w -> p (c r w)"), ps_q[0:2 * NF, 0:CC // 2 * NFFT], ACT.Copy).then_inc(q_r, 1)

        @block.vector
        def _(dve):
            for n in range(2):
                dve.memset(v_in[n][:], 0.0).then_inc(cleared, 1)
            dve.sem_inc(y_r, 1)
            with dve.Fori(0, NCC) as i:
                def copy_y(b):
                    dve.wait_ge(y_ps, i * BATCH + b + 1)
                    dve.wait_ge(y_stored[b % 2], (i * (BATCH // 2) + b // 2 + 1) * 32)
                    dve.tensor_copy(y_sb[b % 2][:].rearrange("p c w -> p (c w)"), ps_y[0:2 * SIDE, 0:CC // 2 * SIDE]).then_inc(y_r, 1)

                dve.wait_ge(a_ready, i * 3 + 3)
                for b in range(BATCH):
                    dve.wait_ge(z_ps, i * BATCH + b + 1)
                    for n, z in ((0, 2), (1, 0), (2, 1)):
                        last = dve.tensor_tensor(prod[:, n, :], spec[:, n, :], ps_z[z][0:NFFT, 0:PC], ALU.mult)
                    last.then_inc(prod_r, 1)
                    if b:
                        copy_y(b - 1)
                copy_y(BATCH - 1)

        @block.sync
        def _(sp):
            for n in range(2):
                sp.sem_inc(y_stored[n], 32)
            with sp.Fori(0, NCC) as i:
                for b in range(BATCH):
                    sp.wait_ge(y_r, i * BATCH + b + 2)
                    for a in range(2):
                        dst = t.Y[b, bass.ds(i * CC, CC), :].rearrange("(c a) (h w) -> a h c w", a=2, w=SIDE)
                        sp.dma_start(dst[a], y_sb[b % 2][a * SIDE:(a + 1) * SIDE]).then_inc(y_stored[b % 2], 16)
            for n in range(2):
                sp.wait_ge(y_stored[n], 32 * (NCC * BATCH // 2 + 1))


def project_out(nc, t, k):
    with ExitStack() as ctx:
        def sb(n, shape):
            return ctx.enter_context(nc.sbuf_tensor(n, shape, F32))

        def psum(n):
            return ctx.enter_context(nc.psum_tensor(n, [128, 512], F32))

        def sem(n):
            return ctx.enter_context(nc.semaphore(n))
        u = [sb(f"u{n}", [128, 2, COLS]) for n in range(2)]
        y = [sb(f"y{n}", [128, 2, COLS]) for n in range(2)]
        s = [sb(f"s{n}", [128, COLS]) for n in range(2)]
        z = [sb(f"z{n}", [128, 2, COLS]) for n in range(2)]
        x1 = sb("x1", [128, TOK])
        xn = sb("xn1", [128, NL, RPI])
        gs = GroupStats(ctx, nc, "gn1")
        ps = [psum(f"ps_wo{n}") for n in range(2)]
        loaded = [sem(f"uys_loaded{n}") for n in range(2)]
        z_ready, o_ps, x1_ready, xn_ready = sem("z_ready"), sem("wo_ps"), sem("x1_ready"), sem("xn_ready")
        x1_stored, xn_stored = sem("x1_stored"), sem("xn_stored")
        block = ctx.enter_context(nc.Block())
        PER = 2

        @block.gpsimd
        def _(pool):
            with pool.Fori(0, BATCH // PER) as i:
                for n in range(PER * NCH):
                    b, c = i * PER + n // NCH, n % NCH
                    cols = slice(c * COLS, (c + 1) * COLS)
                    pool.wait_ge(x1_ready, i * (PER * NCH) + n + 1)
                    for dst, src in ((u, t.U), (y, t.Y)):
                        pool.dma_start(dst[n % 2][:], src[bass.ds(b, 1)].rearrange("b (a p) t -> p (b a) t", p=128)[:, :, cols])\
                          .then_inc(loaded[n % 2], 16)
                    pool.dma_start(s[n % 2][:], t.S[bass.ds(b, 1)].rearrange("b p t -> (b p) t")[:, cols]).then_inc(loaded[n % 2], 16)

        @block.vector
        def _(dve):
            dve.sem_inc(x1_ready, 2)
            with dve.Fori(0, BATCH // PER) as i:
                for a in range(PER):
                    b = i * PER + a
                    dve.wait_ge(x1_stored, (b + 1) * 16)
                    dve.wait_ge(xn_ready, (b + 1) * 4)
                    def gate(c):
                        n = a * NCH + c
                        dve.wait_ge(loaded[n % 2], (i * NCH + n // 2 + 1) * 48)
                        dve.tensor_tensor(z[n % 2][:], u[n % 2][:], y[n % 2][:], ALU.mult).then_inc(z_ready, 1)
                    gate(0)
                    for c in range(NCH):
                        n = a * NCH + c
                        if c + 1 < NCH:
                            gate(c + 1)
                        dve.wait_ge(o_ps, b * NCH + c + 1)
                        dve.tensor_tensor(x1[:, c * COLS:(c + 1) * COLS], s[n % 2][:], ps[n % 2][:, 0:COLS], ALU.add).then_inc(x1_ready, 1)
                        dve.wait_ge(x1_ready, b * NCH + c + 3)
                        dve.bn_stats(gs.parts[:, c, :], x1[:, c * COLS:(c + 1) * COLS]).then_inc(gs.s_parts, 1)
                    gs.on_vector(dve, b)

        @block.tensor
        def _(pe):
            with pe.Fori(0, BATCH // PER) as i:
                for a in range(PER):
                    b = i * PER + a
                    for c in range(NCH):
                        n = a * NCH + c
                        pe.wait_ge(z_ready, b * NCH + c + 1)
                        pe.wait_ge(x1_ready, b * NCH + c + 1)
                        for m in range(2):
                            last = pe.matmul(ps[n % 2][:, 0:COLS], k.w[:, WO + m, :], z[n % 2][:, m, :], start=(m == 0), stop=(m == 1))
                        last.then_inc(o_ps, 1)
                    gs.on_tensor(pe, b, k.avg[:])

        @block.scalar
        def _(act):
            act.sem_inc(xn_ready, 4)
            with act.Fori(0, BATCH // PER) as i:
                for a in range(PER):
                    b = i * PER + a
                    gs.on_scalar(act, b)
                    act.wait_ge(gs.s_shift, b + 1)
                    act.wait_ge(xn_stored, (b + 1) * 16)
                    rows = x1[:].rearrange("p (r n) -> p n r", n=NL)
                    for m in range(4):
                        act.activation(xn[:, 4 * m:4 * m + 4, :], rows[:, 4 * m:4 * m + 4, :], ACT.Identity,
                                       bias=gs.shift[:, 0:1], scale=gs.scale[:, 0:1]).then_inc(xn_ready, 1)

        @block.sync
        def _(sp):
            sp.sem_inc(x1_stored, 16)
            sp.sem_inc(xn_stored, 16)
            with sp.Fori(0, BATCH) as b:
                sp.wait_ge(x1_ready, b * NCH + NCH + 2)
                sp.dma_start(t.X1[bass.ds(b, 1)].rearrange("b p t -> (b p) t"), x1[:]).then_inc(x1_stored, 16)
                sp.wait_ge(xn_ready, b * 4 + 8)
                sp.dma_start(t.XN[:, :, bass.ds(b * RPI, RPI)].rearrange("n p r -> p n r"), xn[:]).then_inc(xn_stored, 16)
            sp.wait_ge(x1_stored, 16 * (BATCH + 1))
            sp.wait_ge(xn_stored, 16 * (BATCH + 1))


def attend(nc, t, k):
    STEPS = NG * NL // 2
    AHEAD = 4
    D, HH = CH, HEADS * HEADS
    with ExitStack() as ctx:
        def sb(n, shape):
            return ctx.enter_context(nc.sbuf_tensor(n, shape, F32))

        def psum(n):
            return ctx.enter_context(nc.psum_tensor(n, [128, 512], F32))

        def sem(n):
            return ctx.enter_context(nc.semaphore(n))

        def bufs(count, n, shape):
            return [sb(f"{n}{m}", [RG, 2] + shape) for m in range(count)]
        xn = [sb(f"xn_in{m}", [128, 2, RG]) for m in range(4)]
        v2, qk, norm_i = bufs(4, "v2_", [D]), bufs(4, "qk_", [2 * D]), bufs(4, "norm_i", [24])
        sq, norm_sq, norm, norm_c = bufs(2, "sq", [3 * D]), bufs(2, "norm_sq", [24]), bufs(2, "norm", [24]), bufs(2, "norm_c", [24])
        vh = bufs(2, "vh", [D])
        small = bufs(1, "small_prod", [HH * HD])[0]
        S, S_sh, A_exp = bufs(2, "S", [HH]), bufs(2, "S_sh", [HH]), bufs(2, "A_exp", [HH])
        S_max, A_sum, A_inv = bufs(2, "S_max", [8]), bufs(2, "A_sum", [8]), bufs(2, "A_inv", [8])
        A, B, Bq, Bqk = bufs(2, "A", [HH]), bufs(2, "B", [HH]), bufs(2, "Bq", [HH]), bufs(2, "Bqk", [HH])
        m_prod = sb("m_prod", [RG, HEADS, 2, HEADS * HD])
        l_prod = sb("l_prod", [RG, HEADS, 2, HD * HD])
        o_prod = sb("o_prod", [RG, HD, 2, HD * HEADS])
        L_max, L_sh, P_exp = bufs(2, "L_max", [HD]), bufs(2, "L_sh", [HD * HD]), bufs(2, "P_exp", [HD * HD])
        P_sum, P_inv, v_sc = bufs(2, "P_sum", [HD]), bufs(2, "P_inv", [HD]), bufs(2, "v_sc", [D])
        o_sb = [sb(f"o_sb{m}", [RG, HD, 2, HEADS]) for m in range(2)]
        ps_qkv = [psum(f"ps_qkv{j}") for j in range(2)]
        ps_m = [psum(f"ps_m{m}") for m in range(2)]
        ps_l = [psum(f"ps_l{m}") for m in range(2)]
        ps_o = [psum(f"ps_o{m}") for m in range(2)]
        xn_loaded = [sem(f"xn_loaded{m}") for m in range(4)]
        names = ("qkv_ps qkv_read nsq norm nc ni vh sprod s smax ssh aexp asum ainv a bprod b bq bqk "
                 "mprod m_ps lprod l_ps lmax lsh pexp psum pinv vsc oprod o_ps o").split()
        s = {n: sem("at_" + n) for n in names}
        o_stored = [sem(f"o_stored{m}") for m in range(2)]
        block = ctx.enter_context(nc.Block())

        def steps(eng, body):
            for m in range(AHEAD):
                body(m, m)
            with eng.Fori(1, STEPS // AHEAD - 1) as i:
                for m in range(AHEAD):
                    body(i * AHEAD + m, m)
            for m in range(AHEAD):
                body(STEPS - AHEAD + m, m)

        @block.sync
        def _(sp):
            with sp.Fori(0, STEPS // AHEAD) as i:
                for m in range(AHEAD):
                    n = i * AHEAD + m
                    sp.wait_ge(s["qkv_ps"], n * 2 + 2)
                    src = t.XN[bass.ds(n % (NL // 2) * 2, 2), :, bass.ds(n // (NL // 2) * RG, RG)]
                    sp.dma_start(xn[m][:], src.rearrange("n p r -> p n r")).then_inc(xn_loaded[m], 16)

        @block.tensor
        def _(pe):
            pe.sem_inc(s["qkv_ps"], 8)
            pe.sem_inc(s["o_ps"], 1)

            def qkv(n, m):
                pe.wait_ge(xn_loaded[m], (n // AHEAD + 1) * 16 if isinstance(n, int) else (n - m) * 4 + 16)
                for j in range(2):
                    pe.wait_ge(s["qkv_read"], n * 2 + j + 1)
                    pe.matmul(ps_qkv[j][0:RG, 0:3 * D], xn[m][:, j, :], k.w[:, WQ:WQ + 3, :].rearrange("p a c -> p (a c)"),
                              start=True, stop=True).then_inc(s["qkv_ps"], 1)

            def mixed(n, m):
                pe.wait_ge(s["mprod"], n + 1)
                for x in range(HEADS):
                    last = pe.matmul(ps_m[m % 2][0:RG, 0:2 * D], k.ident[0:RG, 0:RG], m_prod[:, x].rearrange("p j c -> p (j c)"),
                                     start=(x == 0), stop=(x == HEADS - 1))
                last.then_inc(s["m_ps"], 1)

            def outputs(n, m):
                pe.wait_ge(s["o"], n + 1)
                pe.wait_ge(s["oprod"], n + 3)
                for x in range(HD):
                    last = pe.matmul(ps_o[m % 2][0:RG, 0:2 * D], k.ident[0:RG, 0:RG], o_prod[:, x].rearrange("p j c -> p (j c)"),
                                     start=(x == 0), stop=(x == HD - 1))
                last.then_inc(s["o_ps"], 1)

            def body(n, m):
                late = isinstance(n, int)
                for j in range(2):
                    pe.wait_ge(s["lprod"], n * 2 + j + 1)
                    for x in range(HEADS):
                        last = pe.matmul(ps_l[m % 2][0:RG, j * HD * HD:(j + 1) * HD * HD], k.ident[0:RG, 0:RG], l_prod[:, x, j], start=(x == 0), stop=(x == HEADS - 1))
                last.then_inc(s["l_ps"], 1)
                if not late or n > 0:
                    outputs(n - 1, m - 1)
                if not late or n + 1 < STEPS:
                    mixed(n + 1, m + 1)
                if not late or n + 3 < STEPS:
                    qkv(n + 3, (m + 3) % AHEAD)
            for n in range(3):
                qkv(n, n)
            mixed(0, 0)
            steps(pe, body)
            outputs(STEPS - 1, STEPS - 1)

        @block.scalar
        def _(act):
            act.sem_inc(s["qkv_read"], 2)
            act.sem_inc(s["o"], 2)
            for m in range(2):
                act.sem_inc(o_stored[m], 16)

            def empty(n, m):
                act.wait_ge(s["vsc"], n + 1)
                for j in range(2):
                    act.wait_ge(s["qkv_ps"], n * 2 + j + 9)
                    act.activation(sq[m % 2][:, j, 0:2 * D], ps_qkv[j][0:RG, 0:2 * D], ACT.Square)
                    act.activation(sq[m % 2][:, j, 2 * D:], ps_qkv[j][0:RG, 2 * D:3 * D], ACT.Square, scale=2.0)
                    act.activation(qk[m][:, j], ps_qkv[j][0:RG, 0:2 * D], ACT.Copy)
                    act.activation(v2[m][:, j], ps_qkv[j][0:RG, 2 * D:3 * D], ACT.Copy, scale=2.0).then_inc(s["qkv_read"], 1)

            def norms(n, m):
                act.wait_ge(s["nsq"], n + 1)
                act.activation(norm[m % 2][:], norm_sq[m % 2][:], ACT.Sqrt).then_inc(s["norm"], 1)

            def exp1(n, m):
                act.wait_ge(s["ssh"], n + 1)
                act.activation(A_exp[m % 2][:], S_sh[m % 2][:], ACT.Exp).then_inc(s["aexp"], 1)

            def exp2(n, m):
                act.wait_ge(s["lsh"], n + 1)
                act.wait_ge(s["oprod"], n + 1)
                act.activation(P_exp[m % 2][:], L_sh[m % 2][:], ACT.Exp).then_inc(s["pexp"], 1)

            def leave(n, m):
                act.wait_ge(s["o_ps"], n + 2)
                act.wait_ge(o_stored[m % 2], (n // 2 + 1) * 16 if isinstance(n, int) else (n - m % 2) * 8 + 16)
                act.activation(o_sb[m % 2][:].rearrange("p e j h -> p j e h"),
                               ps_o[m % 2][0:RG, 0:256].rearrange("p (j e h) -> p j e h", j=2, h=HEADS), ACT.Copy).then_inc(s["o"], 1)
                act.wait_ge(s["o"], n + 3)
                dst = t.O[bass.ds(n // (NL // 2) * RG, RG), bass.ds(n % (NL // 2), 1)].rearrange("r n c -> r (n c)")
                act.dma_start(dst, o_sb[m % 2][:].rearrange("p e j h -> p (e j h)")).then_inc(o_stored[m % 2], 16)

            def body(n, m):
                late = isinstance(n, int)
                if not late or n + 1 < STEPS:
                    exp1(n + 1, (m + 1) % 4)
                exp2(n, m)
                if not late or n + 2 < STEPS:
                    empty(n + 2, (m + 2) % 4)
                    norms(n + 2, (m + 2) % 4)
                if not late or n > 0:
                    leave(n - 1, m - 1)
            for n in range(2):
                empty(n, n)
                norms(n, n)
            exp1(0, 0)
            steps(act, body)
            leave(STEPS - 1, STEPS - 1)
            for m in range(2):
                act.wait_ge(o_stored[m], 16 * (STEPS // 2 + 1))

        @block.vector
        def _(dve):
            dve.sem_inc(s["vsc"], 4)

            def heads(ap, g=HEADS):
                return ap.rearrange("p j (h g) -> p j h g", g=g)

            def norms(n, m):
                a, b = m % 2, m % 4
                dve.wait_ge(s["qkv_read"], n * 2 + 4)
                dve.tensor_reduce(norm_sq[a][:], heads(sq[a][:], HD), AX, ALU.add).then_inc(s["nsq"], 1)
                dve.wait_ge(s["norm"], n + 1)
                dve.tensor_scalar(norm_c[a][:], norm[a][:], 1e-12, None, ALU.max).then_inc(s["nc"], 1)
                dve.wait_ge(s["nc"], n + 1)
                dve.reciprocal(norm_i[b][:], norm_c[a][:]).then_inc(s["ni"], 1)
                dve.wait_ge(s["ni"], n + 1)
                dve.tensor_tensor(heads(vh[a][:], HD), heads(v2[b][:], HD), bcast(norm_i[b][:, :, 16:24], 3, HD), ALU.mult).then_inc(s["vh"], 1)

            def scores(n, m):
                a = m % 2
                dve.wait_ge(s["vh"], n + 1)
                for j in range(2):
                    v = vh[a][:, j].rearrange("p (h d) -> p h d", d=HD)
                    last = dve.tensor_tensor(small[:, j].rearrange("p (h g d) -> p h g d", h=HEADS, d=HD), bcast(v, 2, HEADS), bcast(v, 1, HEADS),
                                             ALU.mult)
                last.then_inc(s["sprod"], 1)
                dve.wait_ge(s["sprod"], n + 1)
                dve.tensor_reduce(S[a][:], heads(small[:], HD), AX, ALU.add).then_inc(s["s"], 1)
                dve.wait_ge(s["s"], n + 1)
                dve.tensor_reduce(S_max[a][:], heads(S[a][:]), AX, ALU.max).then_inc(s["smax"], 1)
                dve.wait_ge(s["smax"], n + 1)
                dve.tensor_tensor(heads(S_sh[a][:]), heads(S[a][:]), bcast(S_max[a][:], 3, HEADS), ALU.subtract).then_inc(s["ssh"], 1)

            def mix(n, m):
                a, b = m % 2, m % 4
                dve.wait_ge(s["aexp"], n + 1)
                dve.tensor_reduce(A_sum[a][:], heads(A_exp[a][:]), AX, ALU.add).then_inc(s["asum"], 1)
                dve.wait_ge(s["asum"], n + 1)
                dve.reciprocal(A_inv[a][:], A_sum[a][:]).then_inc(s["ainv"], 1)
                dve.wait_ge(s["ainv"], n + 1)
                dve.tensor_tensor(heads(A[a][:]), heads(A_exp[a][:]), bcast(A_inv[a][:], 3, HEADS), ALU.mult).then_inc(s["a"], 1)
                dve.wait_ge(s["a"], n + 1)
                for j in range(2):
                    x = A[a][:, j].rearrange("p (h g) -> p g h", g=HEADS)
                    last = dve.tensor_tensor(small[:, j, 0:512].rearrange("p (f g h) -> p f g h", f=HEADS, h=HEADS), bcast(x, 2, HEADS), bcast(x, 1, HEADS),
                                             ALU.mult)
                last.then_inc(s["bprod"], 1)
                dve.wait_ge(s["bprod"], n + 1)
                dve.tensor_reduce(B[a][:], heads(small[:, :, 0:512]), AX, ALU.add).then_inc(s["b"], 1)
                dve.wait_ge(s["b"], n + 1)
                dve.tensor_tensor(heads(Bq[a][:]), heads(B[a][:]), bcast(norm_i[b][:, :, 0:8], 3, HEADS), ALU.mult).then_inc(s["bq"], 1)
                dve.wait_ge(s["bq"], n + 1)
                dve.tensor_tensor(heads(Bqk[a][:]), heads(Bq[a][:]), bcast(norm_i[b][:, :, 8:16], 2, HEADS), ALU.mult).then_inc(s["bqk"], 1)
                dve.wait_ge(s["bqk"], n + 1)
                for j in range(2):
                    q = qk[b][:, j, 0:D].rearrange("p (h d) -> p h d", d=HD)
                    last = dve.tensor_tensor(m_prod[:, :, j].rearrange("p f (g e) -> p f g e", e=HD),
                                             bcast(Bqk[a][:, j].rearrange("p (f g) -> p f g", f=HEADS), 3, HD), bcast(q, 2, HEADS), ALU.mult)
                last.then_inc(s["mprod"], 1)

            def logits(n, m):
                dve.wait_ge(s["m_ps"], n + 1)
                for j in range(2):
                    kk = qk[m % 4][:, j, D:].rearrange("p (h d) -> p h d", d=HD)
                    mm = ps_m[m % 2][0:RG, j * 128:(j + 1) * 128].rearrange("p (g e) -> p g e", e=HD)
                    dve.tensor_tensor(l_prod[:, :, j].rearrange("p g (d e) -> p g d e", e=HD), bcast(kk, 3, HD), bcast(mm, 2, HD),
                                      ALU.mult).then_inc(s["lprod"], 1)

            def shift(n, m):
                a = m % 2
                ll = heads(ps_l[a][0:RG, :].rearrange("p (j c) -> p j c", j=2), HD)
                dve.wait_ge(s["l_ps"], n + 1)
                dve.tensor_reduce(L_max[a][:], ll, AX, ALU.max).then_inc(s["lmax"], 1)
                dve.wait_ge(s["lmax"], n + 1)
                dve.tensor_tensor(heads(L_sh[a][:], HD), ll, bcast(L_max[a][:], 3, HD), ALU.subtract).then_inc(s["lsh"], 1)

            def divide(n, m):
                a, b = m % 2, m % 4
                dve.wait_ge(s["pexp"], n + 1)
                dve.tensor_reduce(P_sum[a][:], heads(P_exp[a][:], HD), AX, ALU.add).then_inc(s["psum"], 1)
                dve.wait_ge(s["psum"], n + 1)
                dve.reciprocal(P_inv[a][:], P_sum[a][:]).then_inc(s["pinv"], 1)
                dve.wait_ge(s["pinv"], n + 1)
                dve.wait_ge(s["oprod"], n + 1)
                dve.tensor_tensor(v_sc[a][:].rearrange("p j (d h) -> p j d h", h=HEADS), v2[b][:].rearrange("p j (h d) -> p j d h", d=HD),
                                  bcast(P_inv[a][:], 3, HEADS), ALU.mult).then_inc(s["vsc"], 1)

            def body(n, m):
                late = isinstance(n, int)
                logits(n, m)
                if not late or n + 1 < STEPS:
                    scores(n + 1, m + 1)
                shift(n, m)
                if not late or n + 1 < STEPS:
                    mix(n + 1, m + 1)
                divide(n, m)
                if not late or n + 2 < STEPS:
                    norms(n + 2, m + 2)
            norms(0, 0)
            norms(1, 1)
            scores(0, 0)
            mix(0, 0)
            steps(dve, body)

        @block.gpsimd
        def _(pool):
            pool.sem_inc(s["oprod"], 2)

            def body(n, m):
                a = m % 2
                pool.wait_ge(s["vsc"], n + 5)
                pool.wait_ge(s["o_ps"], n + 1)
                for j in range(2):
                    last = pool.tensor_tensor(o_prod[:, :, j].rearrange("p d (e h) -> p d e h", h=HEADS),
                                              bcast(P_exp[a][:, j].rearrange("p (d e) -> p d e", e=HD), 3, HEADS),
                                              bcast(v_sc[a][:, j].rearrange("p (d h) -> p d h", h=HEADS), 2, HD), ALU.mult)
                last.then_inc(s["oprod"], 1)
            steps(pool, body)


def project_final(nc, t, k):
    with ExitStack() as ctx:
        def sb(n, shape):
            return ctx.enter_context(nc.sbuf_tensor(n, shape, F32))

        def psum(n):
            return ctx.enter_context(nc.psum_tensor(n, [128, 512], F32))

        def sem(n):
            return ctx.enter_context(nc.semaphore(n))
        EQ = 4
        NQ = HD // EQ
        o_in = [sb(f"o_in{n}", [HALF, NL // 2, HD, 2 * HEADS]) for n in range(2)]
        o_row = [sb(f"o_row{n}", [HALF, EQ, 128]) for n in range(2)]
        x_in = [sb(f"x1_in{n}", [128, HD, HALF]) for n in range(2)]
        oT = [sb(f"oT{n}", [128, EQ, HALF]) for n in range(2)]
        res = [sb(f"res{n}", [HALF, EQ, CH]) for n in range(2)]
        ps_t = [psum(f"ps_ot{n}") for n in range(2)]
        ps_o = [psum(f"ps_out{n}") for n in range(2)]
        loaded = [sem(f"fin_loaded{n}") for n in range(2)]
        rowed, turned, copied, summed, done = sem("o_rowed"), sem("o_turned"), sem("o_copied"), sem("out_ps"), sem("out_ready")
        stored = [sem(f"out_stored{n}") for n in range(2)]
        block = ctx.enter_context(nc.Block())

        def parts(b):
            return [(h, q, q % 2, (b * 2 + h) * NQ + q) for h in range(2) for q in range(NQ)]

        @block.sync
        def _(sp):
            with sp.Fori(0, BATCH) as b:
                for h in range(2):
                    sp.wait_ge(summed, (b * 2 + h + 1) * NQ)
                    sp.dma_start(o_in[h][:].rearrange("r n e c -> r (n e c)"),
                                 t.O[bass.ds(b * RPI + h * HALF, HALF)].rearrange("r n c -> r (n c)")).then_inc(loaded[h], 16)
                    src = t.X1[bass.ds(b, 1)].rearrange("b p (e h r) -> h p (b e) r", h=2, r=HALF)
                    sp.dma_start(x_in[h][:], src[h]).then_inc(loaded[h], 16)

        @block.tensor
        def _(pe):
            pe.sem_inc(summed, 2 * NQ)

            def turn(h, q, n, at):
                pe.wait_ge(rowed, at + 1)
                for m in range(EQ):
                    last = pe.transpose(ps_t[n][:, m * HALF:(m + 1) * HALF], o_row[n][:, m, :], k.ident[0:HALF, 0:HALF])
                last.then_inc(turned, 1)

            def project(h, q, n, at):
                pe.wait_ge(copied, at + 1)
                pe.wait_ge(done, at + 1)
                for m in range(EQ):
                    out = ps_o[n][0:HALF, m * CH:(m + 1) * CH]
                    pe.matmul(out, oT[n][:, m, :], k.w[:, PW, :], start=True, stop=False)
                    last = pe.matmul(out, x_in[h][:, q * EQ + m, :], k.ident[:], start=False, stop=True)
                last.then_inc(summed, 1)
            with pe.Fori(0, BATCH) as b:
                todo = parts(b)
                pe.wait_ge(loaded[0], b * 32 + 32)
                turn(*todo[0])
                for p, part in enumerate(todo):
                    if p + 1 < len(todo):
                        turn(*todo[p + 1])
                    if part[0] == 1 and part[1] == 0:
                        pe.wait_ge(loaded[1], b * 32 + 32)
                    project(*part)

        @block.scalar
        def _(act):
            for n in range(2):
                act.sem_inc(stored[n], 16)

            def row(b, h, q, n, at):
                act.wait_ge(loaded[h], b * 32 + 32)
                act.activation(o_row[n][:].rearrange("r e (n c) -> r e n c", c=2 * HEADS),
                               o_in[h][:, :, q * EQ:(q + 1) * EQ, :].rearrange("r n e c -> r e n c"), ACT.Copy).then_inc(rowed, 1)

            def copy(h, q, n, at):
                act.wait_ge(turned, at + 1)
                act.activation(oT[n][:].rearrange("p a r -> p (a r)"), ps_t[n][:, 0:EQ * HALF], ACT.Copy).then_inc(copied, 1)

            def store(b, h, q, n, at):
                act.wait_ge(done, at + 3)
                rows = t.out_rows[bass.ds(b * TOK, TOK), :].rearrange("(e h r) c -> h r e c", h=2, r=HALF)
                act.dma_start(rows[h][:, q * EQ:(q + 1) * EQ, :], res[n][:]).then_inc(stored[n], 16)
            with act.Fori(0, BATCH) as b:
                todo = parts(b)
                row(b, *todo[0])
                for p, part in enumerate(todo):
                    if p + 1 < len(todo):
                        row(b, *todo[p + 1])
                    copy(*part)
                    if p:
                        store(b, *todo[p - 1])
                store(b, *todo[-1])
            for n in range(2):
                act.wait_ge(stored[n], 16 * (BATCH * NQ + 1))

        @block.vector
        def _(dve):
            dve.sem_inc(done, 2)
            with dve.Fori(0, BATCH) as b:
                for h, q, n, at in parts(b):
                    dve.wait_ge(summed, at + 1 + 2 * NQ)
                    dve.wait_ge(stored[n], b * (NQ * 16) + (h * NQ // 2 + q // 2 + 1) * 16)
                    dve.tensor_tensor(res[n][:], ps_o[n][0:HALF, :].rearrange("p (a c) -> p a c", a=EQ),
                                      bcast(k.proj_b[0:HALF, :], 1, EQ), ALU.add).then_inc(done, 1)


def build(nc, t):
    scratch(nc, t)
    with ExitStack() as ctx:
        k = Net()

        def sb(n, shape):
            return ctx.enter_context(nc.sbuf_tensor(n, shape, F32))
        k.w = sb("weights", [128, WEIGHT_TILES, 128])
        k.bias = sb("biases", [128, 10])
        k.ident, k.avg, k.ones = sb("ident", [128, 128]), sb("group_avg", [128, 128]), sb("ones", [128, 128])
        k.rpe_in = sb("rpe_in", [3, 128])
        k.proj_b = sb("proj_b", [128, CH])
        k.fwd_h, k.fwd_w = sb("fwd_h", [120, NF]), sb("fwd_w", [120, 3, NFFT])
        k.tap_p, k.tap_q = sb("tap_p", [TAPS, 2 * NF]), sb("tap_q", [TAPS, 6, NFFT])
        k.inv_w, k.inv_h = sb("inv_w", [NFFT, 3, NFFT]), sb("inv_h", [2 * NF, 2, 2 * SIDE])
        load_weights(nc, t, k)
        project_in(nc, t, k)
        make_taps(nc, t, k)
        convolve(nc, t, k)
        project_out(nc, t, k)
        attend(nc, t, k)
        project_final(nc, t, k)


def tables():
    import numpy as np
    two_pi = 2.0 * np.pi / NFFT
    f, g, m = np.arange(NF), np.arange(NFFT), np.arange(SIDE)
    taps = np.arange(TAPS) - (SIDE - 1)
    c = {}
    c["c_ident"] = np.eye(128)
    c["c_avg"] = np.kron(np.eye(128 // GROUP_CH), np.full((GROUP_CH, GROUP_CH), 1.0 / GROUP_CH))
    a = two_pi * np.outer(m, f)
    fh = np.zeros((120, NF)); fh[0:SIDE], fh[64:120] = np.cos(a), -np.sin(a)
    c["c_fwd_h"] = fh
    a = two_pi * np.outer(m, g)
    cw, sw = np.cos(a), np.sin(a)
    fw = np.zeros((120, 3, NFFT))
    fw[0:SIDE, 0], fw[64:120, 0] = cw, sw
    fw[0:SIDE, 1], fw[64:120, 1] = -sw, cw
    fw[0:SIDE, 2], fw[64:120, 2] = cw - sw, cw + sw
    c["c_fwd_w"] = fw
    a = two_pi * np.outer(taps, f)
    c["c_tap_p"] = np.concatenate([np.cos(a), -np.sin(a)], axis=1)
    a = two_pi * np.outer(taps, g)
    cq, sq = np.cos(a), np.sin(a)
    c["c_tap_q"] = np.stack([cq, sq, -sq - cq, cq - sq, cq - sq, cq + sq], axis=1)
    a = two_pi * np.outer(g, m)
    ci, si = np.cos(a) / NFFT, np.sin(a) / NFFT
    c["c_inv_w"] = np.stack([np.concatenate([ci - si, ci + si], 1), np.concatenate([-si, ci], 1),
                             np.concatenate([-ci, -si], 1)], axis=1)
    a = two_pi * np.outer(f, m)
    weight = np.where((f == 0) | (f == NF - 1), 1.0, 2.0)[:, None] / NFFT
    ih = np.zeros((2 * NF, 2, 2 * SIDE))
    for n, part in enumerate((weight * np.cos(a), -weight * np.sin(a))):
        ih[0:NF, n, 0:SIDE], ih[NF:, n, SIDE:] = part, part
    c["c_inv_h"] = ih
    p, q = np.meshgrid(np.arange(TAPS), np.arange(NFFT), indexing="ij")
    c["c_coords"] = np.stack([(p - (SIDE - 1)).ravel(), (q - (SIDE - 1)).ravel(), np.ones(TAPS * NFFT)])
    return {n: np.ascontiguousarray(v, dtype=np.float32) for n, v in c.items()}


_INS = ['x', 'L0_conv_W_u', 'L0_conv_b_u', 'L0_conv_W_v', 'L0_conv_b_v', 'L0_conv_W_o', 'L0_conv_b_o', 'L0_conv_rpe_in_w',
        'L0_conv_rpe_in_b', 'L0_conv_rpe_h_w', 'L0_conv_rpe_h_b', 'L0_conv_rpe_out_w', 'L0_conv_rpe_out_b', 'L1_conv_Wq',
        'L1_conv_Wk', 'L1_conv_Wv', 'L1_conv_proj_w', 'L1_conv_proj_b']


def kernel(**inputs):
    import numpy as _np
    import concourse.bacc as _bacc
    from concourse import mybir as _mybir
    from concourse.bass_utils import run_bass_kernel_spmd as _run

    nc = _bacc.Bacc("TRN2", target_bir_lowering=False, num_devices=1)
    arrays = {f"in_{n}": _np.ascontiguousarray(inputs[n]) for n in _INS}
    consts = tables()
    arrays.update({f"in_{n}": a for n, a in consts.items()})
    t = Net()
    t.__dict__.update({n[3:]: nc.dram_tensor(n, a.shape, _mybir.dt.from_np(a.dtype), kind="ExternalInput").ap()
                       for n, a in arrays.items()})
    out = nc.dram_tensor("out_0", (BATCH, SIDE, SIDE, CH), F32, kind="ExternalOutput").ap()
    t.x_rows = t.x.rearrange("b h w c -> (b h w) c")
    t.out_rows = out.rearrange("b h w c -> (b h w) c")
    build(nc, t)
    r = _run(nc, [arrays], core_ids=[0])
    return r.results[0]["out_0"]
```

```python
from contextlib import ExitStack

import concourse.bass as bass
from concourse import mybir

BATCH, SIDE, CH = 8, 56, 128
TOK = SIDE * SIDE
EXP = 2 * CH
GROUP_CH = 4
TAPS = 2 * SIDE - 1
NFFT = 2 * SIDE
NF = NFFT // 2 + 1
HEADS, HD = 8, 16

TT = 112
TPC = 4
COLS = TT * TPC
NCH = TOK // COLS
RC = 4 * TAPS
NRC = TAPS * NFFT // RC
CC = 8
NCC = EXP // CC
PADW = 64
RPI = TOK // HEADS // 2
NL = 16
RTOT = BATCH * RPI
PAIRS = NL // 2
RG = 128
HALF = RPI // 2

F32 = mybir.dt.float32
ALU = mybir.AluOpType
ACT = mybir.ActivationFunctionType
AX = mybir.AxisListType.X


def bcast(ap, axis, n):
    shape = list(ap.shape)
    shape.insert(axis, n)
    return ap.unsqueeze(axis).to_broadcast(shape)


def strided(ap, at, dims):
    return bass.AP(ap.tensor, ap.offset + at, [list(ap.ap[0])] + [list(d) for d in dims])


class Net:
    pass


def scratch(nc, t):
    def dram(name, shape):
        return nc.dram_tensor(name, shape, F32, kind="Internal").ap()
    t.XR = dram("x_rms", (BATCH, CH, TOK))
    t.V = dram("conv_in", (BATCH, SIDE, EXP, PADW))
    t.S = dram("shortcut", (BATCH, CH, TOK))
    t.G = dram("taps", (EXP, TAPS, NFFT))
    t.Y = dram("conv_out", (BATCH, EXP, TOK))
    t.X1 = dram("x_mid", (BATCH, CH, TOK))
    t.XN = dram("x_mid_normed", (CH, 2, PAIRS, RTOT))
    t.O = dram("heads_out", (PAIRS * RTOT, HD * 2 * HEADS))


WEIGHT_TILES = 15
WU, WV, WO, RH, RO, WQ, WK, WVV, PW = 0, 2, 4, 6, 9, 11, 12, 13, 14


def load_weights(nc, t, k):
    with ExitStack() as ctx:
        raw = ctx.enter_context(nc.sbuf_tensor("w_raw", [128, WEIGHT_TILES, 128], F32))
        ps = [ctx.enter_context(nc.psum_tensor(f"w_ps{n}", [128, 512], F32)) for n in range(4)]
        loaded = ctx.enter_context(nc.semaphore("w_loaded"))
        turned = ctx.enter_context(nc.semaphore("w_turned"))
        copied = ctx.enter_context(nc.semaphore("w_copied"))
        filled = ctx.enter_context(nc.semaphore("w_filled"))
        consts = ctx.enter_context(nc.semaphore("consts_loaded"))
        block = ctx.enter_context(nc.Block())
        rows = [
            (WU, 2, t.L0_conv_W_u.rearrange("(a p) c -> p a c", p=128)),
            (WV, 2, t.L0_conv_W_v.rearrange("(a p) c -> p a c", p=128)),
            (WO, 2, t.L0_conv_W_o.rearrange("p (a c) -> p a c", a=2)),
            (RH, 3, t.L0_conv_rpe_h_w.rearrange("a p c -> p a c")),
            (RO, 2, t.L0_conv_rpe_out_w.rearrange("(a p) c -> p a c", p=128)),
            (WQ, 1, t.L1_conv_Wq), (WK, 1, t.L1_conv_Wk), (WVV, 1, t.L1_conv_Wv),
            (PW, 1, t.L1_conv_proj_w),
        ]
        biases = [
            (0, 2, t.L0_conv_b_u.rearrange("(a p) -> p a", p=128)),
            (2, 2, t.L0_conv_b_v.rearrange("(a p) -> p a", p=128)),
            (4, 1, t.L0_conv_b_o.rearrange("(a p) -> p a", p=128)),
            (5, 3, t.L0_conv_rpe_h_b.rearrange("a p -> p a")),
            (8, 2, t.L0_conv_rpe_out_b.rearrange("(a p) -> p a", p=128)),
        ]
        consts_in = [(k.ident[:], t.c_ident), (k.avg[:], t.c_avg), (k.fwd_h[:], t.c_fwd_h),
                     (k.fwd_w[:], t.c_fwd_w), (k.tap_p[:], t.c_tap_p), (k.tap_q[:], t.c_tap_q),
                     (k.inv_w[:], t.c_inv_w), (k.inv_h[:], t.c_inv_h),
                     (k.rpe_in[0:2, :], t.L0_conv_rpe_in_w.rearrange("o i -> i o")),
                     (k.rpe_in[2:3, :], t.L0_conv_rpe_in_b.rearrange("(a o) -> a o", a=1)),
                     (k.proj_b[:], t.L1_conv_proj_b.rearrange("(a o) -> a o", a=1).to_broadcast([128, CH]))]

        @block.sync
        def _(sp):
            for at, n, src in rows:
                dst = raw[:, at:at + n, :] if n > 1 else raw[:, at, :]
                sp.dma_start(dst, src).then_inc(loaded, 16)

        @block.scalar
        def _(act):
            for at, n, src in biases:
                act.dma_start(k.bias[:, at:at + n], src, allow_slow_non_contiguous=True).then_inc(consts, 16)
            for dst, src in consts_in:
                act.dma_start(dst, src, allow_slow_non_contiguous=True).then_inc(consts, 16)
            act.wait_ge(consts, 16 * (len(biases) + len(consts_in)))
            act.wait_ge(loaded, 16 * len(rows))

        @block.vector
        def _(dve):
            dve.memset(k.ones[:], 1.0).then_inc(filled, 1)
            dve.wait_ge(filled, 1)
            for n in range(4):
                lo, hi = 4 * n, min(4 * n + 4, WEIGHT_TILES)
                dve.wait_ge(turned, n + 1)
                dve.tensor_copy(k.w[:, lo:hi, :],
                                ps[n][:, 0:128 * (hi - lo)].rearrange("p (a c) -> p a c", c=128)).then_inc(copied, 1)
            dve.wait_ge(copied, 4)

        @block.tensor
        def _(pe):
            pe.wait_ge(loaded, 16 * len(rows))
            pe.wait_ge(consts, 16 * (len(biases) + len(consts_in)))
            for n in range(4):
                lo, hi = 4 * n, min(4 * n + 4, WEIGHT_TILES)
                for m in range(lo, hi):
                    last = pe.transpose(ps[n][:, 128 * (m - lo):128 * (m - lo) + 128], raw[:, m, :], k.ident[:])
                last.then_inc(turned, 1)


class GroupStats:

    def __init__(self, ctx, nc, name):
        def sb(n, shape):
            return ctx.enter_context(nc.sbuf_tensor(f"{name}_{n}", shape, F32))

        def sem(n):
            return ctx.enter_context(nc.semaphore(f"{name}_{n}"))
        self.parts = sb("bn_parts", [128, NCH, 6])
        self.mv = sb("chan_mv", [128, 2])
        self.gm = sb("group_mv", [128, 2])
        self.dev = sb("dev", [128, 1])
        self.dev2 = sb("dev2", [128, 1])
        self.var = sb("var", [128, 1])
        self.std = sb("std", [128, 1])
        self.scale = sb("scale", [128, 1])
        self.shift = sb("shift", [128, 1])
        self.ps = ctx.enter_context(nc.psum_tensor(f"{name}_ps", [128, 512], F32))
        self.s_seen = sem("seen")
        self.s_parts, self.s_mv, self.s_gm_ps, self.s_gm = sem("parts"), sem("mv"), sem("gm_ps"), sem("gm")
        self.s_dev, self.s_dev2, self.s_dev_ps, self.s_var = sem("dev"), sem("dev2"), sem("dev_ps"), sem("var")
        self.s_var_eps, self.s_std, self.s_scale, self.s_shift = sem("var_eps"), sem("std"), sem("scale_r"), sem("shift_r")

    def on_vector(self, dve, b):
        dve.wait_ge(self.s_parts, (b + 1) * NCH)
        dve.sem_inc(self.s_seen, 1)
        dve.bn_aggr(self.mv[:], self.parts[:]).then_inc(self.s_mv, 1)
        dve.wait_ge(self.s_gm_ps, b + 1)
        dve.tensor_copy(self.gm[:], self.ps[:, 0:2]).then_inc(self.s_gm, 1)
        dve.wait_ge(self.s_gm, b + 1)
        dve.tensor_tensor(self.dev[:], self.mv[:, 0:1], self.gm[:, 0:1], ALU.subtract).then_inc(self.s_dev, 1)
        dve.wait_ge(self.s_dev, b + 1)
        dve.tensor_tensor(self.dev2[:], self.dev[:], self.dev[:], ALU.mult).then_inc(self.s_dev2, 1)
        dve.wait_ge(self.s_dev_ps, b + 1)
        dve.tensor_tensor(self.var[:], self.ps[:, 2:3], self.gm[:, 1:2], ALU.add).then_inc(self.s_var, 1)
        dve.wait_ge(self.s_var, b + 1)
        dve.tensor_scalar(self.var[:], self.var[:], 1e-5, None, ALU.add).then_inc(self.s_var_eps, 1)
        dve.wait_ge(self.s_std, b + 1)
        dve.reciprocal(self.scale[:], self.std[:]).then_inc(self.s_scale, 1)
        dve.wait_ge(self.s_scale, b + 1)
        dve.tensor_scalar(self.shift[:], self.gm[:, 0:1], self.scale[:, 0:1], -1.0, ALU.mult, ALU.mult).then_inc(self.s_shift, 1)
        dve.wait_ge(self.s_shift, b + 1)

    def on_tensor(self, pe, b, avg):
        pe.wait_ge(self.s_mv, b + 1)
        pe.matmul(self.ps[:, 0:2], avg, self.mv[:], start=True, stop=True).then_inc(self.s_gm_ps, 1)
        pe.wait_ge(self.s_dev2, b + 1)
        pe.matmul(self.ps[:, 2:3], avg, self.dev2[:], start=True, stop=True).then_inc(self.s_dev_ps, 1)

    def on_scalar(self, act, b):
        act.wait_ge(self.s_var_eps, b + 1)
        act.activation(self.std[:], self.var[:], ACT.Sqrt).then_inc(self.s_std, 1)


def project_in(nc, t, k):
    with ExitStack() as ctx:
        def sb(n, shape):
            return ctx.enter_context(nc.sbuf_tensor(n, shape, F32))

        def psum(n):
            return ctx.enter_context(nc.psum_tensor(n, [128, 512], F32))

        def sem(n):
            return ctx.enter_context(nc.semaphore(n))
        x_in = [sb(f"x_in{n}", [TT, NCH * TPC, CH]) for n in range(2)]
        xT, xg, xr, short = ([sb(f"{n}{m}", [128, TOK]) for m in range(2)] for n in ("xT", "xg", "xr", "short"))
        sq = [sb(f"x_sq{n}", [128, COLS]) for n in range(2)]
        rt, rt_eps, rinv = sb("rt", [TT, NCH * TPC]), sb("rt_eps", [TT, NCH * TPC]), sb("rinv", [TT, NCH * TPC])
        ROWS = COLS // SIDE
        v_sb = [sb(f"v_sb{n}", [128, 2, ROWS, PADW]) for n in range(2)]
        gs = GroupStats(ctx, nc, "gn0")
        ps_ss = psum("ps_sumsq")
        ps_t, ps_bc, ps_v = ([psum(f"{n}{m}") for m in range(2)] for n in ("ps_turn", "ps_bcast", "ps_v"))
        x_loaded = [sem(f"x_loaded{n}") for n in range(2)]
        x_turned, x_copied, xg_ready, short_ready = sem("x_turned"), sem("x_copied"), sem("xg_ready"), sem("short_ready")
        sq_ready, ss_ready, rt_ready, eps_ready = sem("sq_ready"), sem("ss_ready"), sem("rt_ready"), sem("eps_ready")
        rinv_ready, bc_ready, xr_ready = sem("rinv_ready"), sem("bc_ready"), sem("xr_ready")
        v_ps_ready, v_ready, copies_read, v_cleared = sem("v_ps_ready"), sem("v_ready"), sem("copies_read"), sem("v_cleared")
        v_stored, xr_stored, short_stored = ([sem(f"{n}{m}") for m in range(2)] for n in ("v_stored", "xr_stored", "short_stored"))
        block = ctx.enter_context(nc.Block())

        def cols(c):
            return slice(c * COLS, (c + 1) * COLS)

        def images(eng, body):
            def part(b, a):
                body(b, a, b + 2 < BATCH, 0 <= b + 1 < BATCH, b >= 0)
            part(-2, 0)
            part(-1, 1)
            with eng.Fori(0, BATCH // 2 - 1) as i:
                for a in range(2):
                    body(i * 2 + a, a, True, True, True)
            part(BATCH - 2, 0)
            part(BATCH - 1, 1)

        @block.sync
        def _(sp):
            with sp.Fori(0, BATCH // 2) as i:
                for a in range(2):
                    b = i * 2 + a
                    sp.wait_ge(x_turned, b * NCH + NCH)
                    src = t.x_rows[bass.ds(b * TOK, TOK), :]
                    sp.dma_start(x_in[a][:], src.rearrange("(a p) c -> p a c", p=TT)).then_inc(x_loaded[a], 16)

        @block.gpsimd
        def _(pool):
            for n in range(2):
                pool.memset(v_sb[n][:], 0.0).then_inc(v_cleared, 1)

        @block.tensor
        def _(pe):
            pe.sem_inc(x_turned, 2 * NCH)
            pe.sem_inc(ss_ready, 2)

            def body(b, a, turn, norm, project):
                if turn:
                    pe.wait_ge(x_loaded[a], (b + 2 - a) * 8 + 16)
                for c in range(NCH + 1):
                    if c < NCH and project:
                        pe.wait_ge(rinv_ready, b + 1)
                        for m in range(TPC):
                            last = pe.transpose(ps_bc[c % 2][:, m * TT:(m + 1) * TT], rinv[:, c * TPC + m:c * TPC + m + 1].to_broadcast([TT, 128]),
                                                k.ident[0:TT, 0:TT])
                        last.then_inc(bc_ready, 1)
                    if c < NCH and turn:
                        pe.wait_ge(x_copied, (b + 2) * NCH + c + 1)
                        for m in range(TPC):
                            last = pe.transpose(ps_t[(a * NCH + c) % 2][:, m * TT:(m + 1) * TT], x_in[a][:, c * TPC + m, :], k.ident[0:TT, 0:TT])
                        last.then_inc(x_turned, 1)
                    if c and norm:
                        pe.wait_ge(sq_ready, (b + 1) * NCH + c)
                        for m in range(TPC):
                            last = pe.matmul(ps_ss[0:TT, (c - 1) * TPC + m:(c - 1) * TPC + m + 1], sq[(c - 1) % 2][:, m * TT:(m + 1) * TT], k.ones[:, 0:1],
                                             start=True, stop=True)
                        last.then_inc(ss_ready, 1)
                    if c and project:
                        pe.wait_ge(xr_ready, b * NCH + c + 1)
                        for h in range(2):
                            pe.wait_ge(v_ready, (b * NCH + c - 1) * 2 + h + 1)
                            pe.matmul(ps_v[h][:, 0:COLS], k.w[:, WV + h, :], xr[a][:, cols(c - 1)], start=True, stop=True).then_inc(v_ps_ready, 1)
                if turn:
                    gs.on_tensor(pe, b + 2, k.avg[:])
            images(pe, body)

        @block.scalar
        def _(act):
            act.sem_inc(x_copied, 2)
            act.sem_inc(v_ready, 2)
            for n in range(2):
                act.sem_inc(v_stored[n], 32)
                act.sem_inc(xr_stored[n], 16)
                act.sem_inc(short_stored[n], 16)
            act.wait_ge(v_cleared, 2)

            def body(b, a, turn, norm, project):
                def silu(c):
                    n = (a * NCH + c) % 2
                    act.wait_ge(v_stored[n], (b - a) * (NCH * 16) + ((a * NCH + c) // 2 + 1) * 32)
                    for h in range(2):
                        act.wait_ge(v_ps_ready, (b * NCH + c) * 2 + h + 1)
                        act.activation(v_sb[n][:, h, :, 0:SIDE], ps_v[h][:, 0:COLS].rearrange("p (r w) -> p r w", w=SIDE), ACT.Silu,
                                       bias=k.bias[:, 2 + h:3 + h]).then_inc(v_ready, 1)

                def store(c):
                    n = (a * NCH + c) % 2
                    act.wait_ge(v_ready, (b * NCH + c) * 2 + 4)
                    for h in range(2):
                        dst = t.V[bass.ds(b, 1), c * ROWS:(c + 1) * ROWS, h * 128:(h + 1) * 128, :]
                        act.dma_start(dst.rearrange("b r c w -> c (b r) w"), v_sb[n][:, h]).then_inc(v_stored[n], 16)
                if turn:
                    act.wait_ge(copies_read, b + 3)
                for c in range(NCH + 2):
                    if c > 1 and project:
                        silu(c - 2)
                    if c < NCH and turn:
                        act.wait_ge(x_turned, (b + 4) * NCH + c + 1)
                        act.activation(xT[a][:, cols(c)], ps_t[(a * NCH + c) % 2][:, 0:COLS], ACT.Copy).then_inc(x_copied, 1)
                    if c < NCH and norm:
                        act.wait_ge(xg_ready, (b + 1) * NCH + c + 1)
                        act.wait_ge(ss_ready, (b + 1) * NCH + c + 1)
                        act.activation(sq[c % 2][:], xg[1 - a][:, cols(c)], ACT.Square).then_inc(sq_ready, 1)
                    if c > 1 and project:
                        store(c - 2)
                if turn:
                    gs.on_scalar(act, b + 2)
                if norm:
                    act.wait_ge(ss_ready, (b + 2) * NCH + 2)
                    act.activation(rt[:], ps_ss[0:TT, 0:NCH * TPC], ACT.Sqrt, scale=1.0 / CH).then_inc(rt_ready, 1)
                    act.wait_ge(short_ready, (b + 2) * NCH)
                    act.dma_start(t.S[bass.ds(b + 1, 1)].rearrange("b p t -> (b p) t"), short[1 - a][:]).then_inc(short_stored[1 - a], 16)
                if project:
                    act.wait_ge(xr_ready, b * NCH + NCH + 1)
                    act.dma_start(t.XR[bass.ds(b, 1)].rearrange("b p t -> (b p) t"), xr[a][:]).then_inc(xr_stored[a], 16)
            images(act, body)
            for n in range(2):
                act.wait_ge(xr_stored[n], 16 * (BATCH // 2 + 1))
                act.wait_ge(short_stored[n], 16 * (BATCH // 2 + 1))
                act.wait_ge(v_stored[n], 32 * (BATCH * NCH // 2 + 1))

        @block.vector
        def _(dve):
            dve.sem_inc(copies_read, 2)
            dve.sem_inc(xr_ready, 1)

            def body(b, a, turn, norm, project):
                if norm:
                    dve.wait_ge(short_stored[1 - a], (b - a) * 8 + 16 + 16 * a)
                    if project:
                        dve.wait_ge(xr_ready, b * NCH + 1)
                if project:
                    dve.wait_ge(xr_stored[a], (b - a) * 8 + 16)
                for c in range(NCH + 1):
                    if c and project:
                        dve.wait_ge(bc_ready, b * NCH + c)
                        dve.tensor_tensor(xr[a][:, cols(c - 1)], xg[a][:, cols(c - 1)], ps_bc[(c - 1) % 2][:, 0:COLS], ALU.mult).then_inc(xr_ready, 1)
                    if c < NCH and norm:
                        dve.tensor_scalar(xg[1 - a][:, cols(c)], xT[1 - a][:, cols(c)], gs.scale[:, 0:1], gs.shift[:, 0:1], ALU.mult, ALU.add)\
                           .then_inc(xg_ready, 1)
                    if c and turn:
                        dve.wait_ge(x_copied, (b + 2) * NCH + c + 2)
                        dve.bn_stats(gs.parts[:, c - 1, :], xT[a][:, cols(c - 1)]).then_inc(gs.s_parts, 1)
                    if c < NCH and norm:
                        dve.wait_ge(xg_ready, (b + 1) * NCH + c + 1)
                        dve.scalar_tensor_tensor(out=short[1 - a][:, cols(c)], in0=xT[1 - a][:, cols(c)], scalar=k.bias[:, 4:5],
                                                 in1=xg[1 - a][:, cols(c)], op0=ALU.add, op1=ALU.add).then_inc(short_ready, 1)
                if norm:
                    dve.wait_ge(short_ready, (b + 2) * NCH)
                    dve.sem_inc(copies_read, 1)
                if turn:
                    gs.on_vector(dve, b + 2)
                if norm:
                    dve.wait_ge(rt_ready, b + 2)
                    dve.tensor_scalar(rt_eps[:], rt[:], 1e-8, None, ALU.add).then_inc(eps_ready, 1)
                    dve.wait_ge(eps_ready, b + 2)
                    dve.reciprocal(rinv[:], rt_eps[:]).then_inc(rinv_ready, 1)
                    dve.wait_ge(rinv_ready, b + 2)
            images(dve, body)


def make_taps(nc, t, k):
    with ExitStack() as ctx:
        def sb(n, shape):
            return ctx.enter_context(nc.sbuf_tensor(n, shape, F32))

        def psum(n):
            return ctx.enter_context(nc.psum_tensor(n, [128, 512], F32))

        def sem(n):
            return ctx.enter_context(nc.semaphore(n))
        W = 4
        STEPS = NRC // W
        ROUNDS = 4
        acts = sb("acts", [128, NRC * RC])
        coords = [sb(f"coords{n}", [3, W * RC]) for n in range(2)]
        pos, sq = ([sb(f"{n}{m}", s) for m in range(count)] for n, s, count in
                         (("pos_relu", [128, RC], 2 * W), ("pos_sq", [128, RC], W)))
        rt, rt_eps, rinv = sb("pos_rt", [TAPS, 4 * W]), sb("pos_eps", [TAPS, 4 * W]), sb("pos_rinv", [TAPS, 4 * W])
        taps = [sb(f"taps_sb{n}", [128, 2, RC]) for n in range(4)]
        ps_t = [psum(f"ps_pos{n}") for n in range(W)]
        ps_bc = [psum(f"ps_pos_bc{n}") for n in range(3)]
        ps_ss = psum("ps_pos_ss")
        c_loaded = [sem(f"coords_loaded{n}") for n in range(2)]
        lin, relu, sqr, ss, rt_s = sem("pos_lin"), sem("pos_relu_r"), sem("pos_sq_r"), sem("pos_ss"), sem("pos_rt_r")
        eps, inv, bc, act_r = sem("pos_eps_r"), sem("pos_inv"), sem("pos_bc"), sem("acts_ready")
        g_ps, g_sb = sem("taps_ps"), sem("taps_copied")
        g_stored = [sem(f"taps_stored{n}") for n in range(4)]
        block = ctx.enter_context(nc.Block())

        def at_cols(n):
            return bass.ds(n * RC, RC)

        @block.sync
        def _(sp):
            for s in range(STEPS):
                if s >= 2:
                    sp.wait_ge(lin, (s - 1) * W)
                sp.dma_start(coords[s % 2][:], t.c_coords[:, s * W * RC:(s + 1) * W * RC]).then_inc(c_loaded[s % 2], 16)

        @block.tensor
        def _(pe):
            def linear(r, s):
                for m in range(W):
                    at = (s + r * STEPS) * W + m
                    if r or not isinstance(s, int) or s:
                        pe.wait_ge(relu, at - W + 1)
                    if r == 0:
                        pe.wait_ge(c_loaded[s % 2], (s // 2 + 1) * 16)
                        lhs, rhs = k.rpe_in[:], coords[s % 2][:, m * RC:(m + 1) * RC]
                    else:
                        pe.wait_ge(act_r, at - NRC + 1 + 2 * W)
                        lhs, rhs = k.w[:, RH + r - 1, :], acts[:, at_cols(s * W + m)]
                    pe.matmul(ps_t[m][:, 0:RC], lhs, rhs, start=True, stop=True).then_inc(lin, 1)

            def sums_and_spread(at, spread_last, first):
                for m in range(W):
                    pe.wait_ge(sqr, at * W + m + 1)
                    for x in range(4):
                        last = pe.matmul(ps_ss[0:TAPS, 4 * m + x:4 * m + x + 1], sq[m][:, x * TAPS:(x + 1) * TAPS], k.ones[:, 0:1],
                                         start=True, stop=True)
                    if m == W - 1:
                        last.then_inc(ss, 1)
                    if spread_last:
                        spread(at - 1, m, first)

            def spread(at, m, first):
                pe.wait_ge(inv, at + 1)
                if m == 3:
                    pe.wait_ge(act_r, at * W + 1 + 2 * W)
                elif not first:
                    pe.wait_ge(act_r, at * W + 2 * W)
                for x in range(4):
                    last = pe.transpose(ps_bc[m % 3][:, x * TAPS:(x + 1) * TAPS], rinv[:, 4 * m + x:4 * m + x + 1].to_broadcast([TAPS, 128]),
                                        k.ident[0:TAPS, 0:TAPS])
                last.then_inc(bc, 1)
            linear(0, 0)
            for r in range(ROUNDS):
                def step(s, nxt):
                    known = r == 0 and isinstance(s, int)
                    sums_and_spread(s + r * STEPS, not (known and s == 0), known and s == 1)
                    if nxt is not None:
                        linear(*nxt)
                if r == 0:
                    for s in range(STEPS - 1):
                        step(s, (r, s + 1))
                else:
                    with pe.Fori(0, STEPS - 1) as s:
                        step(s, (r, s + 1))
                step(STEPS - 1, (r + 1, 0) if r + 1 < ROUNDS else None)
            for m in range(W):
                spread(ROUNDS * STEPS - 1, m, False)
            with pe.Fori(0, NRC // 2) as i:
                for n in range(2):
                    at = i * 2 + n
                    pe.wait_ge(act_r, at + (ROUNDS - 1) * NRC + 1 + 2 * W)
                    for h in range(2):
                        pe.wait_ge(g_sb, at * 2 + h + 1)
                        pe.matmul(ps_t[2 * n + h][:, 0:RC], k.w[:, RO + h, :], acts[:, at_cols(at)], start=True, stop=True).then_inc(g_ps, 1)

        @block.scalar
        def _(act):
            for n in range(4):
                act.sem_inc(g_stored[n], 16)
            for r in range(ROUNDS):
                bias = 0.0 if r == 0 else k.bias[:, 4 + r:5 + r]

                def step(s, half):
                    for m in range(W):
                        at = (s + r * STEPS) * W + m
                        act.wait_ge(lin, at + 1)
                        act.activation(sq[m][:], ps_t[m][:, 0:RC], ACT.Square, bias=bias).then_inc(sqr, 1)
                        act.wait_ge(act_r, at + 1)
                        act.activation(pos[half * W + m][:], ps_t[m][:, 0:RC], ACT.Relu, bias=bias).then_inc(relu, 1)
                    act.wait_ge(ss, s + r * STEPS + 1)
                    act.activation(rt[:], ps_ss[0:TAPS, 0:4 * W], ACT.Sqrt, scale=1.0 / CH).then_inc(rt_s, 1)
                with act.Fori(0, STEPS // 2) as i:
                    for a in range(2):
                        step(i * 2 + a, (r * STEPS + a) % 2)
                step(STEPS - 1, (r * STEPS + STEPS - 1) % 2)
            act.wait_ge(act_r, ROUNDS * NRC + 2 * W)
            act.sem_inc(g_sb, 4)
            flat = t.G.rearrange("(a p) r q -> p a (r q)", p=128)

            def store(at, n):
                act.wait_ge(g_sb, at * 2 + 6)
                act.dma_start(flat[:, :, at_cols(at)], taps[n][:]).then_inc(g_stored[n], 16)
            with act.Fori(0, NRC // 4) as i:
                for n in range(4):
                    at = i * 4 + n
                    act.wait_ge(g_stored[n], i * 16 + 16)
                    for h in range(2):
                        act.wait_ge(g_ps, at * 2 + h + 1)
                        act.activation(taps[n][:, h, :], ps_t[2 * (n % 2) + h][:, 0:RC], ACT.Identity,
                                       bias=k.bias[:, 8 + h:9 + h]).then_inc(g_sb, 1)
                    store(at, n)
            for n in range(4):
                act.wait_ge(g_stored[n], 16 * (NRC // 4 + 1))

        @block.vector
        def _(dve):
            dve.sem_inc(act_r, 2 * W)
            with dve.Fori(0, ROUNDS * STEPS // 2) as i:
                for half in range(2):
                    at = i * 2 + half
                    dve.wait_ge(rt_s, at + 1)
                    dve.tensor_scalar(rt_eps[:], rt[:], 1e-8, None, ALU.add).then_inc(eps, 1)
                    dve.wait_ge(eps, at + 1)
                    dve.reciprocal(rinv[:], rt_eps[:]).then_inc(inv, 1)
                    dve.wait_ge(inv, at + 1)
                    for m in range(W):
                        dve.wait_ge(bc, at * W + m + 1)
                        dve.wait_ge(relu, at * W + m + 1)
                        dve.tensor_tensor(acts[:, at_cols(at % STEPS * W + m)], pos[half * W + m][:], ps_bc[m % 3][:, 0:RC], ALU.mult)\
                           .then_inc(act_r, 1)


def convolve(nc, t, k):
    PC = CC * NF
    with ExitStack() as ctx:
        def sb(n, shape):
            return ctx.enter_context(nc.sbuf_tensor(n, shape, F32))

        def psum(n):
            return ctx.enter_context(nc.psum_tensor(n, [128, 512], F32))

        def sem(n):
            return ctx.enter_context(nc.semaphore(n))
        g_in = sb("g_in", [TAPS, CC, TAPS])
        g_half = sb("g_half", [TAPS, 2, CC, NF])
        spec = [sb(f"spec{n}", [NFFT, 2, PC]) for n in range(2)]
        v_in = [sb(f"v_in{n}", [SIDE, CC * PADW]) for n in range(2)]
        x_half = [sb(f"x_half{n}", [120, CC // 2, 2, NF]) for n in range(2)]
        terms = sb("terms", [NFFT, 4, PC])
        prod = [sb(f"prod{n}", [NFFT, 2, PC]) for n in range(2)]
        q_half = sb("q_half", [2 * NF, CC // 2, 2, SIDE])
        y_sb = [sb(f"y_sb{n}", [2 * SIDE, CC // 2, SIDE]) for n in range(2)]
        ps_g, ps_x, ps_q, ps_y = psum("ps_g"), psum("ps_x"), psum("ps_q"), psum("ps_y")
        ps_z = [[psum(f"ps_z{m}{n}") for n in range(2)] for m in range(2)]
        cleared = sem("x_half_cleared")
        g_loaded, g_ps, g_read, spec_read = sem("g_loaded"), sem("g_ps"), sem("g_read"), sem("spec_read")
        v_loaded = [sem(f"v_loaded{n}") for n in range(2)]
        x_ps, x_half_r, z_ps, terms_r, prod_r, q_ps, q_r = (sem(n) for n in ("x_ps", "x_half_r", "z_ps", "terms_r", "prod_r", "q_ps", "q_r"))
        y_ps, y_r = sem("y_ps"), sem("y_r")
        y_stored = [sem(f"y_stored{n}") for n in range(2)]
        block = ctx.enter_context(nc.Block())

        def chunks(eng, body):
            with eng.Fori(0, NCC // 2 - 1) as i:
                for a in range(2):
                    body(i * 2 + a, a)
            for a in range(2):
                body(NCC - 2 + a, a)

        def inside(c, b=0):
            return not isinstance(c, int) or c * BATCH + b < NCC * BATCH

        @block.sync
        def _(sp):
            def load_taps(c):
                sp.dma_start(g_in[:], t.G[bass.ds(c * CC, CC), :, 0:TAPS].rearrange("c p q -> p c q")).then_inc(g_loaded, 16)
            load_taps(0)

            def body(c, a):
                for b in range(BATCH):
                    sp.wait_ge(x_ps, c * BATCH + b + 1)
                    sp.dma_start(v_in[b % 2][:], t.V[b, :, bass.ds(c * CC, CC), :].rearrange("h c w -> h (c w)")).then_inc(v_loaded[b % 2], 16)
                    if b == 2 and inside(c + 1):
                        sp.wait_ge(g_ps, c * 4 + 2)
                        load_taps(c + 1)
            chunks(sp, body)

        @block.gpsimd
        def _(pool):
            for n in range(2):
                pool.memset(x_half[n][:], 0.0).then_inc(cleared, 1)

        @block.tensor
        def _(pe):
            pe.sem_inc(x_ps, 2)

            def taps(c, part):
                if not isinstance(c, int) or c or part:
                    pe.wait_ge(g_read, c * 4 + part)
                if part == 0:
                    pe.wait_ge(g_loaded, c * 16 + 16)
                if part < 2:
                    for x in range(4):
                        last = pe.matmul(ps_g[0:TAPS, x * 2 * NF:(x + 1) * 2 * NF], g_in[:, 4 * part + x, :], k.tap_p[:], start=True, stop=True)
                else:
                    for ri in range(2):
                        last = pe.matmul(ps_g[0:NFFT, 0:PC], k.tap_q[:, 2 * (part - 2) + ri, :],
                                         g_half[:, ri].rearrange("p c f -> p (c f)"), start=(ri == 0), stop=(ri == 1))
                last.then_inc(g_ps, 1)

            def image_h(n, b):
                pe.wait_ge(v_loaded[b % 2], (n - b) * 8 + (b // 2 + 1) * 16)
                pe.wait_ge(x_half_r, n + 1)
                for c in range(CC // 2):
                    last = pe.matmul(ps_x[0:120, c * 2 * NF:(c + 1) * 2 * NF], v_in[b % 2][:, c * 2 * PADW:c * 2 * PADW + 120], k.fwd_h[:],
                                     start=True, stop=True)
                last.then_inc(x_ps, 1)

            def image_w(n, b):
                pe.wait_ge(x_half_r, n + 2)
                pe.wait_ge(terms_r, n + 1)
                for x in range(2):
                    last = pe.matmul(ps_z[b % 2][x][0:NFFT, 0:PC], k.fwd_w[:, x, :], x_half[b % 2][:].rearrange("p c a f -> p (c a f)"), start=True, stop=True)
                last.then_inc(z_ps, 1)

            def back_w(n, b):
                pe.wait_ge(prod_r, n * 2 + 4)
                for c in range(CC // 2):
                    for x in range(2):
                        last = pe.matmul(ps_q[0:2 * NF, c * NFFT:(c + 1) * NFFT], prod[b % 2][:, x, c * 2 * NF:(c + 1) * 2 * NF],
                                         k.inv_w[:, x, :], start=(x == 0), stop=(x == 1))
                last.then_inc(q_ps, 1)

            def back_h(n):
                pe.wait_ge(q_r, n + 1)
                pe.wait_ge(y_r, n + 1)
                for x in range(2):
                    last = pe.matmul(ps_y[0:2 * SIDE, 0:CC // 2 * SIDE], k.inv_h[:, x, :], q_half[:, :, x, :],
                                     start=(x == 0), stop=(x == 1))
                last.then_inc(y_ps, 1)
            for part in range(4):
                taps(0, part)
            image_h(0, 0)
            image_h(1, 1)
            image_w(0, 0)
            image_h(2, 2)
            image_w(1, 1)

            def body(c, a):
                for b in range(BATCH):
                    n = c * BATCH + b
                    back_w(n, b)
                    if inside(c, b + 2):
                        image_w(n + 2, b + 2)
                    back_h(n)
                    if inside(c, b + 3):
                        image_h(n + 3, b + 3)
                    if b < 4 and inside(c + 1):
                        taps(c + 1, b)
            chunks(pe, body)

        @block.scalar
        def _(act):
            act.sem_inc(x_half_r, 1)
            for n in range(2):
                act.sem_inc(y_stored[n], 32)

            def copy_x(n, b):
                act.wait_ge(x_ps, n + 3)
                for a, lo in ((0, 0), (1, 64)):
                    for x, to in ((0, 0), (1, 64)):
                        src = ps_x[lo:lo + SIDE, 0:PC].rearrange("p (c x f) -> p c x f", x=2, f=NF)[:, :, x]
                        last = act.activation(x_half[b % 2][to:to + SIDE, :, a], src, ACT.Copy)
                last.then_inc(x_half_r, 1)

            def copy_taps(c, a, part):
                act.wait_ge(g_ps, c * 4 + part + 1)
                if part < 2:
                    act.activation(g_half[:, :, 4 * part:4 * part + 4, :].rearrange("p r c f -> p c r f"),
                                   ps_g[0:TAPS, 0:PC].rearrange("p (c r f) -> p c r f", r=2, f=NF), ACT.Copy).then_inc(g_read, 1)
                else:
                    act.wait_ge(spec_read, c + 1)
                    act.activation(spec[a % 2][:, part - 2, :], ps_g[0:NFFT, 0:PC], ACT.Copy).then_inc(g_read, 1)

            def store(c, b):
                act.wait_ge(y_r, c * BATCH + b + 2)
                dst = t.Y[b, bass.ds(c * CC, CC), :].rearrange("(c a) (h w) -> a h c w", a=2, w=SIDE)
                for x in range(2):
                    act.dma_start(dst[x], y_sb[b % 2][x * SIDE:(x + 1) * SIDE]).then_inc(y_stored[b % 2], 16)
            for part in range(4):
                copy_taps(0, 0, part)
            act.wait_ge(cleared, 2)
            for b in range(3):
                copy_x(b, b)

            def body(c, a):
                for b in range(BATCH):
                    n = c * BATCH + b
                    act.wait_ge(q_ps, n + 1)
                    act.activation(q_half[:].rearrange("p c r w -> p (c r w)"), ps_q[0:2 * NF, 0:CC // 2 * NFFT], ACT.Copy).then_inc(q_r, 1)
                    if inside(c, b + 3):
                        copy_x(n + 3, b + 3)
                    if b < 4 and inside(c + 1):
                        copy_taps(c + 1, a + 1, b)
                    if b:
                        store(c, b - 1)
                store(c, BATCH - 1)
            chunks(act, body)
            for n in range(2):
                act.wait_ge(y_stored[n], 32 * (NCC * BATCH // 2 + 1))

        @block.vector
        def _(dve):
            dve.sem_inc(y_r, 1)
            dve.sem_inc(terms_r, 2)
            dve.sem_inc(spec_read, 2)
            dve.sem_inc(prod_r, 2)

            def multiply(n, b, a):
                dve.wait_ge(z_ps, n + 1)
                dve.wait_ge(prod_r, n * 2 + 2)
                for x, s, z in ((0, 0, 0), (1, 1, 1), (2, 0, 1), (3, 1, 0)):
                    last = dve.tensor_tensor(terms[:, x, :], spec[a][:, s, :], ps_z[b % 2][z][0:NFFT, 0:PC], ALU.mult)
                last.then_inc(terms_r, 1)
                dve.wait_ge(terms_r, n + 3)
                dve.tensor_tensor(prod[b % 2][:, 0, :], terms[:, 0, :], terms[:, 1, :], ALU.subtract).then_inc(prod_r, 1)
                dve.tensor_tensor(prod[b % 2][:, 1, :], terms[:, 2, :], terms[:, 3, :], ALU.add).then_inc(prod_r, 1)

            def copy_y(c, b):
                dve.wait_ge(y_ps, c * BATCH + b + 1)
                dve.wait_ge(y_stored[b % 2], c * (BATCH * 16) + (b // 2 + 1) * 32)
                dve.tensor_copy(y_sb[b % 2][:].rearrange("p c w -> p (c w)"), ps_y[0:2 * SIDE, 0:CC // 2 * SIDE]).then_inc(y_r, 1)
            dve.wait_ge(g_read, 4)
            multiply(0, 0, 0)

            def body(c, a):
                for b in range(BATCH):
                    n = c * BATCH + b
                    if b + 1 < BATCH:
                        multiply(n + 1, b + 1, a)
                    elif inside(c + 1):
                        dve.sem_inc(spec_read, 1)
                        dve.wait_ge(g_read, c * 4 + 8)
                        multiply(n + 1, 0, 1 - a)
                    copy_y(c, b)
            chunks(dve, body)


def project_out(nc, t, k):
    with ExitStack() as ctx:
        def sb(n, shape):
            return ctx.enter_context(nc.sbuf_tensor(n, shape, F32))

        def psum(n):
            return ctx.enter_context(nc.psum_tensor(n, [128, 512], F32))

        def sem(n):
            return ctx.enter_context(nc.semaphore(n))
        PARTS = ((0, 3), (3, NCH))
        xr = [sb(f"xr_in{n}", [128, TOK]) for n in range(2)]
        y = [sb(f"y{n}", [128, 2, TOK]) for n in range(2)]
        s = [sb(f"s{n}", [128, TOK]) for n in range(2)]
        u = [sb(f"u{n}", [128, 2, COLS]) for n in range(2)]
        z = [sb(f"z{n}", [128, 2, COLS]) for n in range(2)]
        x1 = [sb(f"x1_{n}", [128, TOK]) for n in range(2)]
        xn = sb("xn1", [128, 2, PAIRS, RPI])
        gs = GroupStats(ctx, nc, "gn1")
        ps_u = [psum(f"ps_u{n}") for n in range(4)]
        ps = [psum(f"ps_wo{n}") for n in range(2)]
        loaded = [sem(f"chunk_loaded{n}") for n in range(2 * len(PARTS))]
        u_ps, u_ready, z_ready, o_ps, x1_ready, xn_ready = (sem(n) for n in ("u_ps", "u_ready", "z_ready", "wo_ps", "x1_ready", "xn_ready"))
        x1_stored = [sem(f"x1_stored{n}") for n in range(2)]
        xn_stored, norm_seen = sem("xn_stored"), sem("norm_seen")
        block = ctx.enter_context(nc.Block())
        N = BATCH * NCH

        def images(eng, body):
            with eng.Fori(0, BATCH // 2 - 1) as i:
                for a in range(2):
                    body(i * 2 + a, a)
            for a in range(2):
                body(BATCH - 2 + a, a)

        def cols(c):
            return slice(c * COLS, (c + 1) * COLS)

        def inside(n):
            return not isinstance(n, int) or n < N

        @block.sync
        def _(sp):
            def load(b, a):
                for x, (lo, hi) in enumerate(PARTS):
                    at, part = slice(lo * COLS, hi * COLS), loaded[a * len(PARTS) + x]
                    sp.wait_ge(x1_ready, b * NCH + hi)
                    for dst, src in ((xr[a][:, at], t.XR[bass.ds(b, 1), :, at]), (s[a][:, at], t.S[bass.ds(b, 1), :, at])):
                        sp.dma_start(dst, src.rearrange("b p t -> (b p) t")).then_inc(part, 16)
                    sp.dma_start(y[a][:, :, at], t.Y[bass.ds(b, 1)].rearrange("b (a p) t -> p (b a) t", p=128)[:, :, at]).then_inc(part, 16)

            def store(b, a):
                sp.wait_ge(x1_ready, b * NCH + 3 * NCH)
                sp.dma_start(t.X1[bass.ds(b, 1)].rearrange("b p t -> (b p) t"), x1[a][:]).then_inc(x1_stored[a], 16)
                sp.wait_ge(xn_ready, b * 4 + 12)
                sp.dma_start(t.XN[:, :, :, bass.ds(b * RPI, RPI)].rearrange("p j q r -> p (j q) r"), xn[:].rearrange("p j q r -> p (j q) r")).then_inc(xn_stored, 16)
            for a in range(2):
                load(a, a)
            with sp.Fori(1, BATCH // 2) as i:
                for a in range(2):
                    load(i * 2 + a, a)
                    store(i * 2 + a - 2, a)
            for a in range(2):
                store(BATCH - 2 + a, a)

        @block.tensor
        def _(pe):
            def gate(b, at):
                n, m = b * NCH + at, at % 2
                for x, (lo, hi) in enumerate(PARTS):
                    if at % NCH == lo:
                        pe.wait_ge(loaded[at // NCH % 2 * len(PARTS) + x], b * 24 + (at // (2 * NCH) + 1) * 48)
                for h in range(2):
                    pe.wait_ge(u_ready, n * 2 + h + 1)
                    pe.matmul(ps_u[2 * m + h][:, 0:COLS], k.w[:, WU + h, :], xr[at // NCH % 2][:, cols(at % NCH)], start=True, stop=True).then_inc(u_ps, 1)

            def body(b, a):
                for c in range(NCH):
                    n, m = b * NCH + c, (a * NCH + c) % 2
                    pe.wait_ge(z_ready, n + 3)
                    pe.wait_ge(x1_ready, n + 2 * NCH - 1)
                    for h in range(2):
                        last = pe.matmul(ps[m][:, 0:COLS], k.w[:, WO + h, :], z[m][:, h, :], start=(h == 0), stop=(h == 1))
                    last.then_inc(o_ps, 1)
                    if inside(n + 2):
                        gate(b - a, a * NCH + c + 2)
                gs.on_tensor(pe, b, k.avg[:])
            gate(0, 0)
            gate(0, 1)
            images(pe, body)

        @block.vector
        def _(dve):
            dve.sem_inc(x1_ready, 2 * NCH)
            dve.sem_inc(z_ready, 2)

            def gated(b, at):
                n = b * NCH + at
                dve.wait_ge(u_ready, n * 2 + 6)
                dve.tensor_tensor(z[at % 2][:], u[at % 2][:], y[at // NCH % 2][:, :, cols(at % NCH)], ALU.mult).then_inc(z_ready, 1)

            def body(b, a):
                dve.wait_ge(x1_stored[a], (b - a) * 8 + 16)
                dve.wait_ge(xn_ready, b * 4 + 4)
                for c in range(NCH):
                    n, m = b * NCH + c, (a * NCH + c) % 2
                    if inside(n + 1):
                        gated(b - a, a * NCH + c + 1)
                    dve.wait_ge(o_ps, n + 1)
                    dve.tensor_tensor(x1[a][:, cols(c)], s[a][:, cols(c)], ps[m][:, 0:COLS], ALU.add).then_inc(x1_ready, 1)
                    dve.wait_ge(x1_ready, n + 2 * NCH + 1)
                    dve.bn_stats(gs.parts[:, c, :], x1[a][:, cols(c)]).then_inc(gs.s_parts, 1)
                dve.wait_ge(xn_ready, b * 4 + 8)
                gs.on_vector(dve, b)
            gated(0, 0)
            images(dve, body)

        @block.gpsimd
        def _(pool):
            def body(b, a):
                pool.wait_ge(gs.s_shift, b + 1)
                pool.wait_ge(xn_stored, (b + 1) * 16)
                pool.sem_inc(norm_seen, 1)
                rows = x1[a][:].rearrange("p (r q j) -> p j q r", q=PAIRS, j=2)
                for m in range(4):
                    j, q = m // 2, slice(m % 2 * 4, m % 2 * 4 + 4)
                    pool.tensor_scalar(xn[:, j, q, :], rows[:, j, q, :], gs.scale[:, 0:1], gs.shift[:, 0:1], ALU.mult, ALU.add).then_inc(xn_ready, 1)
            images(pool, body)

        @block.scalar
        def _(act):
            act.sem_inc(u_ready, 4)
            act.sem_inc(xn_ready, 8)
            act.sem_inc(xn_stored, 16)
            for m in range(2):
                act.sem_inc(x1_stored[m], 16)

            def silu(b, at):
                n, m = b * NCH + at, at % 2
                for h in range(2):
                    act.wait_ge(u_ps, n * 2 + h + 1)
                    act.wait_ge(z_ready, n + 1)
                    act.activation(u[m][:, h, :], ps_u[2 * m + h][:, 0:COLS], ACT.Silu, bias=k.bias[:, h:h + 1]).then_inc(u_ready, 1)

            def body(b, a):
                for c in range(NCH):
                    if inside(b * NCH + c + 2):
                        silu(b - a, a * NCH + c + 2)
                gs.on_scalar(act, b)
            silu(0, 0)
            silu(0, 1)
            images(act, body)
            for m in range(2):
                act.wait_ge(x1_stored[m], 16 * (BATCH // 2 + 1))
            act.wait_ge(xn_stored, 16 * (BATCH + 1))


def attend(nc, t, k):
    STEPS = PAIRS * RTOT // RG
    AHEAD = 4
    D, HH = CH, HEADS * HEADS
    with ExitStack() as ctx:
        def sb(n, shape):
            return ctx.enter_context(nc.sbuf_tensor(n, shape, F32))

        def psum(n):
            return ctx.enter_context(nc.psum_tensor(n, [128, 512], F32))

        def sem(n):
            return ctx.enter_context(nc.semaphore(n))

        def bufs(count, n, shape):
            return [sb(f"{n}{m}", [RG, 2] + shape) for m in range(count)]
        xn = [sb(f"xn_in{m}", [128, 2, RG]) for m in range(4)]
        v2, qk, norm_i = bufs(4, "v2_", [D]), bufs(4, "qk_", [2 * D]), bufs(4, "norm_i", [24])
        sq, norm_sq, norm, norm_c = bufs(2, "sq", [3 * D]), bufs(2, "norm_sq", [24]), bufs(2, "norm", [24]), bufs(2, "norm_c", [24])
        SHIFTS = HEADS // 2 + 1
        WRAP = HEADS // 2 - 1
        SPARE = 2
        ROWS = SPARE + HEADS + WRAP
        vh = bufs(2, "vh", [D + (SHIFTS - 1) * HD])
        small = bufs(1, "small_prod", [HH * HD])[0]
        S, A_exp = bufs(2, "S", [HEADS * SHIFTS]), bufs(2, "A_exp", [ROWS * HEADS])
        A_sum, A_inv = bufs(2, "A_sum", [8]), bufs(2, "A_inv", [8])
        A = bufs(2, "A", [3 * HH])
        BW = 2 * HEADS
        B_half, B = bufs(2, "B_half", [HEADS * SHIFTS]), bufs(2, "B", [ROWS * BW])
        Bq, Bqk = bufs(2, "Bq", [HH]), bufs(2, "Bqk", [HH])
        m_prod = [sb(f"m_prod{m}", [RG, HEADS, 2, HEADS * HD]) for m in range(2)]
        l_prod = sb("l_prod", [RG, HEADS, 2, HD * HD])
        o_prod = sb("o_prod", [RG, HD, 2, HD * HEADS])
        o_pair = sb("o_pair", [RG, HD // 2, 2, HD * HEADS])
        L_max, L_sh, P_exp = bufs(2, "L_max", [HD]), bufs(2, "L_sh", [HD * HD]), bufs(2, "P_exp", [HD * HD])
        P_sum, P_inv, v_sc = bufs(2, "P_sum", [HD]), bufs(2, "P_inv", [HD]), bufs(2, "v_sc", [D])
        o_sb = [sb(f"o_sb{m}", [RG, HD, 2, HEADS]) for m in range(2)]
        ps_qkv = [psum(f"ps_qkv{j}") for j in range(2)]
        ps_m = [psum(f"ps_m{m}") for m in range(2)]
        ps_l = [psum(f"ps_l{m}") for m in range(2)]
        ps_o = [psum(f"ps_o{m}") for m in range(2)]
        xn_loaded = [sem(f"xn_loaded{m}") for m in range(4)]
        names = ("qkv_ps qkv_read nsq norm nc ni vh vhx sprod s aexp asum ainv a bprod b bx bq bqk "
                 "mprod m_ps lprod l_ps lmax lsh pexp psum pinv vsc oprod opair o_ps o").split()
        s = {n: sem("at_" + n) for n in names}
        o_stored = [sem(f"o_stored{m}") for m in range(2)]
        block = ctx.enter_context(nc.Block())

        def steps(eng, body):
            rounds = STEPS // AHEAD - 1
            for m in range(AHEAD):
                body(m, m)
            with eng.Fori(1, rounds) as i:
                for m in range(AHEAD):
                    body(i * AHEAD + m, m)
            for n in range(rounds * AHEAD, STEPS):
                body(n, n % AHEAD)

        @block.sync
        def _(sp):
            def load(n, m):
                sp.wait_ge(s["qkv_ps"], n * 2 + 2)
                src = t.XN.rearrange("p j q r -> p j (q r)")[:, :, bass.ds(n * RG, RG)]
                sp.dma_start(xn[m][:], src).then_inc(xn_loaded[m], 16)
            with sp.Fori(0, STEPS // AHEAD) as i:
                for m in range(AHEAD):
                    load(i * AHEAD + m, m)
            for n in range(STEPS // AHEAD * AHEAD, STEPS):
                load(n, n % AHEAD)

        @block.tensor
        def _(pe):
            pe.sem_inc(s["qkv_ps"], 8)
            pe.sem_inc(s["o_ps"], 1)
            pe.sem_inc(s["m_ps"], 2)

            def qkv(n, m):
                pe.wait_ge(xn_loaded[m], (n // AHEAD + 1) * 16 if isinstance(n, int) else (n - m) * 4 + 16)
                for j in range(2):
                    pe.wait_ge(s["qkv_read"], n * 2 + j + 1)
                    pe.matmul(ps_qkv[j][0:RG, 0:3 * D], xn[m][:, j, :], k.w[:, WQ:WQ + 3, :].rearrange("p a c -> p (a c)"),
                              start=True, stop=True).then_inc(s["qkv_ps"], 1)

            def mixed(n, m):
                pe.wait_ge(s["mprod"], n + 3)
                for x in range(HEADS):
                    last = pe.matmul(ps_m[m % 2][0:RG, 0:2 * D], k.ident[0:RG, 0:RG], m_prod[m % 2][:, x].rearrange("p j c -> p (j c)"),
                                     start=(x == 0), stop=(x == HEADS - 1))
                last.then_inc(s["m_ps"], 1)

            def outputs(n, m):
                pe.wait_ge(s["o"], n + 1)
                pe.wait_ge(s["opair"], n + 2)
                for x in range(HD // 2):
                    last = pe.matmul(ps_o[m % 2][0:RG, 0:2 * D], k.ident[0:RG, 0:RG], o_pair[:, x].rearrange("p j c -> p (j c)"),
                                     start=(x == 0), stop=(x == HD // 2 - 1))
                last.then_inc(s["o_ps"], 1)

            def body(n, m):
                late = isinstance(n, int)
                for j in range(2):
                    pe.wait_ge(s["lprod"], n * 2 + j + 1)
                    for x in range(HEADS):
                        last = pe.matmul(ps_l[m % 2][0:RG, j * HD * HD:(j + 1) * HD * HD], k.ident[0:RG, 0:RG], l_prod[:, x, j], start=(x == 0), stop=(x == HEADS - 1))
                last.then_inc(s["l_ps"], 1)
                if not late or n + 1 < STEPS:
                    mixed(n + 1, m + 1)
                if not late or n > 0:
                    outputs(n - 1, m - 1)
                if not late or n + 4 < STEPS:
                    qkv(n + 4, m)
            for n in range(4):
                qkv(n, n)
            mixed(0, 0)
            steps(pe, body)
            outputs(STEPS - 1, STEPS - 1)

        @block.scalar
        def _(act):
            act.sem_inc(s["qkv_read"], 2)
            act.sem_inc(s["o"], 2)
            for m in range(2):
                act.sem_inc(o_stored[m], 16)

            def empty(n, m):
                act.wait_ge(s["vsc"], n + 1)
                for j in range(2):
                    act.wait_ge(s["qkv_ps"], n * 2 + j + 9)
                    act.activation(sq[m % 2][:, j, 0:2 * D], ps_qkv[j][0:RG, 0:2 * D], ACT.Square)
                    act.activation(sq[m % 2][:, j, 2 * D:], ps_qkv[j][0:RG, 2 * D:3 * D], ACT.Square, scale=2.0)
                    act.activation(qk[m][:, j], ps_qkv[j][0:RG, 0:2 * D], ACT.Copy)
                    act.activation(v2[m][:, j], ps_qkv[j][0:RG, 2 * D:3 * D], ACT.Copy, scale=2.0).then_inc(s["qkv_read"], 1)

            def norms(n, m):
                act.wait_ge(s["nsq"], n + 1)
                act.activation(norm[m % 2][:], norm_sq[m % 2][:], ACT.Sqrt).then_inc(s["norm"], 1)

            def exp1(n, m):
                act.wait_ge(s["s"], n + 1)
                a, c = m % 2, S[m % 2][:].rearrange("p j (h x) -> p j h x", x=SHIFTS)
                w, row = ROWS * HEADS, HEADS
                rows = A_exp[a][:].rearrange("p j (h x) -> p j h x", x=HEADS)
                act.activation(rows[:, :, SPARE:SPARE + HEADS, 0:SHIFTS], c, ACT.Exp).then_inc(s["aexp"], 1)
                back = SPARE * row + HEADS + row - 1
                for lo, wrap in ((0, 0), (HEADS - WRAP, HEADS)):
                    dst = strided(A_exp[a][:], back + (lo - wrap) * row, [(w, 2), (row, HEADS - lo), (row - 1, WRAP)])
                    act.activation(dst, c[:, :, lo:, 1:1 + WRAP], ACT.Exp).then_inc(s["aexp"], 1)

            def fill(n, m):
                a, c = m % 2, B_half[m % 2][:].rearrange("p j (f x) -> p j f x", x=SHIFTS)
                act.wait_ge(s["b"], n + 1)
                for f, x, end, col, row in ((0, 0, SHIFTS, 0, 0), (HEADS // 2, 0, SHIFTS, HEADS, 0),
                                            (0, 1, 1 + WRAP, 0, 0), (HEADS - WRAP, 1, 1 + WRAP, 0, HEADS)):
                    if x:
                        first, step = (SPARE + f + x - row) * BW + f, BW
                    else:
                        first, step = (SPARE + f) * BW + f - col, 1
                    act.activation(strided(B[a][:], first, [(ROWS * BW, 2), (BW + 1, HEADS - f), (step, end - x)]),
                                   c[:, :, f:, x:end], ACT.Copy).then_inc(s["bx"], 1)

            def repeat(n, m):
                act.wait_ge(s["vh"], n + 1)
                act.activation(vh[m % 2][:, :, D:], vh[m % 2][:, :, 0:(SHIFTS - 1) * HD], ACT.Copy).then_inc(s["vhx"], 1)

            def exp2(n, m):
                act.wait_ge(s["lsh"], n + 1)
                act.wait_ge(s["oprod"], n + 1)
                act.activation(P_exp[m % 2][:], L_sh[m % 2][:], ACT.Exp).then_inc(s["pexp"], 1)

            def leave(n, m):
                act.wait_ge(s["o_ps"], n + 2)
                act.wait_ge(o_stored[m % 2], (n // 2 + 1) * 16 if isinstance(n, int) else (n - m % 2) * 8 + 16)
                act.activation(o_sb[m % 2][:].rearrange("p e j h -> p j e h"),
                               ps_o[m % 2][0:RG, 0:256].rearrange("p (j e h) -> p j e h", j=2, h=HEADS), ACT.Copy).then_inc(s["o"], 1)
                act.wait_ge(s["o"], n + 3)
                act.dma_start(t.O[bass.ds(n * RG, RG)], o_sb[m % 2][:].rearrange("p e j h -> p (e j h)")).then_inc(o_stored[m % 2], 16)

            def body(n, m):
                late = isinstance(n, int)
                if not late or n + 3 < STEPS:
                    empty(n + 3, (m + 3) % 4)
                if not late or n + 2 < STEPS:
                    exp1(n + 2, m + 2)
                if not late or n + 2 < STEPS:
                    fill(n + 2, m + 2)
                exp2(n, m)
                if not late or n + 3 < STEPS:
                    norms(n + 3, m + 3)
                if not late or n + 3 < STEPS:
                    repeat(n + 3, m + 3)
                if not late or n > 0:
                    leave(n - 1, m - 1)
            for n in range(3):
                if n == 2:
                    exp1(0, 0)
                    fill(0, 0)
                empty(n, n)
                norms(n, n)
                repeat(n, n)
            exp1(1, 1)
            fill(1, 1)
            steps(act, body)
            leave(STEPS - 1, STEPS - 1)
            for m in range(2):
                act.wait_ge(o_stored[m], 16 * (STEPS // 2 + 1))

        @block.vector
        def _(dve):
            dve.sem_inc(s["vsc"], 4)

            def heads(ap, g=HEADS):
                return ap.rearrange("p j (h g) -> p j h g", g=g)

            def squares(n, m):
                dve.wait_ge(s["qkv_read"], n * 2 + 4)
                dve.tensor_reduce(norm_sq[m % 2][:], heads(sq[m % 2][:], HD), AX, ALU.add).then_inc(s["nsq"], 1)

            def norms(n, m):
                a, b = m % 2, m % 4
                dve.wait_ge(s["norm"], n + 1)
                dve.tensor_scalar(norm_c[a][:], norm[a][:], 1e-12, None, ALU.max).then_inc(s["nc"], 1)
                dve.wait_ge(s["nc"], n + 1)
                dve.reciprocal(norm_i[b][:], norm_c[a][:]).then_inc(s["ni"], 1)
                dve.wait_ge(s["ni"], n + 1)
                dve.tensor_tensor(heads(vh[a][:, :, 0:D], HD), heads(v2[b][:], HD), bcast(norm_i[b][:, :, 16:24], 3, HD), ALU.mult).then_inc(s["vh"], 1)

            def products(n, m):
                a, w = m % 2, D + (SHIFTS - 1) * HD
                dve.wait_ge(s["vhx"], n + 1)
                for j in range(2):
                    v = vh[a][:, j, 0:D].rearrange("p (h d) -> p h d", d=HD)
                    shifted = strided(vh[a][:], j * w, [(HD, HEADS), (HD, SHIFTS), (1, HD)])
                    last = dve.tensor_tensor(small[:, j, 0:HEADS * SHIFTS * HD].rearrange("p (h x d) -> p h x d", h=HEADS, d=HD),
                                             bcast(v, 2, SHIFTS), shifted, ALU.mult)
                last.then_inc(s["sprod"], 1)

            def scores(n, m):
                dve.wait_ge(s["sprod"], n + 1)
                dve.tensor_reduce(S[m % 2][:], heads(small[:, :, 0:HEADS * SHIFTS * HD], HD), AX, ALU.add).then_inc(s["s"], 1)

            def mix(n, m):
                a, b = m % 2, m % 4
                dve.wait_ge(s["aexp"], 3 * n + 3)
                rows = heads(A_exp[a][:])[:, :, SPARE:SPARE + HEADS]
                dve.tensor_reduce(A_sum[a][:], rows, AX, ALU.add).then_inc(s["asum"], 1)
                dve.wait_ge(s["asum"], n + 1)
                dve.reciprocal(A_inv[a][:], A_sum[a][:]).then_inc(s["ainv"], 1)
                dve.wait_ge(s["ainv"], n + 1)
                for j in range(2):
                    last = dve.tensor_tensor(A[a][:, j].rearrange("p (h y x) -> p h y x", h=HEADS, y=3), bcast(rows[:, j], 2, 3),
                                             bcast(bcast(A_inv[a][:, j], 2, 3), 3, HEADS), ALU.mult)
                last.then_inc(s["a"], 1)
                dve.wait_ge(s["a"], n + 1)
                for j in range(2):
                    at, down = j * 3 * HH + HEADS, 3 * HEADS - 1
                    last = dve.tensor_tensor(small[:, j, 0:HEADS * SHIFTS * HEADS].rearrange("p (f x h) -> p f x h", f=HEADS, h=HEADS),
                                             strided(A[a][:], at, [(1, HEADS), (0, SHIFTS), (down, HEADS)]),
                                             strided(A[a][:], at, [(1, HEADS), (1, SHIFTS), (down, HEADS)]), ALU.mult)
                last.then_inc(s["bprod"], 1)
                dve.wait_ge(s["bprod"], n + 1)
                dve.tensor_reduce(B_half[a][:], heads(small[:, :, 0:HEADS * SHIFTS * HEADS]), AX, ALU.add).then_inc(s["b"], 1)

            def logits(n, m, j):
                dve.wait_ge(s["m_ps"], n + 3)
                kk = qk[m % 4][:, j, D:].rearrange("p (h d) -> p h d", d=HD)
                mm = ps_m[m % 2][0:RG, j * 128:(j + 1) * 128].rearrange("p (g e) -> p g e", e=HD)
                dve.tensor_tensor(l_prod[:, :, j].rearrange("p g (d e) -> p g d e", e=HD), bcast(kk, 3, HD), bcast(mm, 2, HD),
                                  ALU.mult).then_inc(s["lprod"], 1)

            def maxima(n, m):
                a = m % 2
                ll = heads(ps_l[a][0:RG, :].rearrange("p (j c) -> p j c", j=2), HD)
                dve.wait_ge(s["l_ps"], n + 1)
                dve.tensor_reduce(L_max[a][:], ll, AX, ALU.max).then_inc(s["lmax"], 1)

            def shift(n, m):
                a = m % 2
                ll = heads(ps_l[a][0:RG, :].rearrange("p (j c) -> p j c", j=2), HD)
                dve.wait_ge(s["lmax"], n + 1)
                dve.tensor_tensor(heads(L_sh[a][:], HD), ll, bcast(L_max[a][:], 3, HD), ALU.subtract).then_inc(s["lsh"], 1)

            def scale_q(n, m):
                a, b = m % 2, m % 4
                dve.wait_ge(s["bx"], 4 * n + 4)
                dve.tensor_tensor(heads(Bq[a][:]), heads(B[a][:], BW)[:, :, SPARE:SPARE + HEADS, 0:HEADS], bcast(norm_i[b][:, :, 0:8], 3, HEADS), ALU.mult).then_inc(s["bq"], 1)

            def scale_k(n, m):
                a, b = m % 2, m % 4
                dve.wait_ge(s["bq"], n + 1)
                dve.wait_ge(s["mprod"], n + 1)
                dve.tensor_tensor(heads(Bqk[a][:]), heads(Bq[a][:]), bcast(norm_i[b][:, :, 8:16], 2, HEADS), ALU.mult).then_inc(s["bqk"], 1)

            def divide(n, m):
                a, b = m % 2, m % 4
                dve.wait_ge(s["pexp"], n + 1)
                dve.tensor_reduce(P_sum[a][:], heads(P_exp[a][:], HD), AX, ALU.add).then_inc(s["psum"], 1)
                dve.wait_ge(s["psum"], n + 1)
                dve.reciprocal(P_inv[a][:], P_sum[a][:]).then_inc(s["pinv"], 1)
                dve.wait_ge(s["pinv"], n + 1)
                dve.wait_ge(s["oprod"], n + 1)
                dve.tensor_tensor(v_sc[a][:].rearrange("p j (d h) -> p j d h", h=HEADS), v2[b][:].rearrange("p j (h d) -> p j d h", d=HD),
                                  bcast(P_inv[a][:], 3, HEADS), ALU.mult).then_inc(s["vsc"], 1)

            def body(n, m):
                late = isinstance(n, int)
                more = not late or n + 2 < STEPS
                logits(n, m, 0)
                if more:
                    products(n + 2, m + 2)
                logits(n, m, 1)
                if more:
                    scores(n + 2, m + 2)
                if not late or n + 3 < STEPS:
                    squares(n + 3, m + 3)
                if more:
                    mix(n + 2, m + 2)
                maxima(n, m)
                shift(n, m)
                if more:
                    scale_q(n + 2, m + 2)
                    scale_k(n + 2, m + 2)
                divide(n, m)
                if not late or n + 3 < STEPS:
                    norms(n + 3, m + 3)
            for n in range(3):
                if n == 2:
                    products(0, 0)
                    scores(0, 0)
                    mix(0, 0)
                    scale_q(0, 0)
                    scale_k(0, 0)
                squares(n, n)
                norms(n, n)
            products(1, 1)
            scores(1, 1)
            mix(1, 1)
            scale_q(1, 1)
            scale_k(1, 1)
            steps(dve, body)

        @block.gpsimd
        def _(pool):
            pool.sem_inc(s["oprod"], 2)
            pool.sem_inc(s["mprod"], 2)
            pool.sem_inc(s["opair"], 1)

            def mix(n, m):
                pool.wait_ge(s["bqk"], n + 1)
                pool.wait_ge(s["m_ps"], n + 1)
                for j in range(2):
                    q = qk[m % 4][:, j, 0:D].rearrange("p (h d) -> p h d", d=HD)
                    last = pool.tensor_tensor(m_prod[m % 2][:, :, j].rearrange("p f (g e) -> p f g e", e=HD),
                                              bcast(Bqk[m % 2][:, j].rearrange("p (f g) -> p f g", f=HEADS), 3, HD), bcast(q, 2, HEADS), ALU.mult)
                last.then_inc(s["mprod"], 1)

            def output(n, m):
                a = m % 2
                pool.wait_ge(s["vsc"], n + 5)
                pool.wait_ge(s["opair"], n + 1)
                for j in range(2):
                    last = pool.tensor_tensor(o_prod[:, :, j].rearrange("p d (e h) -> p d e h", h=HEADS),
                                              bcast(P_exp[a][:, j].rearrange("p (d e) -> p d e", e=HD), 3, HEADS),
                                              bcast(v_sc[a][:, j].rearrange("p (d h) -> p d h", h=HEADS), 2, HD), ALU.mult)
                last.then_inc(s["oprod"], 1)
                pool.wait_ge(s["oprod"], n + 3)
                pool.wait_ge(s["o_ps"], n + 1)
                pool.tensor_tensor(o_pair[:], o_prod[:, 0:HD // 2], o_prod[:, HD // 2:], ALU.add).then_inc(s["opair"], 1)

            def body(n, m):
                late = isinstance(n, int)
                if not late or n + 2 < STEPS:
                    mix(n + 2, m + 2)
                output(n, m)
            for n in range(2):
                mix(n, n)
            steps(pool, body)


def project_final(nc, t, k):
    with ExitStack() as ctx:
        def sb(n, shape):
            return ctx.enter_context(nc.sbuf_tensor(n, shape, F32))

        def psum(n):
            return ctx.enter_context(nc.psum_tensor(n, [128, 512], F32))

        def sem(n):
            return ctx.enter_context(nc.semaphore(n))
        EQ = 4
        NQ = HD // EQ
        o_in = [sb(f"o_in{n}", [HALF, PAIRS, HD, 2 * HEADS]) for n in range(4)]
        o_row = [sb(f"o_row{n}", [HALF, EQ, 128]) for n in range(2)]
        x_in = [sb(f"x1_in{n}", [128, HD, HALF]) for n in range(4)]
        oT = [sb(f"oT{n}", [128, EQ, HALF]) for n in range(2)]
        xb = [sb(f"x1_bias{n}", [HALF, EQ, CH]) for n in range(2)]
        res = [sb(f"res{n}", [HALF, EQ, CH]) for n in range(NQ)]
        ps_t = [psum(f"ps_ot{n}") for n in range(2)]
        ps_o, ps_x = ([psum(f"{m}{n}") for n in range(2)] for m in ("ps_out", "ps_x1"))
        loaded = [sem(f"fin_loaded{n}") for n in range(4)]
        x_turned, x_read, rowed, turned, copied, summed, done = sem("x1_turned"), sem("x1_read"), sem("o_rowed"), sem("o_turned"), sem("o_copied"), sem("out_ps"), sem("out_ready")
        stored = [sem(f"out_stored{n}") for n in range(NQ)]
        block = ctx.enter_context(nc.Block())

        def parts(i):
            return [(h, q, q % 2, (i * 4 + h) * NQ + q) for h in range(4) for q in range(NQ)]

        @block.sync
        def _(sp):
            with sp.Fori(0, BATCH // 2) as i:
                for h in range(4):
                    b = i * 2 + h // 2
                    sp.wait_ge(summed, (i * 4 + h + 1) * NQ)
                    sp.dma_start(o_in[h][:].rearrange("r q e c -> r q (e c)"),
                                 t.O.rearrange("(q r) c -> r q c", q=PAIRS)[bass.ds(b * RPI + h % 2 * HALF, HALF)]).then_inc(loaded[h], 16)
                    src = t.X1[bass.ds(b, 1)].rearrange("b p (e h r) -> h p (b e) r", h=2, r=HALF)
                    sp.dma_start(x_in[h][:], src[h % 2]).then_inc(loaded[h], 16)

        @block.tensor
        def _(pe):
            pe.sem_inc(summed, 4 * NQ)

            def turn(h, q, n, at):
                pe.wait_ge(rowed, at + 1)
                for m in range(EQ):
                    last = pe.transpose(ps_t[n][:, m * HALF:(m + 1) * HALF], o_row[n][:, m, :], k.ident[0:HALF, 0:HALF])
                last.then_inc(turned, 1)

            def project(h, q, n, at):
                pe.wait_ge(copied, at + 1)
                pe.wait_ge(done, at + 1)
                for m in range(EQ):
                    last = pe.matmul(ps_o[n][0:HALF, m * CH:(m + 1) * CH], oT[n][:, m, :], k.w[:, PW, :], start=True, stop=True)
                last.then_inc(summed, 1)

            def turn_x(h, q, n, at):
                pe.wait_ge(x_read, at + 1)
                for m in range(EQ):
                    last = pe.transpose(ps_x[n][0:HALF, m * CH:(m + 1) * CH], x_in[h][:, q * EQ + m, :], k.ident[:])
                last.then_inc(x_turned, 1)
            with pe.Fori(0, BATCH // 2) as i:
                todo = parts(i)
                turn(*todo[0])
                for p, part in enumerate(todo):
                    if p + 1 < len(todo):
                        turn(*todo[p + 1])
                    if part[1] == 0:
                        pe.wait_ge(loaded[part[0]], i * 32 + 32)
                    turn_x(*part)
                    project(*part)

        @block.scalar
        def _(act):
            for q in range(NQ):
                act.sem_inc(stored[q], 16)

            def row(i, h, q, n, at):
                act.wait_ge(loaded[h], i * 32 + 32)
                act.activation(o_row[n][:].rearrange("r e (n c) -> r e n c", c=2 * HEADS),
                               o_in[h][:, :, q * EQ:(q + 1) * EQ, :].rearrange("r n e c -> r e n c"), ACT.Copy).then_inc(rowed, 1)

            def copy(h, q, n, at):
                act.wait_ge(turned, at + 1)
                act.activation(oT[n][:].rearrange("p a r -> p (a r)"), ps_t[n][:, 0:EQ * HALF], ACT.Copy).then_inc(copied, 1)

            def store(i, h, q, n, at):
                act.wait_ge(done, at + 3)
                rows = t.out_rows[bass.ds((i * 2 + h // 2) * TOK, TOK), :].rearrange("(e h r) c -> h r e c", h=2, r=HALF)
                act.dma_start(rows[h % 2][:, q * EQ:(q + 1) * EQ, :], res[q][:]).then_inc(stored[q], 16)
            with act.Fori(0, BATCH // 2) as i:
                todo = parts(i)
                row(i, *todo[0])
                for p, part in enumerate(todo):
                    if p + 1 < len(todo):
                        row(i, *todo[p + 1])
                    copy(*part)
                    if p:
                        store(i, *todo[p - 1])
                store(i, *todo[-1])
            for q in range(NQ):
                act.wait_ge(stored[q], 16 * (BATCH * 2 + 1))

        @block.vector
        def _(dve):
            dve.sem_inc(done, 2)
            dve.sem_inc(x_read, 2)
            with dve.Fori(0, BATCH // 2) as i:
                for h, q, n, at in parts(i):
                    dve.wait_ge(x_turned, at + 1)
                    dve.wait_ge(done, at + 1)
                    dve.tensor_tensor(xb[n][:], ps_x[n][0:HALF, :].rearrange("p (a c) -> p a c", a=EQ),
                                      bcast(k.proj_b[0:HALF, :], 1, EQ), ALU.add).then_inc(x_read, 1)
                    dve.wait_ge(x_read, at + 3)
                    dve.wait_ge(summed, at + 1 + 4 * NQ)
                    dve.wait_ge(stored[q], i * 64 + h * 16 + 16)
                    dve.tensor_tensor(res[q][:], ps_o[n][0:HALF, :].rearrange("p (a c) -> p a c", a=EQ), xb[n][:], ALU.add).then_inc(done, 1)


def build(nc, t):
    scratch(nc, t)
    with ExitStack() as ctx:
        k = Net()

        def sb(n, shape):
            return ctx.enter_context(nc.sbuf_tensor(n, shape, F32))
        k.w = sb("weights", [128, WEIGHT_TILES, 128])
        k.bias = sb("biases", [128, 10])
        k.ident, k.avg, k.ones = sb("ident", [128, 128]), sb("group_avg", [128, 128]), sb("ones", [128, 128])
        k.rpe_in = sb("rpe_in", [3, 128])
        k.proj_b = sb("proj_b", [128, CH])
        k.fwd_h, k.fwd_w = sb("fwd_h", [SIDE, 2 * NF]), sb("fwd_w", [120, 2, NFFT])
        k.tap_p, k.tap_q = sb("tap_p", [TAPS, 2 * NF]), sb("tap_q", [TAPS, 4, NFFT])
        k.inv_w, k.inv_h = sb("inv_w", [NFFT, 2, NFFT]), sb("inv_h", [2 * NF, 2, 2 * SIDE])
        load_weights(nc, t, k)
        project_in(nc, t, k)
        make_taps(nc, t, k)
        convolve(nc, t, k)
        project_out(nc, t, k)
        attend(nc, t, k)
        project_final(nc, t, k)


def tables():
    import numpy as np
    two_pi = 2.0 * np.pi / NFFT
    f, g, m = np.arange(NF), np.arange(NFFT), np.arange(SIDE)
    taps = np.arange(TAPS) - (SIDE - 1)
    c = {}
    c["c_ident"] = np.eye(128)
    c["c_avg"] = np.kron(np.eye(128 // GROUP_CH), np.full((GROUP_CH, GROUP_CH), 1.0 / GROUP_CH))
    a = two_pi * np.outer(m, f)
    c["c_fwd_h"] = np.concatenate([np.cos(a), -np.sin(a)], axis=1)
    a = two_pi * np.outer(m, g)
    cw, sw = np.cos(a), np.sin(a)
    fw = np.zeros((120, 2, NFFT))
    fw[0:SIDE, 0], fw[64:120, 0] = cw, sw
    fw[0:SIDE, 1], fw[64:120, 1] = -sw, cw
    c["c_fwd_w"] = fw
    a = two_pi * np.outer(taps, f)
    c["c_tap_p"] = np.concatenate([np.cos(a), -np.sin(a)], axis=1)
    a = two_pi * np.outer(taps, g)
    cq, sq = np.cos(a), np.sin(a)
    c["c_tap_q"] = np.stack([cq, sq, -sq, cq], axis=1)
    a = two_pi * np.outer(g, m)
    ci, si = np.cos(a) / NFFT, np.sin(a) / NFFT
    c["c_inv_w"] = np.stack([np.concatenate([ci, si], 1), np.concatenate([-si, ci], 1)], axis=1)
    a = two_pi * np.outer(f, m)
    weight = np.where((f == 0) | (f == NF - 1), 1.0, 2.0)[:, None] / NFFT
    ih = np.zeros((2 * NF, 2, 2 * SIDE))
    for n, part in enumerate((weight * np.cos(a), -weight * np.sin(a))):
        ih[0:NF, n, 0:SIDE], ih[NF:, n, SIDE:] = part, part
    c["c_inv_h"] = ih
    p, q = np.meshgrid(np.arange(TAPS), np.arange(NFFT), indexing="ij")
    c["c_coords"] = np.stack([(p - (SIDE - 1)).ravel(), (q - (SIDE - 1)).ravel(), np.ones(TAPS * NFFT)])
    return {n: np.ascontiguousarray(v, dtype=np.float32) for n, v in c.items()}


_INS = ['x', 'L0_conv_W_u', 'L0_conv_b_u', 'L0_conv_W_v', 'L0_conv_b_v', 'L0_conv_W_o', 'L0_conv_b_o', 'L0_conv_rpe_in_w',
        'L0_conv_rpe_in_b', 'L0_conv_rpe_h_w', 'L0_conv_rpe_h_b', 'L0_conv_rpe_out_w', 'L0_conv_rpe_out_b', 'L1_conv_Wq',
        'L1_conv_Wk', 'L1_conv_Wv', 'L1_conv_proj_w', 'L1_conv_proj_b']


def kernel(**inputs):
    import numpy as _np
    import concourse.bacc as _bacc
    from concourse import mybir as _mybir
    from concourse.bass_utils import run_bass_kernel_spmd as _run

    nc = _bacc.Bacc("TRN2", target_bir_lowering=False, num_devices=1)
    arrays = {f"in_{n}": _np.ascontiguousarray(inputs[n]) for n in _INS}
    consts = tables()
    arrays.update({f"in_{n}": a for n, a in consts.items()})
    t = Net()
    t.__dict__.update({n[3:]: nc.dram_tensor(n, a.shape, _mybir.dt.from_np(a.dtype), kind="ExternalInput").ap()
                       for n, a in arrays.items()})
    out = nc.dram_tensor("out_0", (BATCH, SIDE, SIDE, CH), F32, kind="ExternalOutput").ap()
    t.x_rows = t.x.rearrange("b h w c -> (b h w) c")
    t.out_rows = out.rearrange("b h w c -> (b h w) c")
    build(nc, t)
    r = _run(nc, [arrays], core_ids=[0])
    return r.results[0]["out_0"]
```
